# Optimizing a Trainium2 kernel written in Bass

```python
import numpy as np
import jax
import jax.numpy as jnp

def _softmax(x, axis=-1):
    return jax.nn.softmax(x, axis=axis)

def _gelu(x):
    return jax.nn.gelu(x, approximate=True)

def _silu(x):
    return jax.nn.silu(x)

def _sigmoid(x):
    return jax.nn.sigmoid(x)

def _layernorm(x, axis=-1, eps=1e-05):
    m = jnp.mean(x, axis=axis, keepdims=True)
    v = jnp.var(x, axis=axis, keepdims=True)
    return (x - m) / jnp.sqrt(v + eps)

def _scatter_add(tgt, idx, src, axis=0):
    return tgt.at[idx].add(src)

def _segment_sum(src, seg, n):
    return jax.ops.segment_sum(src, seg, n)
kernel_name = 'mk_lm_tower_d1_tok_ids768_r4_c0c599'

def setup_inputs(seed: int=0):
    np.random.seed(seed)
    _w = jnp.asarray

    def _rec_inputs():
        import jax
        import jax.numpy as jnp
        _rk = jax.random.key(seed)
        x = jax.random.randint(jax.random.fold_in(_rk, 1), (16, 128), 0, 12564, jnp.int32)
        return x
    x = _rec_inputs()

    def _L0_tok_setup():
        import jax, jax.numpy as jnp
        import numpy as np
        LN_EPS = 1e-05
        key = jax.random.key(seed)
        k1, k2, k3 = jax.random.split(key, 3)
        B, S, V, D = (64, 128, 50257, 192)
        input_ids = jax.random.randint(k1, (B, S), 0, V, dtype=jnp.int64)
        word_table = jax.random.normal(k2, (V, D), dtype=jnp.float32) * 0.02
        pos_table = jax.random.normal(k3, (S, D), dtype=jnp.float32) * 0.02
        gamma = jnp.ones((D,), dtype=jnp.float32)
        beta = jnp.zeros((D,), dtype=jnp.float32)
        return {'input_ids': input_ids, 'word_table': word_table, 'pos_table': pos_table, 'gamma': gamma, 'beta': beta}
    _L0_tok_all = _L0_tok_setup()
    _L0_tok_in = {k: v for k, v in _L0_tok_all.items() if k in ('word_table', 'pos_table', 'gamma', 'beta')}
    del _L0_tok_all

    def _L0_attn_setup():
        import jax, jax.numpy as jnp
        import numpy as np
        B, N, D, H = (4, 256, 192, 12)
        HD = D // H
        MLP = 4 * D
        LAMBDA_INIT = 0.1
        LAYER_IDX, MAX_LAYER = (0, 12)

        def _layernorm(x, w, b, eps=1e-05):
            m = x.mean(-1, keepdims=True)
            v = ((x - m) ** 2).mean(-1, keepdims=True)
            return (x - m) * jax.lax.rsqrt(v + eps) * w + b

        def _rmsnorm(x, w, eps=1e-06):
            return x * jax.lax.rsqrt((x * x).mean(-1, keepdims=True) + eps) * w

        def _split_qkv(h, w):
            qkv = (h @ w.T).reshape(h.shape[0], h.shape[1], 3, H, HD)
            qkv = qkv.transpose(2, 0, 3, 1, 4)
            return (qkv[0], qkv[1], qkv[2])

        def _diff_block(x, ln1_w, ln1_b, qkv1_w, qkv2_w, proj_w, proj_b, rms_w, lam1, lam2, ln2_w, ln2_b, fc1_w, fc1_b, fc2_w, fc2_b):
            Bx, Nx, Cx = x.shape
            scale = HD ** (-0.5)
            h = _layernorm(x, ln1_w, ln1_b)
            q1, k1, v1 = _split_qkv(h, qkv1_w)
            q2, k2, _ = _split_qkv(h, qkv2_w)
            a1 = jax.nn.softmax(jnp.einsum('bhnd,bhmd->bhnm', q1, k1) * scale, axis=-1)
            a2 = jax.nn.softmax(jnp.einsum('bhnd,bhmd->bhnm', q2, k2) * scale, axis=-1)
            lam = lam1 - lam2 + LAMBDA_INIT
            diff = a1 - lam * a2
            o = jnp.einsum('bhnm,bhmd->bhnd', diff, v1)
            o = o.transpose(0, 2, 1, 3).reshape(Bx, Nx, Cx)
            o = _rmsnorm(o, rms_w)
            attn_out = o @ proj_w.T + proj_b
            x = x + attn_out
            h2 = _layernorm(x, ln2_w, ln2_b)
            mlp = jax.nn.gelu(h2 @ fc1_w.T + fc1_b, approximate=False) @ fc2_w.T + fc2_b
            return x + mlp
        key = jax.random.key(seed)
        ks = jax.random.split(key, 8)
        s = 0.02
        lam2_init = 1.0 - LAMBDA_INIT * ((LAYER_IDX + 1) / MAX_LAYER)
        return {'x': jax.random.normal(ks[0], (B, N, D), dtype=jnp.float32), 'xpos': jax.random.randint(ks[1], (B, N), 0, N), 'ln1_w': jnp.ones((D,), jnp.float32), 'ln1_b': jnp.zeros((D,), jnp.float32), 'qkv1_w': jax.random.normal(ks[2], (3 * D, D), dtype=jnp.float32) * s, 'qkv2_w': jax.random.normal(ks[3], (3 * D, D), dtype=jnp.float32) * s, 'proj_w': jax.random.normal(ks[4], (D, D), dtype=jnp.float32) * s, 'proj_b': jnp.zeros((D,), jnp.float32), 'rms_w': jnp.ones((D,), jnp.float32), 'lam1': jnp.ones((1, H, 1, 1), jnp.float32), 'lam2': jnp.full((1, H, 1, 1), lam2_init, jnp.float32), 'ln2_w': jnp.ones((D,), jnp.float32), 'ln2_b': jnp.zeros((D,), jnp.float32), 'fc1_w': jax.random.normal(ks[5], (MLP, D), dtype=jnp.float32) * s, 'fc1_b': jnp.zeros((MLP,), jnp.float32), 'fc2_w': jax.random.normal(ks[6], (D, MLP), dtype=jnp.float32) * s, 'fc2_b': jnp.zeros((D,), jnp.float32)}
    _L0_attn_all = _L0_attn_setup()
    _L0_attn_in = {k: v for k, v in _L0_attn_all.items() if k in ('xpos', 'ln1_w', 'ln1_b', 'qkv1_w', 'qkv2_w', 'proj_w', 'proj_b', 'rms_w', 'lam1', 'lam2', 'ln2_w', 'ln2_b', 'fc1_w', 'fc1_b', 'fc2_w', 'fc2_b')}
    del _L0_attn_all

    def _L0_ffn_setup():
        import jax, jax.numpy as jnp
        import numpy as np
        E = 8
        TOP_K = 2
        CAP_RATIO = 1.2
        key = jax.random.key(seed)
        k1, k2, k3, k4 = jax.random.split(key, 4)
        B, L, D, H = (2, 512, 192, 512)
        x = jax.random.normal(k1, (B, L, D), dtype=jnp.float32)
        Wg = jax.random.normal(k2, (D, E), dtype=jnp.float32) * 0.02
        W1 = jax.random.normal(k3, (E, D, 2 * H), dtype=jnp.float32) * 0.02
        W2 = jax.random.normal(k4, (E, H, D), dtype=jnp.float32) * 0.02
        return {'x': x, 'Wg': Wg, 'W1': W1, 'W2': W2}
    _L0_ffn_all = _L0_ffn_setup()
    _L0_ffn_in = {k: v for k, v in _L0_ffn_all.items() if k in ('Wg', 'W1', 'W2')}
    del _L0_ffn_all
    return {'x': x, 'L0_tok_word_table': _L0_tok_in['word_table'], 'L0_tok_pos_table': _L0_tok_in['pos_table'], 'L0_tok_gamma': _L0_tok_in['gamma'], 'L0_tok_beta': _L0_tok_in['beta'], 'L0_attn_xpos': _L0_attn_in['xpos'], 'L0_attn_ln1_w': _L0_attn_in['ln1_w'], 'L0_attn_ln1_b': _L0_attn_in['ln1_b'], 'L0_attn_qkv1_w': _L0_attn_in['qkv1_w'], 'L0_attn_qkv2_w': _L0_attn_in['qkv2_w'], 'L0_attn_proj_w': _L0_attn_in['proj_w'], 'L0_attn_proj_b': _L0_attn_in['proj_b'], 'L0_attn_rms_w': _L0_attn_in['rms_w'], 'L0_attn_lam1': _L0_attn_in['lam1'], 'L0_attn_lam2': _L0_attn_in['lam2'], 'L0_attn_ln2_w': _L0_attn_in['ln2_w'], 'L0_attn_ln2_b': _L0_attn_in['ln2_b'], 'L0_attn_fc1_w': _L0_attn_in['fc1_w'], 'L0_attn_fc1_b': _L0_attn_in['fc1_b'], 'L0_attn_fc2_w': _L0_attn_in['fc2_w'], 'L0_attn_fc2_b': _L0_attn_in['fc2_b'], 'L0_ffn_Wg': _L0_ffn_in['Wg'], 'L0_ffn_W1': _L0_ffn_in['W1'], 'L0_ffn_W2': _L0_ffn_in['W2']}

def reference(x, L0_tok_word_table, L0_tok_pos_table, L0_tok_gamma, L0_tok_beta, L0_attn_xpos, L0_attn_ln1_w, L0_attn_ln1_b, L0_attn_qkv1_w, L0_attn_qkv2_w, L0_attn_proj_w, L0_attn_proj_b, L0_attn_rms_w, L0_attn_lam1, L0_attn_lam2, L0_attn_ln2_w, L0_attn_ln2_b, L0_attn_fc1_w, L0_attn_fc1_b, L0_attn_fc2_w, L0_attn_fc2_b, L0_ffn_Wg, L0_ffn_W1, L0_ffn_W2):
    import jax
    import jax.numpy as jnp

    def _L0_tok_ref(input_ids, word_table, pos_table, gamma, beta):
        import jax, jax.numpy as jnp
        import numpy as np
        LN_EPS = 1e-05
        x = word_table[input_ids] + pos_table[None, :, :]
        mean = jnp.mean(x, axis=-1, keepdims=True)
        var = jnp.mean(jnp.square(x - mean), axis=-1, keepdims=True)
        out = (x - mean) * jax.lax.rsqrt(var + LN_EPS) * gamma + beta
        return out

    def _L0_attn_ref(x, xpos, ln1_w, ln1_b, qkv1_w, qkv2_w, proj_w, proj_b, rms_w, lam1, lam2, ln2_w, ln2_b, fc1_w, fc1_b, fc2_w, fc2_b):
        import jax, jax.numpy as jnp
        import numpy as np
        B, N, D, H = (4, 256, 192, 12)
        HD = D // H
        MLP = 4 * D
        LAMBDA_INIT = 0.1
        LAYER_IDX, MAX_LAYER = (0, 12)

        def _layernorm(x, w, b, eps=1e-05):
            m = x.mean(-1, keepdims=True)
            v = ((x - m) ** 2).mean(-1, keepdims=True)
            return (x - m) * jax.lax.rsqrt(v + eps) * w + b

        def _rmsnorm(x, w, eps=1e-06):
            return x * jax.lax.rsqrt((x * x).mean(-1, keepdims=True) + eps) * w

        def _split_qkv(h, w):
            qkv = (h @ w.T).reshape(h.shape[0], h.shape[1], 3, H, HD)
            qkv = qkv.transpose(2, 0, 3, 1, 4)
            return (qkv[0], qkv[1], qkv[2])

        def _diff_block(x, ln1_w, ln1_b, qkv1_w, qkv2_w, proj_w, proj_b, rms_w, lam1, lam2, ln2_w, ln2_b, fc1_w, fc1_b, fc2_w, fc2_b):
            Bx, Nx, Cx = x.shape
            scale = HD ** (-0.5)
            h = _layernorm(x, ln1_w, ln1_b)
            q1, k1, v1 = _split_qkv(h, qkv1_w)
            q2, k2, _ = _split_qkv(h, qkv2_w)
            a1 = jax.nn.softmax(jnp.einsum('bhnd,bhmd->bhnm', q1, k1) * scale, axis=-1)
            a2 = jax.nn.softmax(jnp.einsum('bhnd,bhmd->bhnm', q2, k2) * scale, axis=-1)
            lam = lam1 - lam2 + LAMBDA_INIT
            diff = a1 - lam * a2
            o = jnp.einsum('bhnm,bhmd->bhnd', diff, v1)
            o = o.transpose(0, 2, 1, 3).reshape(Bx, Nx, Cx)
            o = _rmsnorm(o, rms_w)
            attn_out = o @ proj_w.T + proj_b
            x = x + attn_out
            h2 = _layernorm(x, ln2_w, ln2_b)
            mlp = jax.nn.gelu(h2 @ fc1_w.T + fc1_b, approximate=False) @ fc2_w.T + fc2_b
            return x + mlp
        del xpos
        return _diff_block(x, ln1_w, ln1_b, qkv1_w, qkv2_w, proj_w, proj_b, rms_w, lam1, lam2, ln2_w, ln2_b, fc1_w, fc1_b, fc2_w, fc2_b)

    def _L0_ffn_ref(x, Wg, W1, W2):
        import jax, jax.numpy as jnp
        import numpy as np
        E = 8
        TOP_K = 2
        CAP_RATIO = 1.2
        B, L, D = x.shape
        H = W2.shape[1]
        xf = x.reshape(-1, D)
        N = xf.shape[0]
        capacity = int(CAP_RATIO * N / E)
        logits = xf @ Wg
        scores, idx = jax.lax.top_k(logits, TOP_K)
        weights = jax.nn.softmax(scores, axis=-1)
        xpad = jnp.concatenate([xf, jnp.zeros((1, D), xf.dtype)], axis=0)
        wpad_zero = jnp.zeros((1,), weights.dtype)
        out = jnp.zeros((N, D), x.dtype)
        for k in range(TOP_K):
            ik = idx[:, k]
            onehot = ik[:, None] == jnp.arange(E)[None, :]
            pos = jnp.cumsum(onehot, axis=0) - 1
            posk = jnp.take_along_axis(pos, ik[:, None], axis=1)[:, 0]
            keep = posk < capacity
            buf = jnp.full((E, capacity), N, dtype=jnp.int32)
            buf = buf.at[ik, posk].set(jnp.arange(N, dtype=jnp.int32), mode='drop')
            xg = xpad[buf]
            h = jnp.einsum('ecd,edh->ech', xg, W1)
            act = h[..., :H] * jax.nn.silu(h[..., H:])
            ye = jnp.einsum('ech,ehd->ecd', act, W2)
            wk = jnp.where(keep, weights[:, k], 0.0)
            w_buf = jnp.concatenate([wk, wpad_zero])[buf]
            out = out.at[buf.reshape(-1)].add((w_buf[..., None] * ye).reshape(E * capacity, D), mode='drop')
        return out.reshape(B, L, D)
    h = _L0_tok_ref(x, L0_tok_word_table, L0_tok_pos_table, L0_tok_gamma, L0_tok_beta)
    h = h + _L0_attn_ref(_layernorm(h, axis=-1), L0_attn_xpos, L0_attn_ln1_w, L0_attn_ln1_b, L0_attn_qkv1_w, L0_attn_qkv2_w, L0_attn_proj_w, L0_attn_proj_b, L0_attn_rms_w, L0_attn_lam1, L0_attn_lam2, L0_attn_ln2_w, L0_attn_ln2_b, L0_attn_fc1_w, L0_attn_fc1_b, L0_attn_fc2_w, L0_attn_fc2_b)
    h = h + _L0_ffn_ref(_layernorm(h, axis=-1), L0_ffn_Wg, L0_ffn_W1, L0_ffn_W2)
    return h

_drawn_inputs = setup_inputs


def setup_inputs(seed=0):
    import zlib

    import numpy as np

    out = dict(_drawn_inputs(seed))
    spreads = {'L0_tok_gamma': (1.0, 0.2),
     'L0_tok_beta': (0.0, 0.1),
     'L0_attn_ln1_w': (1.0, 0.6),
     'L0_attn_ln1_b': (0.0, 0.1),
     'L0_attn_proj_b': (0.0, 0.1),
     'L0_attn_rms_w': (1.0, 0.56),
     'L0_attn_lam1': (1.0, 0.6),
     'L0_attn_lam2': (0.9916666746139526, 0.6),
     'L0_attn_ln2_w': (1.0, 0.6),
     'L0_attn_ln2_b': (0.0, 0.8),
     'L0_attn_fc1_b': (0.0, 0.588),
     'L0_attn_fc2_b': (0.0, 0.1)}
    factors = {'L0_attn_qkv2_w': 8.0, 'L0_ffn_Wg': 8.0, 'L0_ffn_W1': 8.0, 'L0_ffn_W2': 8.0}
    for name, (base, spread) in spreads.items():
        noise = np.random.default_rng([zlib.crc32(name.encode()), seed]).standard_normal(out[name].shape)
        drawn = base * np.exp(spread * noise) if base else spread * noise
        out[name] = jnp.asarray(drawn.astype(out[name].dtype))
    for name, factor in factors.items():
        out[name] = (out[name] * factor).astype(out[name].dtype)
    return out
```

```python
from contextlib import ExitStack

import numpy as np

import concourse.bass as bass
from concourse import mybir

ALU = mybir.AluOpType
ACT = mybir.ActivationFunctionType
AX = mybir.AxisListType
F32 = mybir.dt.float32
BF16 = mybir.dt.bfloat16
I32 = mybir.dt.int32
U32 = mybir.dt.uint32
ds = bass.ds

P = 128
B, S, V, D = 16, 128, 12564, 192
KH = D // 2
NH, HD = 12, 16
NHS = 2 * NH
G = 4
NG = B // G
GT = G * P
MLP = 4 * D
MT = MLP // P
FQK = 2 * NHS * HD
QT = FQK // P
PARTS = 3
E, TOPK, HF = 8, 2, 512
N = B * S
CAP = int(1.2 * N / E)
EROWS = 640
ECAP = TOPK * CAP
SLOT_ROWS = E * EROWS
ZERO_ROW = SLOT_ROWS
DROP_ROW = SLOT_ROWS + P
XROWS = DROP_ROW + TOPK * N
YROWS = SLOT_ROWS + P
ST = 5
LN_EPS, RMS_EPS, LAMBDA_INIT = 1e-5, 1e-6, 0.1
Q_SLOTS = (0, 1, 2, 0, 1, 0)
K_SLOTS = (0, 0, 0, 1, 1, 2)
KS = len(Q_SLOTS) * HD
KM = KS + PARTS


class Inputs:

    def __init__(self, ap):
        self.ids = ap["ids"]
        self.table = ap["table"]
        self.pos = ap["pos"]
        self.gamma = ap["gamma"]
        self.beta = ap["beta"]
        self.ln1 = ap["ln1"]
        self.ln2 = ap["ln2"]
        self.wqk = ap["wqk"]
        self.wv = ap["wv"]
        self.proj = ap["proj"]
        self.projb = ap["projb"]
        self.rmsw = ap["rmsw"]
        self.lam1 = ap["lam1"]
        self.lam2 = ap["lam2"]
        self.fc1 = ap["fc1"]
        self.fc1b = ap["fc1b"]
        self.fc2 = ap["fc2"]
        self.fc2b = ap["fc2b"]
        self.wg = ap["wg"]
        self.w1 = ap["w1"]
        self.w2 = ap["w2"]


class Scratch:

    def __init__(self, nc):
        self.qk = nc.dram_tensor("qk_parts", (PARTS, FQK, N), BF16, kind="Internal").ap()
        self.xbuf = nc.dram_tensor("slots_in", (XROWS, D), F32, kind="Internal").ap()
        self.ybuf = nc.dram_tensor("slots_out", (YROWS, D), F32, kind="Internal").ap()


class Resident:

    def __init__(self, sb):
        self.h0 = sb("h0", [P, B, D])
        self.x1 = sb("x1", [P, B, D])
        self.v = sb("v", [P, B, D])
        self.o = sb("o", [P, B, D])
        self.xg = sb("xg", [P, B, D])
        self.logits = sb("logits", [P, B, E])
        self.gate = sb("gate", [P, TOPK, B])
        self.fetch = sb("fetch", [P, TOPK, B], I32)
        self.ident = sb("ident", [P, P])
        self.identb = sb("identb", [P, P], BF16)
        self.ones = sb("ones", [P, P], BF16)
        self.before = sb("before", [P, P], BF16)
        self.eps = sb("eps", [P, 2])
        self.nlam = sb("nlam", [P, NH])
        self.projb = sb("projb", [P, D])
        self.fc2b = sb("fc2b", [P, D])
        self.wproj = sb("wproj", [KH, 2, D])
        self.wfc1 = sb("wfc1", [KH, 2, MLP])
        self.wfc2 = sb("wfc2", [P, MT, D])
        self.wg = sb("wg", [KH, 2, E])
        self.rmsw = sb("rmsw", [KH, 2])
        self.ln2 = sb("ln2", [KH, 2, 2])
        self.fc1b = sb("fc1b", [P, MT])


def credit(engine, *sems):
    for sem in sems:
        engine.nop().then_inc(sem, 1)


class Steps:

    def __init__(self, engine, sem, start=0):
        self.engine, self.sem, self.start, self.n = engine, sem, start, 0

    def mark(self, instruction):
        instruction.then_inc(self.sem, 1)
        self.n += 1

    def settle(self):
        self.engine.wait_ge(self.sem, self.start + self.n)


def over_tiles(row, n):
    return row.unsqueeze(1).broadcast_to([P, n, D])


def moments(dve, steps, stats, mean, var, t):
    me, mo = stats[:, :, 1], stats[:, :, 4]
    n = stats.shape[1]
    a, b, c = t[:, 0, 0:n], t[:, 1, 0:n], t[:, 2, 0:n]
    dve.tensor_tensor(a, me, mo, ALU.subtract)
    dve.tensor_tensor(b, me, mo, ALU.add)
    steps.mark(dve.tensor_tensor(c, stats[:, :, 2], stats[:, :, 5], ALU.add))
    steps.settle()
    dve.tensor_scalar(mean, b, 0.5, None, ALU.mult)
    steps.mark(dve.scalar_tensor_tensor(out=a, in0=a, scalar=0.25, in1=a, op0=ALU.mult, op1=ALU.mult))
    steps.settle()
    return dve.scalar_tensor_tensor(out=var, in0=c, scalar=1.0 / D, in1=a, op0=ALU.mult, op1=ALU.add)


def project_phase(nc, io, m, scratch, ks):
    with ExitStack() as ctx:
        sb = lambda n, s, d=F32: ctx.enter_context(nc.sbuf_tensor(n, s, d))
        sem = lambda n: ctx.enter_context(nc.semaphore(n))
        ids = sb("ids", [P, B], I32)
        emb, normed = m.o, m.xg
        pos = sb("pos", [P, D])
        gamma = sb("gamma", [P, D])
        beta = sb("beta", [P, D])
        lam = sb("lam", [P, 2, NH])
        ln1 = sb("ln1", [KH, 2, 2])
        wqk = sb("wqk", [KH, 2, FQK])
        wv = sb("wv", [KH, 2, D])
        hT = sb("hT", [KH, 2, 2, GT])
        parts = sb("parts", [P, 2, PARTS, GT], BF16)
        rest = sb("rest", [P, 2, GT])
        stats = sb("statsA", [P, B, 6])
        small = sb("smallA", [P, 3, B])
        mv = sb("mvA", [P, 10, B])
        zeros = sb("zeros", [P, D * 8])
        mean0, var0, std0, r0, mean1, var1, std1, r1, v2, r2 = (mv[:, i, :] for i in range(10))
        psT = ctx.enter_context(nc.psum_tensor("psTA", [P, 2, 512], F32))
        psq = ctx.enter_context(nc.psum_tensor("psq", [P, 3, 512], F32))
        psv = ctx.enter_context(nc.psum_tensor("psv", [P, 2, 512], F32))
        ids_in, small_in, pos_in, w_in, rest_in = (sem(x) for x in ("ids_in", "small_in", "pos_in", "w_in", "rest_in"))
        gathered = [sem(f"gathered{g}") for g in range(NG)]
        zeros_out = sem("zeros_out")
        zeros_set, const_set, const_step = sem("zeros_set"), sem("const_set"), sem("const_step")
        emb_ready, var0_ready, std0_ready, n0_ready = (sem(x) for x in ("emb_ready", "var0_ready", "std0_ready", "n0_ready"))
        scaled, h0_ready, var1_ready, std1_ready, v2_ready, std2_ready, normed_ready = (
            sem(x) for x in ("scaled", "h0_ready", "var1_ready", "std1_ready", "v2_ready", "std2_ready", "normed_ready"))
        turned, hT_ready, qk_ready, v_ready, v_kept = (sem(x) for x in ("turned", "hT_ready", "qk_ready", "v_ready", "v_kept"))
        hi_ready, rest_ready, mid_ready, lo_ready = (sem(x) for x in ("hi_ready", "rest_ready", "mid_ready", "lo_ready"))
        parts_out = [sem(f"parts_out{i}") for i in range(2)]
        dve_step = sem("dve_stepA")
        block = ctx.enter_context(nc.Block())

        @block.sync
        def _(sp):
            sp.dma_start(ids[:], io.ids).then_inc(ids_in, 16)
            sp.dma_start(pos[:], io.pos).then_inc(pos_in, 16)
            for dst, src in ((gamma, io.gamma), (beta, io.beta), (m.projb, io.projb), (m.fc2b, io.fc2b)):
                sp.dma_start(dst[:], src.partition_broadcast(P)).then_inc(small_in, 16)
            sp.dma_start(lam[:, 0, :], io.lam1.partition_broadcast(P)).then_inc(small_in, 16)
            sp.dma_start(lam[:, 1, :], io.lam2.partition_broadcast(P)).then_inc(small_in, 16)
            sp.dma_start(ln1[:], io.ln1).then_inc(w_in, 16)
            for dst, src in ((wqk, io.wqk), (wv, io.wv)):
                sp.dma_start(dst[:], src.rearrange("(k p) n -> p k n", k=2)).then_inc(w_in, 16)
            for dst, src in ((m.wproj, io.proj), (m.wfc1, io.fc1), (m.wg, io.wg)):
                sp.dma_start(dst[:], src.rearrange("(k p) n -> p k n", k=2)).then_inc(rest_in, 16)
            sp.dma_start(m.wfc2[:], io.fc2.rearrange("(k p) n -> p k n", k=MT)).then_inc(rest_in, 16)
            for dst, src in ((m.rmsw, io.rmsw), (m.ln2, io.ln2), (m.fc1b, io.fc1b)):
                sp.dma_start(dst[:], src).then_inc(rest_in, 16)
            sp.wait_ge(zeros_set, 1)
            flat = scratch.xbuf[0:SLOT_ROWS, :].rearrange("(c p r) d -> c p (r d)", p=P, r=8)
            for c in range(SLOT_ROWS // (8 * P)):
                sp.dma_start(flat[c], zeros[:]).then_inc(zeros_out, 16)
            sp.dma_start(scratch.ybuf[ZERO_ROW:ZERO_ROW + P, :], zeros[:, 0:D]).then_inc(zeros_out, 16)
            for n in range(NG * QT):
                g, j = n // QT, n % QT
                sp.wait_ge(lo_ready, n + 1)
                dst = scratch.qk[:, j * P:(j + 1) * P, g * GT:(g + 1) * GT].rearrange("c f t -> f c t")
                sp.dma_start(dst, parts[:, n % 2]).then_inc(parts_out[n % 2], 16)
            for i in range(2):
                sp.wait_ge(parts_out[i], 16 * NG * QT // 2)
            sp.wait_ge(zeros_out, 16 * (SLOT_ROWS // (8 * P) + 1))
            sp.wait_ge(rest_in, 16 * 7)
            sp.wait_ge(small_in, 16 * 6)

        @block.gpsimd
        def _(pool):
            steps = Steps(pool, const_step)
            pool.wait_ge(ids_in, 16)
            for b in range(B):
                pool.indirect_dma_start(
                    out=emb[:, b, :], out_offset=None, in_=io.table,
                    in_offset=bass.IndirectOffsetOnAxis(ap=ids[:, b:b + 1], axis=0),
                ).then_inc(gathered[b // G], 16)
                if b == 0:
                    pool.memset(zeros[:], 0.0).then_inc(zeros_set, 1)
                    pool.memset(m.eps[:, 0:1], LN_EPS)
                    pool.memset(m.eps[:, 1:2], RMS_EPS)
                    pool.memset(m.ident[:], 0.0)
                    steps.mark(pool.memset(m.ones[:], 1.0))
                    steps.settle()
                    steps.mark(pool.affine_select(out=m.ident[:], in_=m.ident[:], compare_op=ALU.not_equal, fill=1.0,
                                                  base=0, pattern=[[-1, P]], channel_multiplier=1))
                    pool.affine_select(out=m.before[:], in_=m.ones[:], compare_op=ALU.is_gt, fill=0.0,
                                       base=0, pattern=[[1, P]], channel_multiplier=-1)
                    steps.settle()
                    pool.tensor_copy(m.identb[:], m.ident[:]).then_inc(const_set, 1)
            pool.wait_ge(pos_in, 16)
            pool.wait_ge(small_in, 16 * 6)

            def add_pos(g):
                e = emb[:, g * G:(g + 1) * G, :]
                pool.wait_ge(gathered[g], 16 * G)
                pool.tensor_tensor(e, e, over_tiles(pos[:], G), ALU.add).then_inc(emb_ready, 1)

            def affine(g):
                h = m.h0[:, g * G:(g + 1) * G, :]
                pool.wait_ge(n0_ready, g + 1)
                pool.tensor_tensor(h, h, over_tiles(gamma[:], G), ALU.mult).then_inc(scaled, 1)
                pool.wait_ge(scaled, g + 1)
                pool.tensor_tensor(h, h, over_tiles(beta[:], G), ALU.add).then_inc(h0_ready, 1)

            def low_part(n):
                pool.wait_ge(mid_ready, n + 1)
                pool.tensor_tensor(parts[:, n % 2, 2, :], rest[:, n % 2, :], parts[:, n % 2, 1, :],
                                   ALU.subtract).then_inc(lo_ready, 1)

            add_pos(0)
            affine(0)
            for g in range(NG):
                if g + 1 < NG:
                    add_pos(g + 1)
                    affine(g + 1)
                for j in range(QT):
                    low_part(g * QT + j)

        @block.scalar
        def _(act):
            act.wait_ge(const_set, 1)

            def roots(g):
                T = slice(g * G, (g + 1) * G)
                act.wait_ge(var0_ready, g + 1)
                nc.scalar.activation(std0[:, T], var0[:, T], ACT.Sqrt, bias=m.eps[:, 0:1]).then_inc(std0_ready, 1)
                act.wait_ge(var1_ready, g + 1)
                nc.scalar.activation(std1[:, T], var1[:, T], ACT.Sqrt, bias=m.eps[:, 0:1]).then_inc(std1_ready, 1)
                act.wait_ge(v2_ready, g + 1)
                nc.scalar.activation(r2[:, T], v2[:, T], ACT.Sqrt, bias=m.eps[:, 0:1]).then_inc(std2_ready, 1)

            def split(n):
                act.wait_ge(qk_ready, n + 1)
                if n >= 2:
                    act.wait_ge(parts_out[n % 2], 16 * (n // 2))
                nc.scalar.activation(parts[:, n % 2, 0, :], psq[:, n % 3, :], ACT.Copy).then_inc(hi_ready, 1)
                act.wait_ge(rest_ready, n + 1)
                nc.scalar.activation(parts[:, n % 2, 1, :], rest[:, n % 2, :], ACT.Copy).then_inc(mid_ready, 1)

            roots(0)
            act.wait_ge(w_in, 16 * 3)
            for g in range(NG):
                act.wait_ge(turned, g + 1)
                if g >= 2:
                    act.wait_ge(v_ready, 2 * (g - 1))
                for k in range(2):
                    last = nc.scalar.activation(hT[:, g % 2, k, :], psT[0:KH, k, :], ACT.Identity,
                                                bias=ln1[:, 1, k:k + 1], scale=ln1[:, 0, k:k + 1])
                last.then_inc(hT_ready, 1)
                if g + 1 < NG:
                    roots(g + 1)
                for j in range(QT):
                    split(g * QT + j)

        @block.vector
        def _(dve):
            st = Steps(dve, dve_step)

            def norms(g):
                T = slice(g * G, (g + 1) * G)
                tiles = range(g * G, (g + 1) * G)
                dve.wait_ge(emb_ready, g + 1)
                for b in tiles:
                    last = dve.bn_stats(stats[:, b, :], emb[:, b, :])
                st.mark(last)
                st.settle()
                moments(dve, st, stats[:, T, :], mean0[:, T], var0[:, T], small).then_inc(var0_ready, 1)
                dve.wait_ge(std0_ready, g + 1)
                st.mark(dve.reciprocal(r0[:, T], std0[:, T]))
                st.settle()
                for b in tiles:
                    last = dve.tensor_scalar(m.h0[:, b, :], emb[:, b, :], mean0[:, b:b + 1], r0[:, b:b + 1],
                                             ALU.subtract, ALU.mult)
                last.then_inc(n0_ready, 1)
                dve.wait_ge(h0_ready, g + 1)
                for b in tiles:
                    last = dve.bn_stats(stats[:, b, :], m.h0[:, b, :])
                st.mark(last)
                st.settle()
                moments(dve, st, stats[:, T, :], mean1[:, T], var1[:, T], small).then_inc(var1_ready, 1)
                dve.wait_ge(std1_ready, g + 1)
                st.mark(dve.reciprocal(r1[:, T], std1[:, T]))
                st.settle()
                st.mark(dve.tensor_tensor(v2[:, T], var1[:, T], r1[:, T], ALU.mult))
                st.settle()
                dve.tensor_tensor(v2[:, T], v2[:, T], r1[:, T], ALU.mult).then_inc(v2_ready, 1)
                for b in tiles:
                    last = dve.tensor_scalar(m.x1[:, b, :], m.h0[:, b, :], mean1[:, b:b + 1], r1[:, b:b + 1],
                                             ALU.subtract, ALU.mult)
                st.mark(last)
                dve.wait_ge(std2_ready, g + 1)
                st.mark(dve.reciprocal(v2[:, T], r2[:, T]))
                st.settle()
                for b in tiles:
                    last = dve.tensor_scalar(normed[:, b, :], m.x1[:, b, :], v2[:, b:b + 1], None, ALU.mult)
                last.then_inc(normed_ready, 1)

            dve.memset(ks[KS:P, :, :, :], 1.0)
            dve.wait_ge(small_in, 16 * 6)
            st.mark(dve.tensor_tensor(m.nlam[:], lam[:, 1, :], lam[:, 0, :], ALU.subtract))
            st.settle()
            st.mark(dve.tensor_scalar(m.nlam[:], m.nlam[:], -LAMBDA_INIT, None, ALU.add))
            norms(0)
            for g in range(NG):
                if g + 1 < NG:
                    norms(g + 1)
                for j in range(QT):
                    n = g * QT + j
                    dve.wait_ge(hi_ready, n + 1)
                    if n >= 2:
                        dve.wait_ge(lo_ready, n - 1)
                    dve.tensor_tensor(rest[:, n % 2, :], psq[:, n % 3, :], parts[:, n % 2, 0, :],
                                      ALU.subtract).then_inc(rest_ready, 1)
                for i in range(2):
                    dve.wait_ge(v_ready, 2 * g + i + 1)
                    b = g * G + 2 * i
                    dve.tensor_copy(m.v[:, b:b + 2, :], psv[:, i, 0:2 * D].rearrange("p (b d) -> p b d", b=2)).then_inc(v_kept, 1)

        @block.tensor
        def _(pe):
            pe.wait_ge(const_set, 1)
            pe.wait_ge(w_in, 16 * 3)

            def turn(g):
                pe.wait_ge(normed_ready, g + 1)
                if g:
                    pe.wait_ge(hT_ready, g)
                for k in range(2):
                    for t in range(G):
                        last = pe.transpose(psT[0:KH, k, t * P:(t + 1) * P],
                                            normed[:, g * G + t, k * KH:(k + 1) * KH], m.ident[:])
                last.then_inc(turned, 1)

            turn(0)
            for g in range(NG):
                pe.wait_ge(hT_ready, g + 1)
                for j in range(QT):
                    n = g * QT + j
                    if n >= 3:
                        pe.wait_ge(rest_ready, n - 2)
                    for k in range(2):
                        last = pe.matmul(psq[:, n % 3, :], wqk[:, k, j * P:(j + 1) * P], hT[:, g % 2, k, :],
                                         start=(k == 0), stop=(k == 1))
                    last.then_inc(qk_ready, 1)
                if g + 1 < NG:
                    turn(g + 1)
                for i in range(2):
                    if g:
                        pe.wait_ge(v_kept, 2 * (g - 1) + i + 1)
                    for t in range(2 * i, 2 * i + 2):
                        for k in range(2):
                            last = pe.matmul(psv[:, i, (t % 2) * D:(t % 2 + 1) * D], hT[:, g % 2, k, t * P:(t + 1) * P],
                                             wv[:, k, :], start=(k == 0), stop=(k == 1))
                    last.then_inc(v_ready, 1)


def attention_phase(nc, m, scratch, qs, ks):
    R = NH // 2
    HH = NHS // 2
    with ExitStack() as ctx:
        sb = lambda n, s, d=F32: ctx.enter_context(nc.sbuf_tensor(n, s, d))
        ps = lambda n, s, d=F32: ctx.enter_context(nc.psum_tensor(n, s, d))
        sem = lambda n: ctx.enter_context(nc.semaphore(n))
        ex = sb("ex", [P, 6, 512])
        vcur = sb("vcur", [P, 2, NH, 32])
        nmax = sb("nmax", [P, 2, HH])
        nrest = sb("nrest", [P, 2, HH])
        mparts = sb("mparts", [P, 2, 2 * PARTS, HH], BF16)
        mT = sb("mT", [PARTS * HH, 2, P], BF16)
        oT = sb("oTB", [P, 3, 2 * P])
        rs = sb("rs", [P, 6, 4])
        o1 = sb("o1", [P, 3, 4, HD])
        o2 = sb("o2", [P, 3, 4, HD])
        psS = ps("psS", [P, 2, 4, P])
        psE = ps("psE", [P, 2, 4, P])
        psO = ps("psO", [P, 4, 256])
        psR = ps("psR", [P, 8, P])
        psM = [psR[0:2 * PARTS * HH, 6 + i, 0:P // 2].bitcast(BF16) for i in range(2)]
        stacked = [sem(f"stacked{i}") for i in range(2)]
        max_in = [[sem(f"max_in{i}_{j}") for j in range(2)] for i in range(4)]
        sums_set, zeros_set, v_cur = sem("sums_set"), sem("zeros_setB"), sem("v_cur")
        s_ready, s_max, m_split, m_turned, mT_ready = (sem(x) for x in ("s_ready", "s_max", "m_split", "m_turned", "mT_ready"))
        st_ready, exp_ready, pv_ready, oT_ready, o_turned, o_normed = (
            sem(x) for x in ("st_ready", "exp_ready", "pv_ready", "oT_ready", "o_turned", "o_normed"))
        dve_step = sem("dve_stepB")
        block = ctx.enter_context(nc.Block())
        DM, DN = 2 * 3, 3

        def body(i, last, step):
            for c in range(4):
                step(4 * i + c, c, last and c == 3)

        def loop(engine, step):
            with engine.Fori(0, B // 4 - 1) as i:
                body(i, False, step)
            body(B // 4 - 1, True, step)

        @block.sync
        def _(sp):
            def load(pair, par):
                for dst, slots, row in ((qs, Q_SLOTS, 0), (ks, K_SLOTS, NHS * HD)):
                    for j, part in enumerate(slots):
                        src = scratch.qk[part, row:row + NHS * HD, ds(pair * 2 * P, 2 * P)]
                        sp.dma_start(dst[j * HD:(j + 1) * HD, par, :, :],
                                     src.rearrange("(h r) t -> r h t", r=HD)).then_inc(stacked[par], 16)

            def maxima(b, c, i):
                for half in range(2):
                    sp.wait_ge(mT_ready, 2 * b + half + 1)
                    for t in range(PARTS):
                        sp.dma_start(qs[KS + t:KS + t + 1, c // 2, half * HH:(half + 1) * HH, (c % 2) * P:(c % 2 + 1) * P],
                                     mT[t * HH:(t + 1) * HH, half, :]).then_inc(max_in[c][half], 16)

            load(0, 0)
            load(1, 1)
            maxima(0, 0, 0)

            def step(b, c, end):
                if not end:
                    maxima(b + 1, (c + 1) % 4, None)
                if c % 2 == 1 and step.more:
                    sp.wait_ge(st_ready, R * (b + 1))
                    load(2 * step.i + c // 2 + 2, c // 2)

            with sp.Fori(0, B // 4 - 1) as i:
                step.i, step.more = i, True
                body(i, False, step)
            step.more = False
            body(B // 4 - 1, True, step)

        @block.gpsimd
        def _(pool):
            pool.memset(vcur[:], 1.0).then_inc(sums_set, 1)
            pool.wait_ge(sums_set, 1)
            pool.memset(mparts[:, :, PARTS:, :], 0.0).then_inc(zeros_set, 1)

            def copy(b, c):
                pool.tensor_copy(vcur[:, c % 2, :, 0:HD],
                                 m.v[:, ds(b, 1), :].rearrange("p o (h d) -> p (o h) d", h=NH)).then_inc(v_cur, 1)

            def step(b, c, end):
                if not end:
                    pool.wait_ge(pv_ready, 2 * b + 1)
                    copy(b + 1, (c + 1) % 4)

            pool.wait_ge(zeros_set, 1)
            copy(0, 0)
            loop(pool, step)

        @block.tensor
        def _(pe):
            def scores(b, c, r):
                par, T = c // 2, slice((c % 2) * P, (c % 2 + 1) * P)
                if not (isinstance(b, int) and b == 0 and r < 2):
                    pe.wait_ge(s_max, b * R + r - 1)
                for x in range(4):
                    h = 4 * r + x
                    last = pe.matmul(psS[:, r % 2, x, :], qs[0:KS, par, h, T], ks[0:KS, par, h, T],
                                     start=True, stop=True)
                last.then_inc(s_ready, 1)

            def turn_maxima(b, half):
                pe.wait_ge(m_split, 2 * b + half + 1)
                if half:
                    pe.wait_ge(mT_ready, 2 * b + 1)
                elif not (isinstance(b, int) and b == 0):
                    pe.wait_ge(o_normed, b)
                pe.transpose(psM[half], mparts[:, half, :, :].rearrange("p a h -> p (a h)"), m.identb[:]).then_inc(m_turned, 1)

            def step(b, c, end):
                par, T = c // 2, slice((c % 2) * P, (c % 2 + 1) * P)
                nxt = (c + 1) % 4
                def values(r):
                    pe.wait_ge(exp_ready, R * b + r + 2)
                    if r == 0:
                        pe.wait_ge(v_cur, b + 1)
                        pe.wait_ge(oT_ready, 2 * b + 1)
                    for x in range(2):
                        h = 2 * r + x
                        q = 32 * (h % 4)
                        last = pe.matmul(psO[q:q + 32, h // 4, :], vcur[:, c % 2, h, :],
                                         ex[:, r, x * 256:(x + 1) * 256], start=True, stop=True)
                    if r in (R - 3, R - 1):
                        last.then_inc(pv_ready, 1)

                if not end and nxt % 2 == 0:
                    pe.wait_ge(stacked[nxt // 2], 16 * 12 * (step.i + (2 if nxt == 0 else 1)))
                for r in range(R):
                    pe.wait_ge(exp_ready, R * b + max(r, 1))
                    if r % (R // 2) == 0:
                        pe.wait_ge(max_in[c][r // (R // 2)], 16 * PARTS * (step.i + 1))
                    for x in range(4):
                        h = 4 * r + x
                        last = pe.matmul(psE[:, r % 2, x, :], ks[0:KM, par, h, T], qs[0:KM, par, h, T],
                                         start=True, stop=True)
                    last.then_inc(st_ready, 1)
                    if not end:
                        for q in ((0, 1), (2,), (3,), (4,), (5,), ())[r]:
                            scores(b + 1, nxt, q)
                        if r == 4:
                            turn_maxima(b + 1, 0)
                    if r >= 2:
                        values(r - 2)
                values(R - 2)
                if not end:
                    turn_maxima(b + 1, 1)
                values(R - 1)
                if not end:
                    pe.wait_ge(mT_ready, 2 * b + 4)
                else:
                    pe.wait_ge(o_normed, b + 1)
                for x in range(6):
                    if x % 4 == 0:
                        pe.wait_ge(oT_ready, 2 * b + 2 + x // 4)
                    last = pe.transpose(psR[:, x, :], oT[:, x // 2, (x % 2) * P:(x % 2 + 1) * P], m.ident[:])
                last.then_inc(o_turned, 1)

            credit(pe, pv_ready, o_turned)
            pe.wait_ge(stacked[0], 16 * 12)
            pe.wait_ge(zeros_set, 1)
            for r in range(R):
                scores(0, 0, r)
            turn_maxima(0, 0)
            turn_maxima(0, 1)
            with pe.Fori(0, B // 4 - 1) as i:
                step.i = i
                body(i, False, step)
            step.i = B // 4 - 1
            body(B // 4 - 1, True, step)

        @block.scalar
        def _(act):
            def turn_maxima(b, c, half):
                act.wait_ge(m_turned, 2 * b + half + 1)
                if not (isinstance(b, int) and b == 0):
                    before = max_in[(c - 1) % 4][half]
                    act.wait_ge(before, 16 * PARTS * (turn_maxima.i + (0 if c == 0 else 1)))
                nc.scalar.activation(mT[:, half, :], psM[half][0:PARTS * HH, :], ACT.Copy).then_inc(mT_ready, 1)

            def step(b, c, end):
                for r in range(R):
                    act.wait_ge(st_ready, R * b + r + 1)
                    if r == 0:
                        act.wait_ge(pv_ready, 2 * b + 1)
                    nc.scalar.activation(ex[:, r, :].rearrange("p (x q) -> p x q", x=4), psE[:, r % 2], ACT.Exp,
                                         scale=HD ** -0.5).then_inc(exp_ready, 1)
                    if not end and r in (4, 5):
                        turn_maxima(b + 1, (c + 1) % 4, r - 4)
                act.wait_ge(o_turned, b + 1)
                for bank, H in ((0, slice(0, 2)), (1, slice(2, 3))):
                    act.wait_ge(pv_ready, 2 * b + 2 + bank)
                    nc.scalar.activation(oT[:, H, :], psO[:, H, :], ACT.Copy).then_inc(oT_ready, 1)

            credit(act, exp_ready, oT_ready)
            turn_maxima(0, 0, 0)
            turn_maxima(0, 0, 1)
            with act.Fori(0, B // 4 - 1) as i:
                turn_maxima.i = i
                body(i, False, step)
            turn_maxima.i = B // 4 - 1
            body(B // 4 - 1, True, step)

        @block.vector
        def _(dve):
            def maxima(b, st):
                for r in range(R):
                    half, k = divmod(r, R // 2)
                    dve.wait_ge(s_ready, R * b + r + 1)
                    if k == 0 and not (isinstance(b, int) and b == 0):
                        dve.wait_ge(m_split, 2 * b - 1 + half)
                    dve.tensor_reduce(nmax[:, half, 4 * k:4 * k + 4], psS[:, r % 2], AX.X, ALU.max,
                                      negate=True).then_inc(s_max, 1)
                    if k < R // 2 - 1:
                        continue
                    n, w = nmax[:, half, :], nrest[:, half, :]
                    dve.wait_ge(s_max, R * b + r + 1)
                    if not (isinstance(b, int) and b == 0):
                        dve.wait_ge(m_turned, 2 * b - 1 + half)
                    st.mark(dve.tensor_copy(mparts[:, half, 0, :], n))
                    st.settle()
                    st.mark(dve.tensor_tensor(w, n, mparts[:, half, 0, :], ALU.subtract))
                    st.settle()
                    st.mark(dve.tensor_copy(mparts[:, half, 1, :], w))
                    st.settle()
                    dve.tensor_tensor(mparts[:, half, 2, :], w, mparts[:, half, 1, :], ALU.subtract).then_inc(m_split, 1)

            def step(b, c, end):
                st = Steps(dve, dve_step, (DM + DN) * b + DM)
                if not end:
                    maxima(b + 1, st)
                dve.wait_ge(o_turned, b + 2)
                o = psR[:, 0:6, :].rearrange("p (g s) (h w) -> p g s h w", s=2, h=4)
                r4 = rs[:].rearrange("p (g s) h -> p g s h", s=2)
                st.mark(dve.reciprocal(rs[:], psR[:, 0:6, :].rearrange("p x (h w) -> p x h w", h=4)[:, :, :, HD]))
                st.settle()
                st.mark(dve.tensor_tensor(r4[:, :, 1, :], r4[:, :, 1, :], m.nlam[:].rearrange("p (g h) -> p g h", g=3), ALU.mult))
                st.settle()
                wide = lambda s: r4[:, :, s, :].unsqueeze(3).broadcast_to([P, 3, 4, HD])
                dve.tensor_tensor(o1[:], o[:, :, 0, :, 0:HD], wide(0), ALU.mult)
                st.mark(dve.tensor_tensor(o2[:], o[:, :, 1, :, 0:HD], wide(1), ALU.mult))
                st.settle()
                dve.tensor_tensor(m.o[:, ds(b, 1), :].rearrange("p o d -> p (o d)"),
                                  o1[:].rearrange("p g h d -> p (g h d)"),
                                  o2[:].rearrange("p g h d -> p (g h d)"), ALU.add).then_inc(o_normed, 1)

            credit(dve, o_normed)
            maxima(0, Steps(dve, dve_step))
            loop(dve, step)


def mlp_phase(nc, m):
    with ExitStack() as ctx:
        sb = lambda n, s, d=F32: ctx.enter_context(nc.sbuf_tensor(n, s, d))
        ps = lambda n, s, d=F32: ctx.enter_context(nc.psum_tensor(n, s, d))
        sem = lambda n: ctx.enter_context(nc.semaphore(n))
        staged = sb("staged", [P, 2, G, D])
        fT = sb("fT", [KH, 2, 2, GT])
        gT = sb("gT", [P, 2, MT, GT])
        stats = sb("statsC", [P, B, 6])
        small = sb("smallC", [P, 3, B])
        mv = sb("mvC", [P, 4, B])
        mean, var, std, rr = (mv[:, i, :] for i in range(4))
        psT = ps("psTC", [P, 2, 512])
        psG = ps("psG", [P, 3, 512])
        psY = ps("psY", [P, 2, 512])
        psL = ps("psL", [P, 512])
        var_ready, std_ready, staged_ready, turned, fT_ready, y_ready, y_kept, rows_ready = (
            sem(x) for x in ("var_ready", "std_ready", "staged_ready", "turnedC", "fT_ready", "y_ready", "y_kept", "rows_ready"))
        g_ready, gelu_ready, pool_step, dve_step, l_ready = (sem(x) for x in ("g_ready", "gelu_ready", "pool_stepC", "dve_stepC", "l_ready"))
        block = ctx.enter_context(nc.Block())
        ROUNDS = [(s, g) for s in range(3) for g in range(NG)]

        @block.vector
        def _(dve):
            st = Steps(dve, dve_step)
            n = 0
            for s in range(3):
                src = (m.o, m.x1, m.h0)[s]
                if s:
                    pass
                for b in range(B):
                    if s and b % G == 0:
                        dve.wait_ge(rows_ready, NG * (s - 1) + b // G + 1)
                    last = dve.bn_stats(stats[:, b, :], src[:, b, :])
                st.mark(last)
                st.settle()
                last = moments(dve, st, stats[:], mean, var, small)
                if s == 0:
                    st.mark(last)
                    st.mark(dve.tensor_tensor(std, mean, mean, ALU.mult))
                    st.settle()
                    last = dve.tensor_tensor(var, var, std, ALU.add)
                last.then_inc(var_ready, 1)
                dve.wait_ge(std_ready, s + 1)
                st.mark(dve.reciprocal(rr, std))
                st.settle()

                def stage(g):
                    k = NG * s + g
                    if k >= 2:
                        dve.wait_ge(turned, k - 1)
                    for t in range(G):
                        b = g * G + t
                        if s == 0:
                            last = dve.tensor_scalar(staged[:, k % 2, t, :], src[:, b, :], rr[:, b:b + 1], None, ALU.mult)
                        else:
                            dst = staged[:, k % 2, t, :] if s == 1 else m.xg[:, b, :]
                            last = dve.tensor_scalar(dst, src[:, b, :], mean[:, b:b + 1], rr[:, b:b + 1],
                                                     ALU.subtract, ALU.mult)
                    last.then_inc(staged_ready, 1)

                stage(0)
                for g in range(NG):
                    if g + 1 < NG:
                        stage(g + 1)
                    if s == 2:
                        continue
                    for i in range(2):
                        dve.wait_ge(y_ready, n + 1)
                        b = g * G + 2 * i
                        x = m.x1[:, b:b + 2, :]
                        dst = x if s == 0 else m.o[:, b:b + 2, :]
                        dve.tensor_tensor(dst, psY[:, i, 0:2 * D].rearrange("p (b d) -> p b d", b=2), x,
                                          ALU.add).then_inc(y_kept, 1)
                        n += 1
            dve.wait_ge(l_ready, 1)
            dve.tensor_copy(m.logits[:], psL[:, 0:B * E].rearrange("p (b e) -> p b e", e=E))

        @block.gpsimd
        def _(pool):
            st = Steps(pool, pool_step)
            for g in range(NG):
                x = m.x1[:, g * G:(g + 1) * G, :]
                pool.wait_ge(y_kept, 2 * (g + 1))
                pool.tensor_tensor(x, x, over_tiles(m.projb[:], G), ALU.add).then_inc(rows_ready, 1)
            for g in range(NG):
                h, y = m.h0[:, g * G:(g + 1) * G, :], m.o[:, g * G:(g + 1) * G, :]
                st.mark(pool.tensor_tensor(h, h, over_tiles(m.fc2b[:], G), ALU.add))
                st.settle()
                pool.wait_ge(y_kept, 2 * NG + 2 * (g + 1))
                pool.tensor_tensor(h, h, y, ALU.add).then_inc(rows_ready, 1)

        @block.scalar
        def _(act):
            for s in range(3):
                act.wait_ge(var_ready, s + 1)
                nc.scalar.activation(std, var, ACT.Sqrt, bias=m.eps[:, 1:2] if s == 0 else m.eps[:, 0:1]).then_inc(std_ready, 1)
                for g in range(NG):
                    k = NG * s + g
                    act.wait_ge(turned, k + 1)
                    if k >= 2:
                        act.wait_ge(y_ready, 2 * (k - 1) if k - 2 < 2 * NG else 4 * NG + k - 2 * NG - 1)
                    for h in range(2):
                        src, dst = psT[0:KH, h, :], fT[:, k % 2, h, :]
                        if s == 0:
                            last = nc.scalar.activation(dst, src, ACT.Identity, scale=m.rmsw[:, h:h + 1])
                        elif s == 1:
                            last = nc.scalar.activation(dst, src, ACT.Identity, bias=m.ln2[:, 1, h:h + 1], scale=m.ln2[:, 0, h:h + 1])
                        else:
                            last = nc.scalar.activation(dst, src, ACT.Identity)
                    last.then_inc(fT_ready, 1)
                    if s == 1:
                        for j in range(MT):
                            n = g * MT + j
                            act.wait_ge(g_ready, n + 1)
                            if j == 0 and g >= 2:
                                act.wait_ge(y_ready, 2 * NG + 2 * (g - 1))
                            nc.scalar.activation(gT[:, g % 2, j, :], psG[:, n % 3, :], ACT.Gelu,
                                                 bias=m.fc1b[:, j:j + 1]).then_inc(gelu_ready, 1)

        @block.tensor
        def _(pe):
            def turn(k):
                s, g = ROUNDS[k]
                pe.wait_ge(staged_ready, k + 1)
                if k:
                    pe.wait_ge(fT_ready, k)
                for h in range(2):
                    for t in range(G):
                        src = staged[:, k % 2, t, :] if s < 2 else m.xg[:, g * G + t, :]
                        last = pe.transpose(psT[0:KH, h, t * P:(t + 1) * P], src[:, h * KH:(h + 1) * KH], m.ident[:])
                last.then_inc(turned, 1)

            n = 0
            turn(0)
            for k, (s, g) in enumerate(ROUNDS):
                pe.wait_ge(fT_ready, k + 1)
                if s == 1:
                    for j in range(MT):
                        q = g * MT + j
                        if q >= 3:
                            pe.wait_ge(gelu_ready, q - 2)
                        for h in range(2):
                            last = pe.matmul(psG[:, q % 3, :], m.wfc1[:, h, j * P:(j + 1) * P], fT[:, k % 2, h, :],
                                             start=(h == 0), stop=(h == 1))
                        last.then_inc(g_ready, 1)
                if g + 1 < NG:
                    turn(k + 1)
                if s == 2:
                    for t in range(G):
                        b = g * G + t
                        for h in range(2):
                            last = pe.matmul(psL[:, b * E:(b + 1) * E], fT[:, k % 2, h, t * P:(t + 1) * P], m.wg[:, h, :],
                                             start=(h == 0), stop=(h == 1))
                    last.then_inc(y_ready, 1)
                    if g == NG - 1:
                        pe.wait_ge(y_ready, 4 * NG + NG)
                        pe.nop().then_inc(l_ready, 1)
                    continue
                if s == 1:
                    pe.wait_ge(gelu_ready, MT * (g + 1))
                for i in range(2):
                    if n >= 2:
                        pe.wait_ge(y_kept, n - 1)
                    for t in range(2 * i, 2 * i + 2):
                        out = psY[:, i, (t % 2) * D:(t % 2 + 1) * D]
                        T = slice(t * P, (t + 1) * P)
                        if s == 0:
                            for h in range(2):
                                last = pe.matmul(out, fT[:, k % 2, h, T], m.wproj[:, h, :], start=(h == 0), stop=(h == 1))
                        else:
                            for j in range(MT):
                                last = pe.matmul(out, gT[:, g % 2, j, T], m.wfc2[:, j, :], start=(j == 0), stop=(j == MT - 1))
                    last.then_inc(y_ready, 1)
                    n += 1
                if g == NG - 1:
                    turn(k + 1)


def route_phase(nc, m, scratch):
    with ExitStack() as ctx:
        sb = lambda n, s, d=F32: ctx.enter_context(nc.sbuf_tensor(n, s, d))
        sem = lambda n: ctx.enter_context(nc.semaphore(n))
        best = sb("best", [P, B, 8])
        besti = sb("besti", [P, B, 8], U32)
        chosen = sb("chosen", [P, TOPK, B])
        hot = sb("hot", [P, TOPK, B, E])
        hotb = sb("hotb", [P, TOPK, B, E], BF16)
        lane = sb("lane", [P, TOPK, B, E])
        picked = sb("picked", [P, TOPK, B, E])
        place = sb("place", [P, TOPK, B])
        keep = sb("keep", [P, TOPK, B])
        gone = sb("gone", [P, TOPK, B])
        row = sb("row", [P, TOPK, B])
        alt = sb("alt", [P, TOPK, B])
        t1 = sb("t1", [P, TOPK, B])
        e1 = sb("e1", [P, B])
        den = sb("den", [P, B])
        send = sb("send", [P, TOPK, B], I32)
        psC = ctx.enter_context(nc.psum_tensor("psC", [P, TOPK, B, E], F32))
        lane_set, hot_ready, counted, gap_ready, exp_ready, send_ready, sent = (
            sem(x) for x in ("lane_set", "hot_ready", "counted", "gap_ready", "exp_readyD", "send_ready", "sent"))
        dve_step = sem("dve_stepD")
        block = ctx.enter_context(nc.Block())

        @block.gpsimd
        def _(pool):
            pool.iota(lane[:], pattern=[[0, TOPK * B], [1, E]], base=0, channel_multiplier=0,
                      allow_small_or_imprecise_dtypes=True).then_inc(lane_set, 1)
            pool.iota(alt[:], pattern=[[1, TOPK * B]], base=0, channel_multiplier=0,
                      allow_small_or_imprecise_dtypes=True).then_inc(lane_set, 1)
            pool.iota(gone[:], pattern=[[P, TOPK * B]], base=DROP_ROW, channel_multiplier=1,
                      allow_small_or_imprecise_dtypes=True).then_inc(lane_set, 1)
            pool.wait_ge(send_ready, 1)
            for k in range(TOPK):
                for b in range(B):
                    pool.indirect_dma_start(
                        out=scratch.xbuf, out_offset=bass.IndirectOffsetOnAxis(ap=send[:, k, b:b + 1], axis=0),
                        in_=m.xg[:, b, :], in_offset=None).then_inc(sent, 16)
            pool.wait_ge(sent, 16 * TOPK * B)

        @block.scalar
        def _(act):
            act.wait_ge(gap_ready, 1)
            nc.scalar.activation(e1[:], den[:], ACT.Exp).then_inc(exp_ready, 1)

        @block.tensor
        def _(pe):
            pe.wait_ge(hot_ready, 1)
            pe.matmul(psC[:], m.before[:], hotb[:], start=True, stop=False, skip_group_check=True)
            for d in range(1, B):
                last = pe.matmul(psC[:, :, d:B, :], m.ones[:], hotb[:, :, 0:B - d, :], start=False,
                                 stop=(d == B - 1), skip_group_check=True)
            last.then_inc(counted, 1)

        @block.vector
        def _(dve):
            st = Steps(dve, dve_step)
            for b in range(B):
                last = dve.max(best[:, b, :], m.logits[:, b, :])
            st.mark(last)
            st.settle()
            for b in range(B):
                last = dve.max_index(besti[:, b, :], best[:, b, :], m.logits[:, b, :])
            st.mark(last)
            st.settle()
            for k in range(TOPK):
                last = dve.tensor_copy(chosen[:, k, :], besti[:, :, k])
            st.mark(last)
            st.mark(dve.tensor_tensor(den[:], best[:, :, 1], best[:, :, 0], ALU.subtract))
            st.settle()
            dve.nop().then_inc(gap_ready, 1)
            dve.wait_ge(lane_set, 3)
            for k in range(TOPK):
                last = dve.tensor_tensor(hot[:, k], lane[:, k], chosen[:, k, :].unsqueeze(2).broadcast_to([P, B, E]),
                                         ALU.is_equal)
            st.mark(last)
            st.settle()
            dve.tensor_copy(hotb[:], hot[:]).then_inc(hot_ready, 1)
            dve.wait_ge(exp_ready, 1)
            st.mark(dve.tensor_scalar(den[:], e1[:], 1.0, None, ALU.add))
            st.settle()
            st.mark(dve.reciprocal(m.gate[:, 0, :], den[:]))
            st.settle()
            st.mark(dve.tensor_tensor(m.gate[:, 1, :], m.gate[:, 0, :], e1[:], ALU.mult))
            dve.wait_ge(counted, 1)
            st.mark(dve.tensor_tensor(picked[:], hot[:], psC[:], ALU.mult))
            st.settle()
            st.mark(dve.tensor_reduce(place[:], picked[:], AX.X, ALU.add))
            st.settle()
            st.mark(dve.tensor_scalar(keep[:], place[:], float(CAP), None, ALU.is_lt))
            st.mark(dve.scalar_tensor_tensor(out=row[:], in0=chosen[:], scalar=float(EROWS), in1=place[:],
                                             op0=ALU.mult, op1=ALU.add))
            st.settle()
            st.mark(dve.tensor_scalar(row[:, 1, :], row[:, 1, :], float(CAP), None, ALU.add))
            st.mark(dve.tensor_tensor(m.gate[:], m.gate[:], keep[:], ALU.mult))
            st.settle()
            st.mark(dve.tensor_tensor(t1[:], row[:], gone[:], ALU.subtract))
            st.mark(dve.tensor_scalar(alt[:], row[:], -float(ZERO_ROW), None, ALU.add))
            st.settle()
            st.mark(dve.tensor_tensor(t1[:], t1[:], keep[:], ALU.mult))
            st.mark(dve.tensor_tensor(alt[:], alt[:], keep[:], ALU.mult))
            st.settle()
            dve.tensor_tensor(send[:], t1[:], gone[:], ALU.add).then_inc(send_ready, 1)
            dve.tensor_scalar(m.fetch[:], alt[:], float(ZERO_ROW), None, ALU.add)


def expert_phase(nc, io, m, scratch):
    with ExitStack() as ctx:
        sb = lambda n, s, d=F32: ctx.enter_context(nc.sbuf_tensor(n, s, d))
        ps = lambda n, s, d=F32: ctx.enter_context(nc.psum_tensor(n, s, d))
        sem = lambda n: ctx.enter_context(nc.semaphore(n))
        w1 = sb("w1", [KH, 2, 2, 2 * HF])
        w2 = sb("w2", [P, 2, HF // P, D])
        rows = sb("rows", [P, 2, ST, D])
        xT = sb("xT", [KH, 2, 2, EROWS])
        silu = sb("silu", [P, 2, CAP])
        act_ = sb("act_", [P, 2, HF // P, EROWS])
        y = sb("y", [P, 2, ST, D])
        psT = ps("psTE", [P, 2, 512])
        psU = ps("psU", [P, 4, 512])
        psY = ps("psYE", [P, 2, 512])
        w_in = [sem(f"w_inE{i}") for i in range(2)]
        rows_in = [sem(f"rows_in{i}") for i in range(2)]
        y_out = [sem(f"y_out{i}") for i in range(2)]
        turned, xT_ready, up_ready, silu_ready, act_ready, down_ready, y_kept = (
            sem(x) for x in ("turnedE", "xT_ready", "up_ready", "silu_ready", "act_ready", "down_ready", "y_keptE"))
        act_zeroed, y_free = sem("act_zeroed"), sem("y_free")
        block = ctx.enter_context(nc.Block())
        HT = HF // P
        UPS = HT * TOPK

        def loop(engine, step):
            with engine.Fori(0, E // 2) as i:
                for c in range(2):
                    step(2 * i + c, c, i)

        @block.sync
        def _(sp):
            def load(e, c):
                sp.dma_start(rows[:, c], scratch.xbuf[ds(e * EROWS, EROWS), :].rearrange("(t p) d -> p t d", p=P)).then_inc(rows_in[c], 16)
                sp.dma_start(w1[:, c], io.w1[ds(e * D, D), :].rearrange("(k p) n -> p k n", k=2)).then_inc(w_in[c], 16)
                sp.dma_start(w2[:, c], io.w2[ds(e * HF, HF), :].rearrange("(k p) n -> p k n", k=HT)).then_inc(w_in[c], 16)

            credit(sp, y_free, y_free)
            load(0, 0)
            load(1, 1)

            def step(e, c, i, more):
                sp.wait_ge(y_kept, ST * (e + 1) + 1)
                sp.dma_start(scratch.ybuf[ds(e * EROWS, EROWS), :].rearrange("(t p) d -> p t d", p=P),
                             y[:, c]).then_inc(y_out[c], 16)
                if more:
                    load(e + 2, c)
                sp.wait_ge(y_out[c], 16 * (i + 1))
                sp.nop().then_inc(y_free, 1)

            with sp.Fori(0, E // 2 - 1) as i:
                for c in range(2):
                    step(2 * i + c, c, i, True)
            for c in range(2):
                step(E - 2 + c, c, E // 2 - 1, False)

        @block.tensor
        def _(pe):
            def step(e, c, i):
                pe.wait_ge(rows_in[c], 16 * (i + 1))
                for t in range(ST):
                    pe.wait_ge(xT_ready, ST * e + max(t, 1))
                    for h in range(2):
                        last = pe.transpose(psT[0:KH, t % 2, h * P:(h + 1) * P], rows[:, c, t, h * KH:(h + 1) * KH], m.ident[:])
                    last.then_inc(turned, 1)
                pe.wait_ge(w_in[c], 32 * (i + 1))
                pe.wait_ge(xT_ready, ST * (e + 1) + 1)
                for u in range(UPS):
                    j, k = u // TOPK, u % TOPK
                    T = slice(k * CAP, (k + 1) * CAP)
                    pe.wait_ge(act_ready, UPS * e + max(u, 1))
                    for half in range(2):
                        col = half * HF + j * P
                        for h in range(2):
                            last = pe.matmul(psU[:, 2 * (u % 2) + half, 0:CAP], w1[:, c, h, col:col + P], xT[:, c, h, T],
                                             start=(h == 0), stop=(h == 1))
                    last.then_inc(up_ready, 1)
                pe.wait_ge(act_ready, UPS * (e + 1) + 1)
                for t in range(ST):
                    pe.wait_ge(y_kept, ST * e + max(t, 1))
                    for j in range(HT):
                        last = pe.matmul(psY[:, t % 2, 0:D], act_[:, c, j, t * P:(t + 1) * P], w2[:, c, j, :],
                                         start=(j == 0), stop=(j == HT - 1))
                    last.then_inc(down_ready, 1)

            pe.wait_ge(act_zeroed, 1)
            loop(pe, step)

        @block.scalar
        def _(act):
            def step(e, c, i):
                for u in range(UPS):
                    act.wait_ge(up_ready, UPS * e + u + 1)
                    act.wait_ge(act_ready, UPS * e + max(u, 1))
                    nc.scalar.activation(silu[:, u % 2, :], psU[:, 2 * (u % 2) + 1, 0:CAP], ACT.Silu).then_inc(silu_ready, 1)
                act.wait_ge(y_free, e + 1)
                for t in range(ST):
                    act.wait_ge(down_ready, ST * e + t + 1)
                    nc.scalar.activation(y[:, c, t, :], psY[:, t % 2, 0:D], ACT.Copy).then_inc(y_kept, 1)

            credit(act, y_kept)
            loop(act, step)

        @block.gpsimd
        def _(pool):
            pool.memset(act_[:, :, :, ECAP:EROWS], 0.0).then_inc(act_zeroed, 1)

        @block.vector
        def _(dve):
            def step(e, c, i):
                for t in range(ST):
                    dve.wait_ge(turned, ST * e + t + 1)
                    dve.tensor_copy(xT[:, c, :, t * P:(t + 1) * P],
                                    psT[0:KH, t % 2, 0:2 * P].rearrange("p (h q) -> p h q", h=2)).then_inc(xT_ready, 1)
                for u in range(UPS):
                    j, k = u // TOPK, u % TOPK
                    dve.wait_ge(silu_ready, UPS * e + u + 1)
                    dve.tensor_tensor(act_[:, c, j, k * CAP:(k + 1) * CAP], psU[:, 2 * (u % 2), 0:CAP], silu[:, u % 2, :],
                                      ALU.mult).then_inc(act_ready, 1)

            credit(dve, xT_ready, act_ready)
            loop(dve, step)


def combine_phase(nc, m, scratch, out):
    with ExitStack() as ctx:
        sem = lambda n: ctx.enter_context(nc.semaphore(n))
        back = ctx.enter_context(nc.sbuf_tensor("back", [P, TOPK, B, D], F32))
        fetched = [sem(f"fetched{b}") for b in range(B)]
        first, done, stored = sem("first"), sem("done"), sem("stored")
        block = ctx.enter_context(nc.Block())

        @block.gpsimd
        def _(pool):
            for b in range(B):
                for k in range(TOPK):
                    pool.indirect_dma_start(
                        out=back[:, k, b, :], out_offset=None, in_=scratch.ybuf,
                        in_offset=bass.IndirectOffsetOnAxis(ap=m.fetch[:, k, b:b + 1], axis=0)).then_inc(fetched[b], 16)

        @block.vector
        def _(dve):
            for b in range(B):
                dve.wait_ge(fetched[b], 16 * TOPK)
                h = m.h0[:, b, :]
                dve.scalar_tensor_tensor(out=h, in0=back[:, 0, b, :], scalar=m.gate[:, 0, b:b + 1], in1=h,
                                         op0=ALU.mult, op1=ALU.add).then_inc(first, 1)
                dve.wait_ge(first, b + 1)
                dve.scalar_tensor_tensor(out=h, in0=back[:, 1, b, :], scalar=m.gate[:, 1, b:b + 1], in1=h,
                                         op0=ALU.mult, op1=ALU.add).then_inc(done, 1)

        @block.sync
        def _(sp):
            for g in range(NG):
                sp.wait_ge(done, G * (g + 1))
                T = slice(g * G, (g + 1) * G)
                sp.dma_start(out[T].rearrange("b p d -> p b d"), m.h0[:, T, :]).then_inc(stored, 16)
            sp.wait_ge(stored, 16 * NG)


def build(nc, io, out):
    scratch = Scratch(nc)
    with ExitStack() as ctx:
        def sb(n, s, d=F32):
            return ctx.enter_context(nc.sbuf_tensor(n, s, d))

        m = Resident(sb)
        with nc.sbuf_tensor("qs", [P, 2, NHS, 2 * P], BF16) as qs, nc.sbuf_tensor("ks", [P, 2, NHS, 2 * P], BF16) as ks:
            project_phase(nc, io, m, scratch, ks)
            attention_phase(nc, m, scratch, qs, ks)
        mlp_phase(nc, m)
        route_phase(nc, m, scratch)
        expert_phase(nc, io, m, scratch)
        combine_phase(nc, m, scratch, out)


def kernel(**inputs):
    import concourse.bacc as _bacc
    from concourse.bass_utils import run_bass_kernel_spmd as _run

    a = {k: np.asarray(v) for k, v in inputs.items()}
    columns = lambda w: w.reshape(2, KH).T
    qkv1, qkv2 = (a[f"L0_attn_qkv{i}_w"].T.reshape(D, 3, NH, HD) for i in (1, 2))
    laid = {
        "ids": a["x"].T, "table": a["L0_tok_word_table"], "pos": a["L0_tok_pos_table"],
        "gamma": a["L0_tok_gamma"], "beta": a["L0_tok_beta"],
        "ln1": np.stack([columns(a["L0_attn_ln1_w"]), columns(a["L0_attn_ln1_b"])], 1),
        "ln2": np.stack([columns(a["L0_attn_ln2_w"]), columns(a["L0_attn_ln2_b"])], 1),
        "wqk": np.stack([qkv1[:, 0:2], qkv2[:, 0:2]], 3).reshape(D, FQK), "wv": qkv1[:, 2].reshape(D, D), "proj": a["L0_attn_proj_w"].T,
        "projb": a["L0_attn_proj_b"], "rmsw": columns(a["L0_attn_rms_w"]),
        "lam1": a["L0_attn_lam1"].reshape(NH), "lam2": a["L0_attn_lam2"].reshape(NH),
        "fc1": a["L0_attn_fc1_w"].T, "fc1b": a["L0_attn_fc1_b"].reshape(MT, P).T,
        "fc2": a["L0_attn_fc2_w"].T, "fc2b": a["L0_attn_fc2_b"],
        "wg": a["L0_ffn_Wg"], "w1": a["L0_ffn_W1"].reshape(E * D, 2 * HF), "w2": a["L0_ffn_W2"].reshape(E * HF, D),
    }
    nc = _bacc.Bacc("TRN2", target_bir_lowering=False, num_devices=1)
    arrays, io = {}, {}
    for name, x in laid.items():
        x = np.ascontiguousarray(x)
        arrays[f"in_{name}"] = x
        io[name] = nc.dram_tensor(f"in_{name}", x.shape, mybir.dt.from_np(x.dtype), kind="ExternalInput").ap()
    out = nc.dram_tensor("out", (B, S, D), F32, kind="ExternalOutput").ap()
    build(nc, Inputs(io), out)
    r = _run(nc, [arrays], core_ids=[0])
    return r.results[0]["out"]
```

```python
from contextlib import ExitStack

import numpy as np

import concourse.bass as bass
from concourse import mybir

ALU = mybir.AluOpType
ACT = mybir.ActivationFunctionType
AX = mybir.AxisListType
F32 = mybir.dt.float32
F32R = mybir.dt.float32r
BF16 = mybir.dt.bfloat16
I32 = mybir.dt.int32
U32 = mybir.dt.uint32
ds = bass.ds

P = 128
B, S, V, D = 16, 128, 12564, 192
KH = D // 2
NH, HD = 12, 16
NHS = 2 * NH
G = 4
NG = B // G
GT = G * P
MLP = 4 * D
MT = MLP // P
FQK = 2 * NHS * HD
QT = FQK // P
PARTS = 3
E, TOPK, HF = 8, 2, 512
N = B * S
CAP = int(1.2 * N / E)
SPAN = CAP + CAP % 2
PAD = D // 3
EROWS = 640
ST = EROWS // P
SLOTS = E * ST
LN_EPS, RMS_EPS, LAMBDA_INIT = 1e-5, 1e-6, 0.1
Q_SLOTS = (0, 1, 2, 0, 0, 1)
K_SLOTS = (0, 1, 0, 1, 2, 0)
KS = len(Q_SLOTS) * HD
KM = KS + PARTS


class Inputs:

    def __init__(self, ap):
        self.ids = ap["ids"]
        self.table = ap["table"]
        self.pos = ap["pos"]
        self.gamma = ap["gamma"]
        self.beta = ap["beta"]
        self.ln1 = ap["ln1"]
        self.ln2 = ap["ln2"]
        self.wqk = ap["wqk"]
        self.wv = ap["wv"]
        self.proj = ap["proj"]
        self.projb = ap["projb"]
        self.rmsw = ap["rmsw"]
        self.lam1 = ap["lam1"]
        self.lam2 = ap["lam2"]
        self.fc1 = ap["fc1"]
        self.fc1b = ap["fc1b"]
        self.fc2 = ap["fc2"]
        self.fc2b = ap["fc2b"]
        self.wg = ap["wg"]
        self.w1 = ap["w1"]
        self.w2 = ap["w2"]


class Scratch:

    def __init__(self, nc):
        self.qk = nc.dram_tensor("qk_parts", (2, PARTS, HD, NHS, N), BF16, kind="Internal").ap()
        self.x = nc.dram_tensor("expert_in", (N + P, D + PAD), F32, kind="Internal").ap()
        self.y = nc.dram_tensor("expert_out", (TOPK * N + E * EROWS, D), F32, kind="Internal").ap()


class Resident:

    def __init__(self, sb):
        self.h0 = sb("h0", [P, B, D])
        self.x1 = sb("x1", [P, B, D])
        self.v = sb("v", [P, B, D])
        self.o = sb("o", [P, B, D])
        self.xg = sb("xg", [P, B, D])
        self.logits = sb("logits", [P, B, E])
        self.gate = sb("gate", [P, TOPK, B])
        self.fetch = sb("fetch", [P, SLOTS], I32)
        self.send = sb("send", [P, SLOTS], I32)
        self.ident = sb("ident", [P, P])
        self.identb = sb("identb", [P, P], BF16)
        self.ones = sb("ones", [P, P], BF16)
        self.before = sb("before", [P, P], BF16)
        self.eps = sb("eps", [P, 3])
        self.nlam = sb("nlam", [P, NH])
        self.projb = sb("projb", [P, D])
        self.fc2b = sb("fc2b", [P, D])
        self.wproj = sb("wproj", [KH, 2, D])
        self.wfc1 = sb("wfc1", [KH, 2, MLP])
        self.wfc2 = sb("wfc2", [P, MT, D])
        self.wg = sb("wg", [KH, 2, E])
        self.rmsw = sb("rmsw", [KH, 2])
        self.ln2 = sb("ln2", [KH, 2, 2])
        self.fc1b = sb("fc1b", [P, MT])


def credit(engine, *sems):
    for sem in sems:
        engine.nop().then_inc(sem, 1)


class Steps:

    def __init__(self, engine, sem, start=0):
        self.engine, self.sem, self.start, self.n = engine, sem, start, 0

    def mark(self, instruction):
        instruction.then_inc(self.sem, 1)
        self.n += 1

    def settle(self):
        self.engine.wait_ge(self.sem, self.start + self.n)


def over_tiles(row, n):
    return row.unsqueeze(1).broadcast_to([P, n, D])


def moments(dve, steps, stats, mean, var, t):
    me, mo = stats[:, :, 1], stats[:, :, 4]
    n = stats.shape[1]
    a, b, c = t[:, 0, 0:n], t[:, 1, 0:n], t[:, 2, 0:n]
    dve.tensor_tensor(a, me, mo, ALU.subtract)
    dve.tensor_tensor(b, me, mo, ALU.add)
    steps.mark(dve.tensor_tensor(c, stats[:, :, 2], stats[:, :, 5], ALU.add))
    steps.settle()
    dve.tensor_scalar(mean, b, 0.5, None, ALU.mult)
    steps.mark(dve.scalar_tensor_tensor(out=a, in0=a, scalar=0.25, in1=a, op0=ALU.mult, op1=ALU.mult))
    steps.settle()
    return dve.scalar_tensor_tensor(out=var, in0=c, scalar=1.0 / D, in1=a, op0=ALU.mult, op1=ALU.add)


def project_phase(nc, io, m, scratch, qs, ks, stacked):
    NB, NQ = 4, 4
    STACK = 2 * QT + 1
    with ExitStack() as ctx:
        sb = lambda n, s, d=F32: ctx.enter_context(nc.sbuf_tensor(n, s, d))
        sem = lambda n: ctx.enter_context(nc.semaphore(n))
        ids = sb("ids", [P, B], I32)
        emb, normed = m.o, m.xg
        pos = sb("pos", [P, D])
        gamma = sb("gamma", [P, D])
        beta = sb("beta", [P, D])
        lam = sb("lam", [P, 2, NH])
        ln1 = sb("ln1", [KH, 2, 2])
        wqk = sb("wqk", [KH, 2, FQK])
        wv = sb("wv", [KH, 2, D])
        hT = sb("hT", [KH, 2, 2, GT])
        parts = sb("parts", [P, NB, PARTS, GT], BF16)
        rest = sb("rest", [P, NB, GT])
        stats = sb("statsA", [P, B, 6])
        small = sb("smallA", [P, 3, B])
        mv = sb("mvA", [P, 10, B])
        mean0, var0, std0, r0, mean1, var1 = (mv[:, i, :] for i in range(6))
        stds, rs = mv[:, 6:8, :], mv[:, 8:10, :]
        psT = ctx.enter_context(nc.psum_tensor("psTA", [P, 2, 512], F32))
        psq = ctx.enter_context(nc.psum_tensor("psq", [P, NQ, 512], F32))
        psv = ctx.enter_context(nc.psum_tensor("psv", [P, 2, 512], F32))
        ids_in, pos_in, row_in, lam_in, w_in, rest_in = (sem(x) for x in ("ids_in", "pos_in", "row_in", "lam_in", "w_in", "rest_in"))
        gathered = [sem(f"gathered{g}") for g in range(NG)]
        const_set, const_step, ones_set, ones_copied = (
            sem(x) for x in ("const_set", "const_step", "ones_set", "ones_copied"))
        emb_ready, var0_ready, std0_ready = (sem(x) for x in ("emb_ready", "var0_ready", "std0_ready"))
        var1_ready, stds_ready, normed_ready, x1_ready = (sem(x) for x in ("var1_ready", "stds_ready", "normed_ready", "x1_ready"))
        turned, hT_ready, qk_ready, v_ready, v_kept = (sem(x) for x in ("turned", "hT_ready", "qk_ready", "v_ready", "v_kept"))
        hi_ready, rest_ready, mid_ready, lo_ready = (sem(x) for x in ("hi_ready", "rest_ready", "mid_ready", "lo_ready"))
        parts_out = [sem(f"parts_out{i}") for i in range(NB)]
        dve_step = sem("dve_stepA")
        block = ctx.enter_context(nc.Block())

        @block.sync
        def _(sp):
            sp.dma_start(ids[:], io.ids).then_inc(ids_in, 16)
            sp.dma_start(pos[:], io.pos).then_inc(pos_in, 16)
            for dst, src in ((gamma, io.gamma), (beta, io.beta)):
                sp.dma_start(dst[:], src.partition_broadcast(P)).then_inc(row_in, 16)
            sp.dma_start(ln1[:], io.ln1).then_inc(w_in, 16)
            for dst, src in ((wqk, io.wqk), (wv, io.wv)):
                sp.dma_start(dst[:], src.rearrange("(k p) n -> p k n", k=2)).then_inc(w_in, 16)

            def weights(dst, src):
                return lambda: sp.dma_start(dst[:], src.rearrange("(k p) n -> p k n", p=dst.shape[0])).then_inc(rest_in, 16)

            def rows_and_columns():
                for k, row in enumerate((io.lam1, io.lam2)):
                    sp.dma_start(lam[:, k, :], row.partition_broadcast(P)).then_inc(lam_in, 16)
                for dst, src in ((m.projb, io.projb), (m.fc2b, io.fc2b)):
                    sp.dma_start(dst[:], src.partition_broadcast(P)).then_inc(rest_in, 16)
                for dst, src in ((m.rmsw, io.rmsw), (m.ln2, io.ln2), (m.fc1b, io.fc1b)):
                    sp.dma_start(dst[:], src).then_inc(rest_in, 16)

            def stack(pair, half):
                return lambda: load_pair(sp, scratch, qs, ks, stacked, pair, pair, half)

            between = {1: rows_and_columns, 2: weights(m.wproj, io.proj), 3: weights(m.wg, io.wg),
                       4: weights(m.wfc1, io.fc1), 6: weights(m.wfc2, io.fc2)}
            for i in range(4):
                between[STACK + 2 * i] = stack(i // 2, i % 2)

            for n in range(NG * QT):
                g, j = n // QT, n % QT
                sp.wait_ge(lo_ready, n + 1)
                rows = scratch.qk[j // (QT // 2)].rearrange("c r h t -> (r h) c t")
                dst = rows[(j % (QT // 2)) * P:(j % (QT // 2) + 1) * P, :, g * GT:(g + 1) * GT]
                sp.dma_start(dst, parts[:, n % NB]).then_inc(parts_out[n % NB], 16)
                if n == STACK:
                    for i in range(NB):
                        sp.wait_ge(parts_out[i], 16 * len(range(i, n + 1, NB)))
                if n in between:
                    between[n]()
            for i in range(NB):
                sp.wait_ge(parts_out[i], 16 * len(range(i, NG * QT, NB)))
            sp.wait_ge(rest_in, 16 * 9)

        @block.gpsimd
        def _(pool):
            steps = Steps(pool, const_step)
            pool.wait_ge(ids_in, 16)
            for b in range(B):
                pool.indirect_dma_start(
                    out=emb[:, b, :], out_offset=None, in_=io.table,
                    in_offset=bass.IndirectOffsetOnAxis(ap=ids[:, b:b + 1], axis=0),
                ).then_inc(gathered[b // G], 16)
                if b == G - 1:
                    pool.memset(m.eps[:, 0:1], LN_EPS)
                    pool.memset(m.eps[:, 1:2], RMS_EPS)
                    pool.memset(m.eps[:, 2:3], LN_EPS ** 2)
                    pool.memset(m.ident[:], 0.0)
                    steps.mark(pool.memset(m.ones[:], 1.0))
                    steps.settle()
                    steps.mark(pool.affine_select(out=m.ident[:], in_=m.ident[:], compare_op=ALU.not_equal, fill=1.0,
                                                  base=0, pattern=[[-1, P]], channel_multiplier=1))
                    pool.affine_select(out=m.before[:], in_=m.ones[:], compare_op=ALU.is_gt, fill=0.0,
                                       base=0, pattern=[[1, P]], channel_multiplier=-1)
                    steps.settle()
                    pool.tensor_copy(m.identb[:], m.ident[:]).then_inc(const_set, 1)
            pool.wait_ge(pos_in, 16)

            def add_pos(g):
                e = emb[:, g * G:(g + 1) * G, :]
                pool.wait_ge(gathered[g], 16 * G)
                pool.tensor_tensor(e, e, over_tiles(pos[:], G), ALU.add).then_inc(emb_ready, 1)

            def outer_norm(g):
                pool.wait_ge(normed_ready, g + 1)
                for b in range(g * G, (g + 1) * G):
                    pool.tensor_scalar(m.x1[:, b, :], m.h0[:, b, :], mean1[:, b:b + 1], rs[:, 0, b:b + 1],
                                       ALU.subtract, ALU.mult).then_inc(x1_ready, 1)

            def low_part(n):
                pool.wait_ge(mid_ready, n + 1)
                pool.tensor_tensor(parts[:, n % NB, 2, :], rest[:, n % NB, :], parts[:, n % NB, 1, :],
                                   ALU.subtract).then_inc(lo_ready, 1)

            add_pos(1)
            for g in range(NG):
                for j in range(QT):
                    low_part(g * QT + j)
                    if j == 1 and g + 2 < NG:
                        add_pos(g + 2)
                    if j == 3:
                        outer_norm(g)

        @block.scalar
        def _(act):
            act.wait_ge(const_set, 1)

            def root0(g):
                T = slice(g * G, (g + 1) * G)
                act.wait_ge(var0_ready, g + 1)
                nc.scalar.activation(std0[:, T], var0[:, T], ACT.Sqrt, bias=m.eps[:, 0:1]).then_inc(std0_ready, 1)

            def root1(g):
                T = slice(g * G, (g + 1) * G)
                act.wait_ge(var1_ready, g + 1)
                nc.scalar.activation(stds[:, 0, T], var1[:, T], ACT.Sqrt, bias=m.eps[:, 0:1])
                nc.scalar.activation(stds[:, 1, T], var1[:, T], ACT.Sqrt, bias=m.eps[:, 2:3],
                                     scale=1.0 + LN_EPS).then_inc(stds_ready, 1)

            def high(n):
                act.wait_ge(qk_ready, n + 1)
                if n >= NB:
                    act.wait_ge(parts_out[n % NB], 16 * (n // NB))
                nc.scalar.activation(parts[:, n % NB, 0, :], psq[:, n % NQ, :], ACT.Copy).then_inc(hi_ready, 1)

            def middle(n):
                act.wait_ge(rest_ready, n + 1)
                nc.scalar.activation(parts[:, n % NB, 1, :], rest[:, n % NB, :], ACT.Copy).then_inc(mid_ready, 1)

            def features(g):
                act.wait_ge(turned, g + 1)
                if g >= 2:
                    act.wait_ge(v_ready, 2 * (g - 1))
                for k in range(2):
                    last = nc.scalar.activation(hT[:, g % 2, k, :], psT[0:KH, k, :], ACT.Identity,
                                                bias=ln1[:, 1, k:k + 1], scale=ln1[:, 0, k:k + 1])
                last.then_inc(hT_ready, 1)

            def keep_v(g, i):
                act.wait_ge(v_ready, 2 * g + i + 1)
                b = g * G + 2 * i
                nc.scalar.activation(m.v[:, b:b + 2, :], psv[:, i, 0:2 * D].rearrange("p (b d) -> p b d", b=2),
                                     ACT.Copy).then_inc(v_kept, 1)

            act.wait_ge(ones_set, 1)
            nc.scalar.activation(ks[KS:P, 1], ks[KS:P, 0], ACT.Copy).then_inc(ones_copied, 1)
            root0(0)
            root1(0)
            act.wait_ge(w_in, 16 * 3)
            features(0)
            for g in range(NG):
                for j in range(QT + 1):
                    if j < QT:
                        high(g * QT + j)
                    if j:
                        middle(g * QT + j - 1)
                    if j == 2 and g + 1 < NG:
                        root0(g + 1)
                if g + 1 < NG:
                    root1(g + 1)
                keep_v(g, 0)
                if g + 1 < NG:
                    features(g + 1)
                keep_v(g, 1)

        @block.vector
        def _(dve):
            st = Steps(dve, dve_step)

            def stats0(g, T, tiles):
                if g:
                    dve.wait_ge(emb_ready, g)
                for b in tiles:
                    last = dve.bn_stats(stats[:, b, :], emb[:, b, :])
                st.mark(last)
                st.settle()

            def moments0(g, T, tiles):
                moments(dve, st, stats[:, T, :], mean0[:, T], var0[:, T], small).then_inc(var0_ready, 1)

            def scale0(g, T, tiles):
                dve.wait_ge(std0_ready, g + 1)
                st.mark(dve.reciprocal(r0[:, T], std0[:, T]))
                for b in tiles:
                    last = dve.scalar_tensor_tensor(out=m.h0[:, b, :], in0=emb[:, b, :], scalar=mean0[:, b:b + 1],
                                                    in1=gamma[:], op0=ALU.subtract, op1=ALU.mult)
                st.mark(last)
                st.settle()

            def shift0(g, T, tiles):
                for b in tiles:
                    last = dve.scalar_tensor_tensor(out=m.h0[:, b, :], in0=m.h0[:, b, :], scalar=r0[:, b:b + 1],
                                                    in1=beta[:], op0=ALU.mult, op1=ALU.add)
                st.mark(last)
                st.settle()

            def stats1(g, T, tiles):
                for b in tiles:
                    last = dve.bn_stats(stats[:, b, :], m.h0[:, b, :])
                st.mark(last)
                st.settle()
                moments(dve, st, stats[:, T, :], mean1[:, T], var1[:, T], small).then_inc(var1_ready, 1)

            def norm1(g, T, tiles):
                dve.wait_ge(stds_ready, g + 1)
                st.mark(dve.reciprocal(rs[:, :, T], stds[:, :, T]))
                st.settle()
                for b in tiles:
                    last = dve.tensor_scalar(normed[:, b, :], m.h0[:, b, :], mean1[:, b:b + 1], rs[:, 1, b:b + 1],
                                             ALU.subtract, ALU.mult)
                last.then_inc(normed_ready, 1)

            NORMS = (stats0, moments0, scale0, shift0, stats1, norm1)

            def norms(g, k):
                NORMS[k](g, slice(g * G, (g + 1) * G), range(g * G, (g + 1) * G))

            dve.memset(ks[KS:P, 0, :, :], 1.0).then_inc(ones_set, 1)
            dve.wait_ge(pos_in, 16)
            dve.wait_ge(gathered[0], 16 * G)
            st.mark(dve.tensor_tensor(emb[:, 0:G, :], emb[:, 0:G, :], over_tiles(pos[:], G), ALU.add))
            st.settle()
            dve.wait_ge(row_in, 16 * 2)
            for k in range(len(NORMS)):
                norms(0, k)
            for g in range(NG):
                for j in range(QT):
                    n = g * QT + j
                    dve.wait_ge(hi_ready, n + 1)
                    if n >= NB:
                        dve.wait_ge(lo_ready, n - NB + 1)
                    dve.tensor_tensor(rest[:, n % NB, :], psq[:, n % NQ, :], parts[:, n % NB, 0, :],
                                      ALU.subtract).then_inc(rest_ready, 1)
                    if g + 1 < NG:
                        norms(g + 1, j)
            dve.wait_ge(lam_in, 16 * 2)
            st.mark(dve.tensor_tensor(m.nlam[:], lam[:, 1, :], lam[:, 0, :], ALU.subtract))
            st.settle()
            dve.tensor_scalar(m.nlam[:], m.nlam[:], -LAMBDA_INIT, None, ALU.add)

        @block.tensor
        def _(pe):
            pe.wait_ge(const_set, 1)
            pe.wait_ge(w_in, 16 * 3)

            def turn(g):
                pe.wait_ge(normed_ready, g + 1)
                if g:
                    pe.wait_ge(hT_ready, g)
                for k in range(2):
                    for t in range(G):
                        last = pe.transpose(psT[0:KH, k, t * P:(t + 1) * P],
                                            normed[:, g * G + t, k * KH:(k + 1) * KH], m.ident[:])
                last.then_inc(turned, 1)

            turn(0)
            for g in range(NG):
                pe.wait_ge(hT_ready, g + 1)
                for j in range(QT):
                    n = g * QT + j
                    if n >= NQ:
                        pe.wait_ge(rest_ready, n - NQ + 1)
                    for k in range(2):
                        last = pe.matmul(psq[:, n % NQ, :], wqk[:, k, j * P:(j + 1) * P], hT[:, g % 2, k, :],
                                         start=(k == 0), stop=(k == 1))
                    last.then_inc(qk_ready, 1)
                for i in range(2):
                    if g:
                        pe.wait_ge(v_kept, 2 * (g - 1) + i + 1)
                    for t in range(2 * i, 2 * i + 2):
                        for k in range(2):
                            last = pe.matmul(psv[:, i, (t % 2) * D:(t % 2 + 1) * D], hT[:, g % 2, k, t * P:(t + 1) * P],
                                             wv[:, k, :], start=(k == 0), stop=(k == 1))
                    last.then_inc(v_ready, 1)
                    if i == 0 and g + 1 < NG:
                        turn(g + 1)


def runs(slots):
    cut = [j for j in range(len(slots)) if j == 0 or slots[j] != slots[j - 1] + 1] + [len(slots)]
    return [(a, slots[a], b - a) for a, b in zip(cut[:-1], cut[1:])]


PAIR_LOADS = len(runs(Q_SLOTS)) + len(runs(K_SLOTS))


def load_pair(engine, scratch, qs, ks, stacked, pair, par, half):
    H = slice(half * NHS // 2, (half + 1) * NHS // 2)
    for side, (dst, slots) in enumerate(((qs, Q_SLOTS), (ks, K_SLOTS))):
        for slot, part, n in runs(slots):
            src = scratch.qk[side, part:part + n].rearrange("c r h t -> (c r) h t")
            engine.dma_start(dst[slot * HD:(slot + n) * HD, par, H, :],
                             src[:, H, ds(pair * 2 * P, 2 * P)]).then_inc(stacked[par][half], 16)


def attention_phase(nc, m, scratch, qs, ks, stacked):
    R = NH // 2
    HH = NHS // 2
    with ExitStack() as ctx:
        sb = lambda n, s, d=F32: ctx.enter_context(nc.sbuf_tensor(n, s, d))
        ps = lambda n, s, d=F32: ctx.enter_context(nc.psum_tensor(n, s, d))
        sem = lambda n: ctx.enter_context(nc.semaphore(n))
        ex = sb("ex", [P, 6, 512])
        vcur = sb("vcur", [P, 2, NH, 32])
        nmax = sb("nmax", [P, 2, HH])
        nrest = sb("nrest", [P, 2, HH])
        mparts = sb("mparts", [P, 2, 2 * PARTS, HH], BF16)
        mT = sb("mT", [PARTS * HH, 2, P], BF16)
        oT = sb("oTB", [P, 3, 2 * P])
        rs = sb("rs", [P, 6, 4])
        o1 = sb("o1", [P, 3, 4, HD])
        o2 = sb("o2", [P, 3, 4, HD])
        psS = ps("psS", [P, 2, 4, P])
        psE = ps("psE", [P, 2, 4, P])
        psO = ps("psO", [P, 4, 256])
        psR = ps("psR", [P, 8, P])
        psM = [psO[0:2 * PARTS * HH, 3, i * P // 2:(i + 1) * P // 2].bitcast(BF16) for i in range(2)]
        max_in = [[sem(f"max_in{i}_{j}") for j in range(2)] for i in range(4)]
        sums_set, zeros_set, v_cur = sem("sums_set"), sem("zeros_setB"), sem("v_cur")
        s_ready, s_max, m_split, m_turned, mT_ready = (sem(x) for x in ("s_ready", "s_max", "m_split", "m_turned", "mT_ready"))
        st_ready, exp_ready, pv_ready, oT_ready, o_turned, o_normed = (
            sem(x) for x in ("st_ready", "exp_ready", "pv_ready", "oT_ready", "o_turned", "o_normed"))
        dve_step = sem("dve_stepB")
        block = ctx.enter_context(nc.Block())
        DM, DN = 2 * 3, 3
        TURNS = B // 4

        def rows(engine, step):
            for c in range(4):
                step(c, 0, c)
            with engine.Fori(1, TURNS - 1) as i:
                for c in range(4):
                    step(4 * i + c, i, c)
            for c in range(4):
                step(B - 4 + c, TURNS - 1, c)

        def exists(b):
            return not isinstance(b, int) or 0 <= b < B

        def passed(engine, signal, value):
            if not isinstance(value, int) or value > 0:
                engine.wait_ge(signal, value)

        @block.sync
        def _(sp):
            def maxima(b, i, c, half):
                sp.wait_ge(mT_ready, 2 * b + half + 1)
                for t in range(PARTS):
                    sp.dma_start(qs[KS + t:KS + t + 1, c // 2, half * HH:(half + 1) * HH, (c % 2) * P:(c % 2 + 1) * P],
                                 mT[t * HH:(t + 1) * HH, half, :]).then_inc(max_in[c][half], 16)

            for half in range(2):
                maxima(0, 0, 0, half)

            def step(b, i, c):
                for half in range(2):
                    if exists(b + 1):
                        maxima(b + 1, i, (c + 1) % 4, half)
                    if c % 2 == 1 and (not isinstance(i, int) or i < TURNS - 1):
                        sp.wait_ge(st_ready, R * b + (half + 1) * R // 2)
                        load_pair(sp, scratch, qs, ks, stacked, 2 * i + c // 2 + 2, c // 2, half)

            rows(sp, step)

        @block.gpsimd
        def _(pool):
            pool.memset(vcur[:], 1.0).then_inc(sums_set, 1)
            pool.wait_ge(sums_set, 1)
            pool.memset(mparts[:, :, PARTS:, :], 0.0).then_inc(zeros_set, 1)
            pool.wait_ge(zeros_set, 1)

            def copy(b, c):
                pool.tensor_copy(vcur[:, c % 2, :, 0:HD],
                                 m.v[:, ds(b, 1), :].rearrange("p o (h d) -> p (o h) d", h=NH)).then_inc(v_cur, 1)

            copy(0, 0)

            def step(b, i, c):
                if exists(b + 1):
                    passed(pool, pv_ready, 2 * b)
                    copy(b + 1, c + 1)

            rows(pool, step)

        @block.tensor
        def _(pe):
            def scores(b, c, r):
                par, T = c // 2, slice((c % 2) * P, (c % 2 + 1) * P)
                passed(pe, s_max, b * R + r - 1)
                for x in range(4):
                    h = 4 * r + x
                    last = pe.matmul(psS[:, r % 2, x, :], qs[0:KS, par, h, T], ks[0:KS, par, h, T],
                                     start=True, stop=True)
                last.then_inc(s_ready, 1)

            def turn_maxima(b, half):
                pe.wait_ge(m_split, 2 * b + half + 1)
                passed(pe, mT_ready, 2 * b + half)
                if half == 0:
                    passed(pe, oT_ready, 2 * (b - 1))
                pe.transpose(psM[half], mparts[:, half, :, :].rearrange("p a h -> p (a h)"), m.identb[:]).then_inc(m_turned, 1)

            def values(b, c, r):
                pe.wait_ge(exp_ready, R * b + r + 1)
                if r == 0:
                    pe.wait_ge(v_cur, b + 1)
                    passed(pe, oT_ready, 2 * b - 1)
                if r == 4:
                    passed(pe, oT_ready, 2 * b)
                    if exists(b + 1):
                        pe.wait_ge(mT_ready, 2 * b + 4)
                for x in range(2):
                    h = 2 * r + x
                    q = 32 * (h % 4)
                    last = pe.matmul(psO[q:q + 32, h // 4, :], vcur[:, c % 2, h, :],
                                     ex[:, r, x * 256:(x + 1) * 256], start=True, stop=True)
                if r in (R - 3, R - 1):
                    last.then_inc(pv_ready, 1)

            def turn_back(b):
                pe.wait_ge(oT_ready, 2 * b + 2)
                passed(pe, o_normed, b)
                for x in range(6):
                    last = pe.transpose(psR[:, x, :], oT[:, x // 2, (x % 2) * P:(x % 2 + 1) * P], m.ident[:])
                last.then_inc(o_turned, 1)

            def step(b, i, c):
                par, T = c // 2, slice((c % 2) * P, (c % 2 + 1) * P)
                for r in range(R):
                    passed(pe, exp_ready, R * b + r - 1)
                    if r % (R // 2) == 0:
                        pe.wait_ge(max_in[c][r // (R // 2)], 16 * PARTS * (i + 1))
                    for x in range(4):
                        h = 4 * r + x
                        last = pe.matmul(psE[:, r % 2, x, :], ks[0:KM, par, h, T], qs[0:KM, par, h, T],
                                         start=True, stop=True)
                    last.then_inc(st_ready, 1)
                    if r == 1 and c % 2 == 1 and exists(b + 1):
                        pe.wait_ge(stacked[1 - par][1], 16 * PAIR_LOADS * (i + 1 + par))
                    if r < R - 2 and exists(b + 1):
                        scores(b + 1, (c + 1) % 4, r + 2)
                    if r >= R - 2 and exists(b + 2):
                        if r == R - 2 and c % 2 == 0:
                            pe.wait_ge(stacked[1 - par][0], 16 * PAIR_LOADS * (i + 1 + par))
                        scores(b + 2, (c + 2) % 4, r - (R - 2))
                    if r == 2 and exists(b + 1):
                        turn_maxima(b + 1, 0)
                    if r == 5 and exists(b + 1):
                        turn_maxima(b + 1, 1)
                    if r == 3 and exists(b - 1):
                        turn_back(b - 1)
                    if r >= 2:
                        values(b, c, r - 2)
                    elif exists(b - 1):
                        values(b - 1, c - 1, r + 4)

            for half in range(2):
                pe.wait_ge(stacked[0][half], 16 * PAIR_LOADS)
            pe.wait_ge(zeros_set, 1)
            for r in range(R):
                scores(0, 0, r)
            turn_maxima(0, 0)
            turn_maxima(0, 1)
            for r in range(2):
                scores(1, 1, r)
            rows(pe, step)
            for r in (4, 5):
                values(B - 1, 3, r)
            turn_back(B - 1)

        @block.scalar
        def _(act):
            def turn_maxima(b, i, c, half):
                act.wait_ge(m_turned, 2 * b + 2 + half + 1)
                act.wait_ge(max_in[c][half], 16 * PARTS * (i + 1))
                nc.scalar.activation(mT[:, half, :], psM[half][0:PARTS * HH, :], ACT.Copy).then_inc(mT_ready, 1)

            def keep(b, bank):
                act.wait_ge(pv_ready, 2 * b + 1 + bank)
                H = slice(0, 2) if bank == 0 else slice(2, 3)
                if bank == 0:
                    passed(act, o_turned, b)
                nc.scalar.activation(oT[:, H, :], psO[:, H, :], ACT.Copy).then_inc(oT_ready, 1)

            def step(b, i, c):
                for r in range(R):
                    act.wait_ge(st_ready, R * b + r + 1)
                    if r % 4 == 0:
                        passed(act, pv_ready, 2 * b - 1 + r // 4)
                    nc.scalar.activation(ex[:, r, :].rearrange("p (x q) -> p x q", x=4), psE[:, r % 2], ACT.Exp,
                                         scale=HD ** -0.5).then_inc(exp_ready, 1)
                    if r == 1 and exists(b - 1):
                        keep(b - 1, 1)
                    if r in (2, 5) and exists(b + 1):
                        turn_maxima(b, i, c, r // 3)
                keep(b, 0)

            for half in range(2):
                act.wait_ge(m_turned, half + 1)
                nc.scalar.activation(mT[:, half, :], psM[half][0:PARTS * HH, :], ACT.Copy).then_inc(mT_ready, 1)
            rows(act, step)
            keep(B - 1, 1)

        @block.vector
        def _(dve):
            def maximum(b, r, st):
                half, k = divmod(r, R // 2)
                dve.wait_ge(s_ready, R * b + r + 1)
                if k == 0:
                    passed(dve, m_split, 2 * b - 1 + half)
                dve.tensor_reduce(nmax[:, half, 4 * k:4 * k + 4], psS[:, r % 2], AX.X, ALU.max,
                                  negate=True).then_inc(s_max, 1)
                if k < R // 2 - 1:
                    return
                n, w = nmax[:, half, :], nrest[:, half, :]
                dve.wait_ge(s_max, R * b + r + 1)
                passed(dve, m_turned, 2 * b - 1 + half)
                st.mark(dve.tensor_copy(mparts[:, half, 0, :], n))
                st.settle()
                st.mark(dve.tensor_tensor(w, n, mparts[:, half, 0, :], ALU.subtract))
                st.settle()
                st.mark(dve.tensor_copy(mparts[:, half, 1, :], w))
                st.settle()
                dve.tensor_tensor(mparts[:, half, 2, :], w, mparts[:, half, 1, :], ALU.subtract).then_inc(m_split, 1)

            def norm(b, st):
                dve.wait_ge(o_turned, b + 1)
                o = psR[:, 0:6, :].rearrange("p (g s) (h w) -> p g s h w", s=2, h=4)
                r4 = rs[:].rearrange("p (g s) h -> p g s h", s=2)
                st.mark(dve.reciprocal(rs[:], psR[:, 0:6, :].rearrange("p x (h w) -> p x h w", h=4)[:, :, :, HD]))
                st.settle()
                st.mark(dve.tensor_tensor(r4[:, :, 1, :], r4[:, :, 1, :], m.nlam[:].rearrange("p (g h) -> p g h", g=3), ALU.mult))
                st.settle()
                wide = lambda s: r4[:, :, s, :].unsqueeze(3).broadcast_to([P, 3, 4, HD])
                dve.tensor_tensor(o1[:], o[:, :, 0, :, 0:HD], wide(0), ALU.mult)
                st.mark(dve.tensor_tensor(o2[:], o[:, :, 1, :, 0:HD], wide(1), ALU.mult))
                st.settle()
                dve.tensor_tensor(m.o[:, ds(b, 1), :].rearrange("p o d -> p (o d)"),
                                  o1[:].rearrange("p g h d -> p (g h d)"),
                                  o2[:].rearrange("p g h d -> p (g h d)"), ALU.add).then_inc(o_normed, 1)

            def step(b, i, c):
                st = Steps(dve, dve_step, DM if isinstance(b, int) and b == 0 else (DM + DN) * b + DM - DN)
                if exists(b + 1):
                    for r in range(2, R):
                        maximum(b + 1, r, st)
                if exists(b - 1):
                    norm(b - 1, st)
                if exists(b + 2):
                    for r in range(2):
                        maximum(b + 2, r, st)

            st = Steps(dve, dve_step)
            for r in range(R):
                maximum(0, r, st)
            for r in range(2):
                maximum(1, r, st)
            rows(dve, step)
            norm(B - 1, Steps(dve, dve_step, DM * B + DN * (B - 1)))


def mlp_phase(nc, m, scratch):
    with ExitStack() as ctx:
        sb = lambda n, s, d=F32: ctx.enter_context(nc.sbuf_tensor(n, s, d))
        ps = lambda n, s, d=F32: ctx.enter_context(nc.psum_tensor(n, s, d))
        sem = lambda n: ctx.enter_context(nc.semaphore(n))
        zeros = sb("zeros", [P, D * 8])
        zeros_set, zeros_out, x_out = sem("zeros_set"), sem("zeros_out"), sem("x_out")
        staged = sb("staged", [P, 2, G, D])
        fT = sb("fT", [KH, 2, 2, GT])
        gT = sb("gT", [P, 2, MT, GT])
        stats = sb("statsC", [P, B, 6])
        small = sb("smallC", [P, 3, G])
        mv = sb("mvC", [P, 3, 4, B])
        psT = ps("psTC", [P, 2, 512])
        psG = ps("psG", [P, 3, 512])
        psY = ps("psY", [P, 2, 512])
        psL = ps("psL", [P, 512])
        var_ready, std_ready, staged_ready, turned, fT_ready, y_ready, y_kept = (
            sem(x) for x in ("var_ready", "std_ready", "staged_ready", "turnedC", "fT_ready", "y_ready", "y_kept"))
        g_ready, gelu_ready, dve_step, l_ready = (sem(x) for x in ("g_ready", "gelu_ready", "dve_stepC", "l_ready"))
        biased, bias2_ready, summed = (sem(x) for x in ("biased", "bias2_ready", "summed"))
        block = ctx.enter_context(nc.Block())
        ITEMS = [(0, 0), (0, 1), (0, 2), (1, 0), (0, 3), (1, 1), (2, 0), (1, 2), (2, 1), (1, 3), (2, 2), (2, 3)]
        WITH_Y = [x for x in ITEMS if x[0] < 2]

        def y_count(s, g):
            return 2 * (WITH_Y.index((s, g)) + 1)

        def tiles(g):
            return slice(g * G, (g + 1) * G)

        def staged_in(k):
            s, g = ITEMS[k]
            return k - 2 if s == 0 or ITEMS.index((s - 1, g)) < k - 2 else k - 1

        @block.sync
        def _(sp):
            sp.wait_ge(zeros_set, 1)
            sp.dma_start(scratch.x[N:N + P, :], zeros[:, 0:D + PAD]).then_inc(zeros_out, 16)
            flat = scratch.y[0:TOPK * N, :].rearrange("(c p r) d -> c p (r d)", p=P, r=8)
            for c in range(TOPK * N // (8 * P)):
                sp.dma_start(flat[c], zeros[:]).then_inc(zeros_out, 16)
            for g in range(NG):
                sp.wait_ge(staged_ready, ITEMS.index((2, g)) + 1)
                for dst, src in ((slice(0, D), slice(0, D)), (slice(D, D + PAD), slice(D - PAD, D))):
                    sp.dma_start(scratch.x[g * GT:(g + 1) * GT, dst].rearrange("(b p) d -> p b d", p=P),
                                 m.xg[:, tiles(g), src]).then_inc(x_out, 16)
            sp.wait_ge(zeros_out, 16 * (TOPK * N // (8 * P) + 1))
            sp.wait_ge(x_out, 2 * 16 * NG)

        @block.vector
        def _(dve):
            st = Steps(dve, dve_step)

            def stage(k):
                s, g = ITEMS[k]
                T = tiles(g)
                mean, var, std, rr = (mv[:, s, i, T] for i in range(4))
                src = (m.o, m.x1, m.h0)[s]
                if s:
                    dve.wait_ge(y_kept, y_count(s - 1, g))
                for b in range(g * G, (g + 1) * G):
                    last = dve.bn_stats(stats[:, b, :], src[:, b, :])
                st.mark(last)
                st.settle()
                last = moments(dve, st, stats[:, T], mean, var, small)
                if s == 0:
                    st.mark(last)
                    st.mark(dve.tensor_tensor(std, mean, mean, ALU.mult))
                    st.settle()
                    last = dve.tensor_tensor(var, var, std, ALU.add)
                last.then_inc(var_ready, 1)
                dve.wait_ge(std_ready, k + 1)
                st.mark(dve.reciprocal(rr, std))
                st.settle()
                if k >= 2:
                    dve.wait_ge(turned, k - 1)
                for t in range(G):
                    b = g * G + t
                    mb, rb = mv[:, s, 0, b:b + 1], mv[:, s, 3, b:b + 1]
                    if s == 0:
                        last = dve.tensor_scalar(staged[:, k % 2, t, :], src[:, b, :], rb, None, ALU.mult)
                    else:
                        dst = staged[:, k % 2, t, :] if s == 1 else m.xg[:, b, :]
                        last = dve.tensor_scalar(dst, src[:, b, :], mb, rb, ALU.subtract, ALU.mult)
                last.then_inc(staged_ready, 1)

            def keep(s, g):
                dst = m.h0 if s else m.x1
                if s:
                    dve.wait_ge(summed, g + 1)
                else:
                    dve.wait_ge(biased, g + 1)
                for i in range(2):
                    dve.wait_ge(y_ready, y_count(s, g) - 1 + i)
                    b = g * G + 2 * i
                    x = dst[:, b:b + 2, :]
                    dve.tensor_tensor(x, psY[:, i, 0:2 * D].rearrange("p (b d) -> p b d", b=2), x,
                                      ALU.add).then_inc(y_kept, 1)

            stage(0)
            stage(1)
            for k, (s, g) in enumerate(ITEMS):
                for ahead in (1, 2):
                    if k + ahead < len(ITEMS) and staged_in(k + ahead) == k:
                        stage(k + ahead)
                if s < 2:
                    keep(s, g)
            dve.wait_ge(l_ready, NG)
            dve.tensor_copy(m.logits[:], psL[:, 0:B * E].rearrange("p (b e) -> p b e", e=E))

        @block.gpsimd
        def _(pool):
            for g in range(NG):
                x = m.x1[:, tiles(g), :]
                pool.tensor_tensor(x, x, over_tiles(m.projb[:], G), ALU.add).then_inc(biased, 1)
            pool.memset(zeros[:], 0.0).then_inc(zeros_set, 1)
            for g in range(NG):
                h = m.h0[:, tiles(g), :]
                pool.tensor_tensor(h, h, over_tiles(m.fc2b[:], G), ALU.add).then_inc(bias2_ready, 1)
            for g in range(NG):
                h = m.h0[:, tiles(g), :]
                pool.wait_ge(bias2_ready, g + 1)
                pool.wait_ge(y_kept, y_count(0, g))
                pool.tensor_tensor(h, h, m.x1[:, tiles(g), :], ALU.add).then_inc(summed, 1)

        @block.scalar
        def _(act):
            def root(k):
                s, g = ITEMS[k]
                act.wait_ge(var_ready, k + 1)
                nc.scalar.activation(mv[:, s, 2, tiles(g)], mv[:, s, 1, tiles(g)], ACT.Sqrt,
                                     bias=m.eps[:, 1:2] if s == 0 else m.eps[:, 0:1]).then_inc(std_ready, 1)

            def features(k):
                s, g = ITEMS[k]
                act.wait_ge(turned, k + 1)
                if k >= 2:
                    s2, g2 = ITEMS[k - 2]
                    if s2 == 0:
                        act.wait_ge(y_ready, y_count(s2, g2))
                    elif s2 == 1:
                        act.wait_ge(g_ready, MT * (g2 + 1))
                    else:
                        act.wait_ge(l_ready, g2 + 1)
                for h in range(2):
                    src, dst = psT[0:KH, h, :], fT[:, k % 2, h, :]
                    if s == 0:
                        last = nc.scalar.activation(dst, src, ACT.Identity, scale=m.rmsw[:, h:h + 1])
                    elif s == 1:
                        last = nc.scalar.activation(dst, src, ACT.Identity, bias=m.ln2[:, 1, h:h + 1], scale=m.ln2[:, 0, h:h + 1])
                    else:
                        last = nc.scalar.activation(dst, src, ACT.Identity)
                last.then_inc(fT_ready, 1)

            root(0)
            root(1)
            for k, (s, g) in enumerate(ITEMS):
                features(k)
                if s == 1:
                    for j in range(MT):
                        n = g * MT + j
                        act.wait_ge(g_ready, n + 1)
                        if j == 0 and g >= 2:
                            act.wait_ge(y_ready, y_count(1, g - 2))
                        nc.scalar.activation(gT[:, g % 2, j, :], psG[:, n % 3, :], ACT.Gelu,
                                             bias=m.fc1b[:, j:j + 1]).then_inc(gelu_ready, 1)
                for ahead in (1, 2):
                    if k + ahead < len(ITEMS) and staged_in(k + ahead) == k:
                        root(k + ahead)

        @block.tensor
        def _(pe):
            def turn(k):
                s, g = ITEMS[k]
                pe.wait_ge(staged_ready, k + 1)
                if k:
                    pe.wait_ge(fT_ready, k)
                for h in range(2):
                    for t in range(G):
                        src = staged[:, k % 2, t, :] if s < 2 else m.xg[:, g * G + t, :]
                        last = pe.transpose(psT[0:KH, h, t * P:(t + 1) * P], src[:, h * KH:(h + 1) * KH], m.ident[:])
                last.then_inc(turned, 1)

            def products(k, i):
                s, g = ITEMS[k]
                if WITH_Y.index((s, g)):
                    pe.wait_ge(y_kept, y_count(s, g) - 3 + i)
                for t in range(2 * i, 2 * i + 2):
                    out = psY[:, i, (t % 2) * D:(t % 2 + 1) * D]
                    T = slice(t * P, (t + 1) * P)
                    if s == 0:
                        for h in range(2):
                            last = pe.matmul(out, fT[:, k % 2, h, T], m.wproj[:, h, :], start=(h == 0), stop=(h == 1))
                    else:
                        for j in range(MT):
                            last = pe.matmul(out, gT[:, g % 2, j, T], m.wfc2[:, j, :], start=(j == 0), stop=(j == MT - 1))
                last.then_inc(y_ready, 1)

            turn(0)
            for k, (s, g) in enumerate(ITEMS):
                more = k + 1 < len(ITEMS)
                pe.wait_ge(fT_ready, k + 1)
                if s == 0:
                    products(k, 0)
                    products(k, 1)
                    turn(k + 1)
                elif s == 1:
                    for j in range(MT):
                        q = g * MT + j
                        if q >= 3:
                            pe.wait_ge(gelu_ready, q - 2)
                        for h in range(2):
                            last = pe.matmul(psG[:, q % 3, :], m.wfc1[:, h, j * P:(j + 1) * P], fT[:, k % 2, h, :],
                                             start=(h == 0), stop=(h == 1))
                        last.then_inc(g_ready, 1)
                    pe.wait_ge(gelu_ready, MT * (g + 1))
                    products(k, 0)
                    turn(k + 1)
                    products(k, 1)
                else:
                    for t in range(G):
                        b = g * G + t
                        for h in range(2):
                            last = pe.matmul(psL[:, b * E:(b + 1) * E], fT[:, k % 2, h, t * P:(t + 1) * P], m.wg[:, h, :],
                                             start=(h == 0), stop=(h == 1))
                    last.then_inc(l_ready, 1)
                    if more:
                        turn(k + 1)


def route_phase(nc, m):
    with ExitStack() as ctx:
        sb = lambda n, s, d=F32: ctx.enter_context(nc.sbuf_tensor(n, s, d))
        sem = lambda n: ctx.enter_context(nc.semaphore(n))
        best = sb("best", [P, B, 8])
        besti = sb("besti", [P, B, 8], U32)
        chosen = sb("chosen", [P, TOPK, B])
        hot = sb("hot", [P, TOPK, B, E])
        hotb = sb("hotb", [P, TOPK, B, E], BF16)
        lane = sb("lane", [P, TOPK, B, E])
        picked = sb("picked", [P, TOPK, B, E])
        place = sb("place", [P, TOPK, B])
        keep = sb("keep", [P, TOPK, B])
        local = sb("local", [P, TOPK, B])
        bound = sb("bound", [P, TOPK * B, ST + 1])
        over = sb("over", [P, TOPK * B, ST + 1])
        inner = sb("inner", [P, TOPK * B, ST])
        within = sb("within", [P, TOPK * B])
        slot = sb("slot", [P, TOPK * B, P], BF16)
        point = sb("point", [P, P])
        token = sb("token", [P, 1])
        row = sb("row", [P, TOPK * B])
        marked = sb("marked", [P, 2, TOPK * B, ST])
        values = sb("values", [P, TOPK * B, 2, E, ST], BF16)
        second = sb("second", [P, SLOTS])
        spare = sb("spare", [P, SLOTS])
        full = sb("full", [P, SLOTS])
        target = sb("target", [P, SLOTS])
        source = sb("source", [P, SLOTS])
        e1 = sb("e1", [P, B])
        den = sb("den", [P, B])
        psC = ctx.enter_context(nc.psum_tensor("psC", [P, TOPK, B, E], F32))
        psI = ctx.enter_context(nc.psum_tensor("psI", [P, 2, SLOTS], F32))
        const_set, hot_ready, counted, gap_ready, exp_ready, slot_ready, values_ready, found = (
            sem(x) for x in ("const_setD", "hot_ready", "counted", "gap_ready", "exp_readyD", "slot_ready", "values_ready", "found"))
        dve_step = sem("dve_stepD")
        block = ctx.enter_context(nc.Block())
        CONSTS = 7

        @block.gpsimd
        def _(pool):
            def iota(out, pattern, base=0, down=0):
                pool.iota(out, pattern=pattern, base=base, channel_multiplier=down,
                          allow_small_or_imprecise_dtypes=True).then_inc(const_set, 1)

            iota(lane[:], [[0, TOPK * B], [1, E]])
            iota(bound[:], [[0, TOPK * B], [P, ST + 1]])
            iota(row[:], [[1, TOPK * B]])
            iota(token[:], [[0, 1]], base=1, down=1)
            iota(point[:], [[1, P]])
            iota(second[:], [[0, E], [P, ST]], down=1)
            iota(spare[:], [[P, SLOTS]], base=TOPK * N, down=1)

        @block.scalar
        def _(act):
            act.wait_ge(gap_ready, 1)
            nc.scalar.activation(e1[:], den[:], ACT.Exp).then_inc(exp_ready, 1)

        @block.tensor
        def _(pe):
            pe.wait_ge(hot_ready, 1)
            pe.matmul(psC[:], m.before[:], hotb[:], start=True, stop=False, skip_group_check=True)
            for d in range(1, B):
                last = pe.matmul(psC[:, :, d:B, :], m.ones[:], hotb[:, :, 0:B - d, :], start=False,
                                 stop=(d == B - 1), skip_group_check=True)
            last.then_inc(counted, 1)
            pe.wait_ge(values_ready, 1)
            for k in range(TOPK):
                pe.wait_ge(slot_ready, k + 1)
                for n in range(k * B, (k + 1) * B):
                    last = pe.matmul(psI[:], slot[:, n, :], values[:, n], start=(n == 0), stop=(n == TOPK * B - 1))
            last.then_inc(found, 1)

        @block.vector
        def _(dve):
            st = Steps(dve, dve_step)
            for b in range(B):
                last = dve.max(best[:, b, :], m.logits[:, b, :])
            st.mark(last)
            st.settle()
            for b in range(B):
                last = dve.max_index(besti[:, b, :], best[:, b, :], m.logits[:, b, :])
            st.mark(last)
            st.settle()
            for k in range(TOPK):
                last = dve.tensor_copy(chosen[:, k, :], besti[:, :, k])
            st.mark(last)
            dve.tensor_tensor(den[:], best[:, :, 1], best[:, :, 0], ALU.subtract).then_inc(gap_ready, 1)
            st.settle()
            dve.wait_ge(const_set, CONSTS)
            for k in range(TOPK):
                last = dve.tensor_tensor(hot[:, k], lane[:, k], chosen[:, k, :].unsqueeze(2).broadcast_to([P, B, E]),
                                         ALU.is_equal)
            st.mark(last)
            st.settle()
            dve.tensor_copy(hotb[:], hot[:]).then_inc(hot_ready, 1)
            dve.wait_ge(exp_ready, 1)
            st.mark(dve.tensor_scalar(den[:], e1[:], 1.0, None, ALU.add))
            st.mark(dve.tensor_scalar(second[:], second[:], float(CAP), float(N), ALU.is_ge, ALU.mult))
            st.settle()
            st.mark(dve.reciprocal(m.gate[:, 0, :], den[:]))
            st.settle()
            st.mark(dve.tensor_tensor(m.gate[:, 1, :], m.gate[:, 0, :], e1[:], ALU.mult))
            dve.wait_ge(counted, 1)
            st.mark(dve.tensor_tensor(picked[:], hot[:], psC[:], ALU.mult))
            st.settle()
            st.mark(dve.tensor_reduce(place[:], picked[:], AX.X, ALU.add))
            st.settle()
            dve.tensor_scalar(keep[:], place[:], float(CAP), None, ALU.is_lt)
            dve.tensor_copy(local[:, 0, :], place[:, 0, :])
            st.mark(dve.tensor_scalar(local[:, 1, :], place[:, 1, :], float(CAP), None, ALU.add))
            st.settle()
            flat = local[:].rearrange("p k b -> p (k b)")
            kept = keep[:].rearrange("p k b -> p (k b)")
            wide = lambda x: x.unsqueeze(2).broadcast_to([P, TOPK * B, ST])
            dve.tensor_tensor(m.gate[:], m.gate[:], keep[:], ALU.mult)
            st.mark(dve.tensor_tensor(over[:], flat.unsqueeze(2).broadcast_to([P, TOPK * B, ST + 1]), bound[:], ALU.is_ge))
            st.settle()
            dve.tensor_tensor(inner[:], over[:, :, 0:ST], over[:, :, 1:ST + 1], ALU.subtract)
            st.mark(dve.tensor_reduce(within[:], over[:, :, 1:ST + 1], AX.X, ALU.add))
            st.settle()
            st.mark(dve.scalar_tensor_tensor(out=within[:], in0=within[:], scalar=-float(P), in1=flat,
                                             op0=ALU.mult, op1=ALU.add))
            st.mark(dve.tensor_tensor(inner[:], inner[:], wide(kept), ALU.mult))
            st.settle()
            dve.tensor_scalar(marked[:, 0], inner[:], token[:], None, ALU.mult)
            st.mark(dve.tensor_tensor(marked[:, 1], inner[:], wide(row[:]), ALU.mult))
            st.settle()
            experts = hot[:].rearrange("p k b e -> p (k b) e").unsqueeze(3).broadcast_to([P, TOPK * B, E, ST])
            for x in range(2):
                last = dve.tensor_tensor(values[:, :, x], experts, marked[:, x].unsqueeze(2).broadcast_to([P, TOPK * B, E, ST]),
                                         ALU.mult)
            last.then_inc(values_ready, 1)
            for k in range(TOPK):
                T = slice(k * B, (k + 1) * B)
                dve.tensor_tensor(slot[:, T, :], within[:, T].unsqueeze(2).broadcast_to([P, B, P]),
                                  point[:].unsqueeze(1).broadcast_to([P, B, P]), ALU.is_equal).then_inc(slot_ready, 1)
            dve.wait_ge(found, 1)
            dve.tensor_scalar(full[:], psI[:, 0, :], 0.5, None, ALU.is_ge)
            st.mark(dve.tensor_scalar(target[:], psI[:, 0, :], -1.0, None, ALU.add))
            st.settle()
            st.mark(dve.scalar_tensor_tensor(out=target[:], in0=psI[:, 1, :], scalar=float(P), in1=target[:],
                                             op0=ALU.mult, op1=ALU.add))
            st.settle()
            st.mark(dve.tensor_tensor(source[:], target[:], second[:], ALU.subtract))
            st.mark(dve.tensor_tensor(target[:], target[:], spare[:], ALU.subtract))
            st.settle()
            st.mark(dve.scalar_tensor_tensor(out=source[:], in0=source[:], scalar=-float(N), in1=full[:],
                                             op0=ALU.add, op1=ALU.mult))
            st.mark(dve.tensor_tensor(target[:], target[:], full[:], ALU.mult))
            st.settle()
            dve.tensor_scalar(m.fetch[:], source[:], float(N), None, ALU.add)
            dve.tensor_tensor(m.send[:], target[:], spare[:], ALU.add)


def expert_phase(nc, io, m, scratch):
    with ExitStack() as ctx:
        sb = lambda n, s, d=F32: ctx.enter_context(nc.sbuf_tensor(n, s, d))
        ps = lambda n, s, d=F32: ctx.enter_context(nc.psum_tensor(n, s, d))
        sem = lambda n: ctx.enter_context(nc.semaphore(n))
        w1 = sb("w1", [P, 2, 2 * HF])
        w1h = sb("w1h", [P, 2, 2, 2 * HF], F32R)
        w1l = sb("w1l", [P, 2, 2, 2 * HF], F32R)
        w2 = sb("w2", [P, 2, HF // P, D])
        rows = sb("rows", [P, 2, ST, D + PAD])
        xh = sb("xh", [P, 2, 2, EROWS], F32R)
        xl = sb("xl", [P, 2, EROWS], F32R)
        silu = sb("silu", [P, 2, SPAN])
        act_ = sb("act_", [P, 2, HF // P, EROWS])
        y = sb("y", [P, 2, ST, D])
        psT = ps("psTE", [P, 2, 512])
        psU = ps("psU", [P, 4, 512])
        psY = ps("psYE", [P, 2, 512])
        w1_in = sem("w1_in")
        w2_in = [sem(f"w2_in{i}") for i in range(2)]
        rows_in = [sem(f"rows_in{i}") for i in range(2)]
        y_out = [sem(f"y_out{i}") for i in range(2)]
        turned, xh_ready, xl_ready, wh_ready, wl_ready, up_ready, silu_ready, act_ready, down_ready, y_kept = (
            sem(x) for x in ("turnedE", "xh_ready", "xl_ready", "wh_ready", "wl_ready", "up_ready", "silu_ready", "act_ready",
                             "down_ready", "y_keptE"))
        act_zeroed, y_free = sem("act_zeroed"), sem("y_free")
        block = ctx.enter_context(nc.Block())
        HT = HF // P
        UPS = HT * 2

        def loop(engine, step):
            with engine.Fori(0, E // 2 - 1) as i:
                for c in range(2):
                    step(2 * i + c, c, i, True)
            for c in range(2):
                step(E - 2 + c, c, E // 2 - 1, c == 0)

        @block.sync
        def _(sp):
            def load_w1(e):
                for dst, n, half, row in ((0, P, 0, 0), (0, PAD, 1, P), (PAD, PAD, 1, P)):
                    sp.dma_start(w1[dst:dst + n, half, :], io.w1[ds(e * D + row, n), :]).then_inc(w1_in, 16)

            def load_w2(e, c):
                sp.dma_start(w2[:, c], io.w2[ds(e * HF, HF), :].rearrange("(k p) n -> p k n", k=HT)).then_inc(w2_in[c], 16)

            credit(sp, y_free, y_free)
            load_w1(0)
            load_w2(0, 0)
            sp.wait_ge(wl_ready, 1)
            load_w1(1)
            load_w2(1, 1)

            def step(e, c, i, more):
                two_more = not isinstance(e, int)
                if two_more:
                    sp.wait_ge(wl_ready, e + 2)
                    load_w1(e + 2)
                sp.wait_ge(y_kept, ST * (e + 1) + 1)
                if two_more:
                    load_w2(e + 2, c)
                sp.wait_ge(y_out[c], 16 * ST * (i + 1))
                sp.nop().then_inc(y_free, 1)

            loop(sp, step)

        @block.tensor
        def _(pe):
            def turn(e, c, t):
                pe.wait_ge(xl_ready, ST * e + max(t, 1))
                for h in range(2):
                    last = pe.transpose(psT[:, t % 2, h * P:(h + 1) * P], rows[:, c, t, h * P:(h + 1) * P], m.ident[:])
                last.then_inc(turned, 1)

            def step(e, c, i, more):
                pe.wait_ge(wl_ready, e + 1)
                pe.wait_ge(xl_ready, ST * (e + 1) + 1)
                for u in range(UPS):
                    k, j = divmod(u, HT)
                    T = slice(k * SPAN, (k + 1) * SPAN)
                    pe.wait_ge(act_ready, UPS * e + max(u, 1))
                    for half in range(2):
                        C = slice(half * HF + j * P, half * HF + (j + 1) * P)
                        passes = ((w1h[:, c, 0, C], xh[:, c, 0, T]), (w1h[:, c, 0, C], xl[:, c, T]),
                                  (w1l[:, c, 0, C], xh[:, c, 0, T]), (w1h[:, c, 1, C], xh[:, c, 1, T]),
                                  (w1l[:, c, 1, C], xh[:, c, 1, T]))
                        for n, (w, x) in enumerate(passes):
                            last = pe.matmul(psU[:, 2 * (u % 2) + half, 0:SPAN], w, x, start=(n == 0), stop=(n == 4))
                    last.then_inc(up_ready, 1)
                pe.wait_ge(w2_in[c], 16 * (i + 1))
                if more:
                    pe.wait_ge(rows_in[1 - c], 16 * ST * (i + 1 + c))
                for t in range(ST):
                    if more:
                        turn(e + 1, 1 - c, t)
                    pe.wait_ge(act_ready, UPS * e + (HT if (t + 1) * P <= SPAN else UPS) + 1)
                    pe.wait_ge(y_kept, ST * e + max(t, 1))
                    for j in range(HT):
                        last = pe.matmul(psY[:, t % 2, 0:D], act_[:, c, j, t * P:(t + 1) * P], w2[:, c, j, :],
                                         start=(j == 0), stop=(j == HT - 1))
                    last.then_inc(down_ready, 1)

            pe.wait_ge(act_zeroed, 1)
            pe.wait_ge(rows_in[0], 16 * ST)
            for t in range(ST):
                turn(0, 0, t)
            loop(pe, step)

        @block.scalar
        def _(act):
            def rows_high(e, c, t):
                act.wait_ge(turned, ST * e + t + 1)
                nc.scalar.activation(xh[:, c, :, t * P:(t + 1) * P], psT[:, t % 2, 0:2 * P].rearrange("p (h q) -> p h q", h=2),
                                     ACT.Copy).then_inc(xh_ready, 1)

            def weights_high(e, c, half):
                if half == 0:
                    act.wait_ge(w1_in, 16 * 3 * (e + 1))
                nc.scalar.activation(w1h[:, c, half, :], w1[:, half, :], ACT.Copy).then_inc(wh_ready, 1)

            def step(e, c, i, more):
                for u in range(UPS):
                    act.wait_ge(up_ready, UPS * e + u + 1)
                    act.wait_ge(act_ready, UPS * e + max(u, 1))
                    nc.scalar.activation(silu[:, u % 2, :], psU[:, 2 * (u % 2) + 1, 0:SPAN], ACT.Silu).then_inc(silu_ready, 1)
                    if more and u in (2, 4):
                        weights_high(e + 1, 1 - c, u // 2 - 1)
                act.wait_ge(y_free, e + 1)
                for t in range(ST):
                    if more:
                        rows_high(e + 1, 1 - c, t)
                    act.wait_ge(down_ready, ST * e + t + 1)
                    nc.scalar.activation(y[:, c, t, :], psY[:, t % 2, 0:D], ACT.Copy).then_inc(y_kept, 1)

            credit(act, y_kept)
            for half in range(2):
                weights_high(0, 0, half)
            for t in range(ST):
                rows_high(0, 0, t)
            loop(act, step)

        @block.gpsimd
        def _(pool):
            def gather(e):
                for t in range(ST):
                    pool.indirect_dma_start(
                        out=rows[:, e % 2, t, :], out_offset=None, in_=scratch.x,
                        in_offset=bass.IndirectOffsetOnAxis(ap=m.fetch[:, e * ST + t:e * ST + t + 1], axis=0),
                    ).then_inc(rows_in[e % 2], 16)

            def scatter(e):
                for t in range(ST):
                    pool.wait_ge(y_kept, ST * e + t + 2)
                    pool.indirect_dma_start(
                        out=scratch.y, out_offset=bass.IndirectOffsetOnAxis(ap=m.send[:, e * ST + t:e * ST + t + 1], axis=0),
                        in_=y[:, e % 2, t, :], in_offset=None).then_inc(y_out[e % 2], 16)

            gather(0)
            pool.memset(act_[:, :, :, 2 * SPAN:EROWS], 0.0).then_inc(act_zeroed, 1)
            gather(1)
            for e in range(E):
                if e + 2 < E:
                    pool.wait_ge(turned, ST * (e + 1))
                    gather(e + 2)
                scatter(e)
            for c in range(2):
                pool.wait_ge(y_out[c], 16 * ST * E // 2)

        @block.vector
        def _(dve):
            def rows_low(e, c, t):
                T = slice(t * P, (t + 1) * P)
                dve.wait_ge(xh_ready, ST * e + t + 1)
                dve.tensor_tensor(xl[:, c, T], psT[:, t % 2, 0:P], xh[:, c, 0, T], ALU.subtract)
                dve.tensor_tensor(xh[PAD:P, c, 1, T], psT[PAD:P, t % 2, P:2 * P], xh[PAD:P, c, 1, T],
                                  ALU.subtract).then_inc(xl_ready, 1)

            def weights_low(e, c, half):
                dve.wait_ge(wh_ready, 2 * e + half + 1)
                last = dve.tensor_tensor(w1l[:, c, half, :], w1[:, half, :], w1h[:, c, half, :], ALU.subtract)
                if half:
                    last.then_inc(wl_ready, 1)

            def step(e, c, i, more):
                for u in range(UPS):
                    k, j = divmod(u, HT)
                    dve.wait_ge(silu_ready, UPS * e + u + 1)
                    dve.tensor_tensor(act_[:, c, j, k * SPAN:(k + 1) * SPAN], psU[:, 2 * (u % 2), 0:SPAN], silu[:, u % 2, :],
                                      ALU.mult).then_inc(act_ready, 1)
                    if more and u in (3, 5):
                        weights_low(e + 1, 1 - c, (u - 3) // 2)
                if more:
                    for t in range(ST):
                        rows_low(e + 1, 1 - c, t)

            credit(dve, xl_ready, act_ready)
            for half in range(2):
                weights_low(0, 0, half)
            for t in range(ST):
                rows_low(0, 0, t)
            loop(dve, step)


def combine_phase(nc, m, scratch, out):
    with ExitStack() as ctx:
        sem = lambda n: ctx.enter_context(nc.semaphore(n))
        back = ctx.enter_context(nc.sbuf_tensor("back", [P, TOPK, B, D], F32))
        fetched = [sem(f"fetched{g}") for g in range(NG)]
        first, done, stored = sem("first"), sem("done"), sem("stored")
        block = ctx.enter_context(nc.Block())

        @block.sync
        def _(sp):
            for g in range(NG):
                for k in range(TOPK):
                    src = scratch.y[k * N + g * GT:k * N + (g + 1) * GT, :]
                    sp.dma_start(back[:, k, g * G:(g + 1) * G, :],
                                 src.rearrange("(b p) d -> p b d", p=P)).then_inc(fetched[g], 16)
            for g in range(NG):
                sp.wait_ge(done, G * (g + 1))
                T = slice(g * G, (g + 1) * G)
                sp.dma_start(out[T].rearrange("b p d -> p b d"), m.h0[:, T, :]).then_inc(stored, 16)
            sp.wait_ge(stored, 16 * NG)

        @block.vector
        def _(dve):
            for g in range(NG):
                dve.wait_ge(fetched[g], 16 * TOPK)
                for k in range(TOPK):
                    if k:
                        dve.wait_ge(first, G * (g + 1))
                    for b in range(g * G, (g + 1) * G):
                        h = m.h0[:, b, :]
                        dve.scalar_tensor_tensor(out=h, in0=back[:, k, b, :], scalar=m.gate[:, k, b:b + 1], in1=h,
                                                 op0=ALU.mult, op1=ALU.add).then_inc(done if k else first, 1)


def build(nc, io, out):
    scratch = Scratch(nc)
    with ExitStack() as ctx:
        def sb(n, s, d=F32):
            return ctx.enter_context(nc.sbuf_tensor(n, s, d))

        m = Resident(sb)
        with nc.sbuf_tensor("qs", [P, 2, NHS, 2 * P], BF16) as qs, nc.sbuf_tensor("ks", [P, 2, NHS, 2 * P], BF16) as ks:
            stacked = [[ctx.enter_context(nc.semaphore(f"stacked{i}_{j}")) for j in range(2)] for i in range(2)]
            project_phase(nc, io, m, scratch, qs, ks, stacked)
            attention_phase(nc, m, scratch, qs, ks, stacked)
        mlp_phase(nc, m, scratch)
        route_phase(nc, m)
        expert_phase(nc, io, m, scratch)
        combine_phase(nc, m, scratch, out)


def kernel(**inputs):
    import concourse.bacc as _bacc
    from concourse.bass_utils import run_bass_kernel_spmd as _run

    a = {k: np.asarray(v) for k, v in inputs.items()}
    columns = lambda w: w.reshape(2, KH).T
    qkv1, qkv2 = (a[f"L0_attn_qkv{i}_w"].T.reshape(D, 3, NH, HD) for i in (1, 2))
    laid = {
        "ids": a["x"].T, "table": a["L0_tok_word_table"], "pos": a["L0_tok_pos_table"],
        "gamma": a["L0_tok_gamma"], "beta": a["L0_tok_beta"],
        "ln1": np.stack([columns(a["L0_attn_ln1_w"]), columns(a["L0_attn_ln1_b"])], 1),
        "ln2": np.stack([columns(a["L0_attn_ln2_w"]), columns(a["L0_attn_ln2_b"])], 1),
        "wqk": np.stack([qkv1[:, 0:2], qkv2[:, 0:2]], 3).transpose(0, 1, 4, 2, 3).reshape(D, FQK), "wv": qkv1[:, 2].reshape(D, D), "proj": a["L0_attn_proj_w"].T,
        "projb": a["L0_attn_proj_b"], "rmsw": columns(a["L0_attn_rms_w"]),
        "lam1": a["L0_attn_lam1"].reshape(NH), "lam2": a["L0_attn_lam2"].reshape(NH),
        "fc1": a["L0_attn_fc1_w"].T, "fc1b": a["L0_attn_fc1_b"].reshape(MT, P).T,
        "fc2": a["L0_attn_fc2_w"].T, "fc2b": a["L0_attn_fc2_b"],
        "wg": a["L0_ffn_Wg"], "w1": a["L0_ffn_W1"].reshape(E * D, 2 * HF), "w2": a["L0_ffn_W2"].reshape(E * HF, D),
    }
    nc = _bacc.Bacc("TRN2", target_bir_lowering=False, num_devices=1)
    arrays, io = {}, {}
    for name, x in laid.items():
        x = np.ascontiguousarray(x)
        arrays[f"in_{name}"] = x
        io[name] = nc.dram_tensor(f"in_{name}", x.shape, mybir.dt.from_np(x.dtype), kind="ExternalInput").ap()
    out = nc.dram_tensor("out", (B, S, D), F32, kind="ExternalOutput").ap()
    build(nc, Inputs(io), out)
    r = _run(nc, [arrays], core_ids=[0])
    return r.results[0]["out"]
```

```python
from contextlib import ExitStack

import numpy as np

import concourse.bass as bass
from concourse import mybir

ALU = mybir.AluOpType
ACT = mybir.ActivationFunctionType
AX = mybir.AxisListType
F32 = mybir.dt.float32
F32R = mybir.dt.float32r
BF16 = mybir.dt.bfloat16
I32 = mybir.dt.int32
U32 = mybir.dt.uint32
ds = bass.ds

P = 128
B, S, V, D = 16, 128, 12564, 192
KH = D // 2
NH, HD = 12, 16
NHS = 2 * NH
G = 4
NG = B // G
GT = G * P
MLP = 4 * D
MT = MLP // P
FQK = 2 * NHS * HD
QT = FQK // P
PARTS = 3
E, TOPK, HF = 8, 2, 512
N = B * S
CAP = int(1.2 * N / E)
SPAN = CAP + CAP % 2
EROWS = 640
ST = EROWS // P
SLOTS = E * ST
LN_EPS, RMS_EPS, LAMBDA_INIT = 1e-5, 1e-6, 0.1
Q_SLOTS = (0, 1, 2, 0, 0, 1)
K_SLOTS = (0, 1, 0, 1, 2, 0)
KS = len(Q_SLOTS) * HD
HH = NHS // 2


class Inputs:

    def __init__(self, ap):
        self.ids = ap["ids"]
        self.table = ap["table"]
        self.pos = ap["pos"]
        self.gamma = ap["gamma"]
        self.beta = ap["beta"]
        self.ln1 = ap["ln1"]
        self.ln2 = ap["ln2"]
        self.wqk = ap["wqk"]
        self.wv = ap["wv"]
        self.proj = ap["proj"]
        self.projb = ap["projb"]
        self.rmsw = ap["rmsw"]
        self.lam1 = ap["lam1"]
        self.lam2 = ap["lam2"]
        self.fc1 = ap["fc1"]
        self.fc1b = ap["fc1b"]
        self.fc2 = ap["fc2"]
        self.fc2b = ap["fc2b"]
        self.wg = ap["wg"]
        self.w1 = ap["w1"]
        self.w2 = ap["w2"]


class Scratch:

    def __init__(self, nc):
        self.qk = nc.dram_tensor("qk_parts", (2, PARTS, HD, NHS, N), BF16, kind="Internal").ap()
        self.x = nc.dram_tensor("expert_in", (N + P, D + PAD), F32, kind="Internal").ap()
        self.y = nc.dram_tensor("expert_out", (TOPK * N + E * EROWS, D), F32, kind="Internal").ap()


class Early:

    def __init__(self, sb):
        self.wfc1 = sb("wfc1", [P, 2, MLP])
        self.wfc1h = sb("wfc1h", [P, 2, MLP], F32R)
        self.wfc1l = sb("wfc1l", [P, 2, MLP], F32R)
        self.pick = sb("pick", [PARTS * HH, HH, P], BF16)
        self.mean1 = sb("mean1", [P, B])
        self.rs = sb("rs1", [P, 2, B])


PAD = D - P


def split_product(pe, out, wh, wl, xh, xl):
    passes = ((wh[:, 0], xh[:, 0]), (wh[:, 0], xl), (wl[:, 0], xh[:, 0]), (wh[:, 1], xh[:, 1]), (wl[:, 1], xh[:, 1]))
    for n, (w, x) in enumerate(passes):
        last = pe.matmul(out, w, x, start=(n == 0), stop=(n == len(passes) - 1))
    return last


def load_split(engine, dst, src, signal):
    for first, half, row, n in ((0, 0, 0, P), (0, 1, P, PAD), (PAD, 1, P, PAD)):
        engine.dma_start(dst[first:first + n, half, :], src(row, n)).then_inc(signal, 16)


class Resident:

    def __init__(self, sb):
        self.h0 = sb("h0", [P, B, D])
        self.x1 = sb("x1", [P, B, D])
        self.v = sb("v", [P, B, D])
        self.o = sb("o", [P, B, D])
        self.xg = sb("xg", [P, B, D])
        self.logits = sb("logits", [P, B, E])
        self.gate = sb("gate", [P, TOPK, B])
        self.fetch = sb("fetch", [P, SLOTS], I32)
        self.send = sb("send", [P, SLOTS], I32)
        self.ident = sb("ident", [P, P])
        self.identb = sb("identb", [P, P], BF16)
        self.ones = sb("ones", [P, P], BF16)
        self.before = sb("before", [P, P], BF16)
        self.eps = sb("eps", [P, 3])
        self.nlam = sb("nlam", [P, NH])
        self.projb = sb("projb", [P, D])
        self.fc2b = sb("fc2b", [P, D])
        self.wproj = sb("wproj", [KH, 2, D])
        self.wfc2 = sb("wfc2", [P, MT, D])
        self.wg = sb("wg", [KH, 2, E])
        self.rmsw = sb("rmsw", [KH, 2])
        self.ln2 = sb("ln2", [P, 2, 2])
        self.fc1b = sb("fc1b", [P, MT])


def credit(engine, *sems):
    for sem in sems:
        engine.nop().then_inc(sem, 1)


class Steps:

    def __init__(self, engine, sem, start=0):
        self.engine, self.sem, self.start, self.n = engine, sem, start, 0

    def mark(self, instruction):
        instruction.then_inc(self.sem, 1)
        self.n += 1

    def settle(self):
        self.engine.wait_ge(self.sem, self.start + self.n)


def over_tiles(row, n):
    return row.unsqueeze(1).broadcast_to([P, n, D])


def moments(dve, steps, stats, mean, var, t):
    me, mo = stats[:, :, 1], stats[:, :, 4]
    n = stats.shape[1]
    a, b, c = t[:, 0, 0:n], t[:, 1, 0:n], t[:, 2, 0:n]
    dve.tensor_tensor(a, me, mo, ALU.subtract)
    dve.tensor_tensor(b, me, mo, ALU.add)
    steps.mark(dve.tensor_tensor(c, stats[:, :, 2], stats[:, :, 5], ALU.add))
    steps.settle()
    dve.tensor_scalar(mean, b, 0.5, None, ALU.mult)
    steps.mark(dve.scalar_tensor_tensor(out=a, in0=a, scalar=0.25, in1=a, op0=ALU.mult, op1=ALU.mult))
    steps.settle()
    return dve.scalar_tensor_tensor(out=var, in0=c, scalar=1.0 / D, in1=a, op0=ALU.mult, op1=ALU.add)


def project_phase(nc, io, m, early, scratch, parts, parts_out, qs, ks, stacked):
    NQ = 4
    STACK = 2 * QT + 1
    NORM_AT = {1: (0, 0, 1, 2, 2, 3), 2: (3, 4, 5, 6, 7, 8), 3: (9, 10, 11, 12, 13, 14)}
    with ExitStack() as ctx:
        sb = lambda n, s, d=F32: ctx.enter_context(nc.sbuf_tensor(n, s, d))
        sem = lambda n: ctx.enter_context(nc.semaphore(n))
        ids = sb("ids", [P, B], I32)
        emb = m.o
        normed = m.xg[:].rearrange("p b d -> p (b d)")[:, 0:2 * G * 2 * P].rearrange("p (i t d) -> p i t d", i=2, t=G)
        hT = m.x1[:].rearrange("p b d -> p (b d)")[:, 0:4 * GT].rearrange("p (i k q) -> p i k q", i=2, k=2)
        wqkh, wqkl = early.wfc1h, early.wfc1l
        pos = sb("pos", [P, D])
        gamma = sb("gamma", [P, D])
        beta = sb("beta", [P, D])
        lam = sb("lam", [P, 2, NH])
        ln1 = sb("ln1", [P, 2, 2])
        wqk = sb("wqk", [P, 2, FQK])
        wv = sb("wv", [P, 2, D])
        hh = sb("hh", [P, 2, 2, GT], F32R)
        hl = sb("hl", [P, 2, GT], F32R)
        rest = sb("rest", [P, NB, GT])
        chosen = sb("chosenA", [PARTS * HH, HH])
        stats = sb("statsA", [P, B, 6])
        mean1, rs = early.mean1, early.rs
        small = sb("smallA", [P, 3, B])
        mv = sb("mvA", [P, 7, B])
        mean0, var0, std0, r0, var1 = (mv[:, i, :] for i in range(5))
        stds = mv[:, 5:7, :]
        psT = ctx.enter_context(nc.psum_tensor("psTA", [P, 2, 512], F32))
        psq = ctx.enter_context(nc.psum_tensor("psq", [P, NQ, 512], F32))
        psv = ctx.enter_context(nc.psum_tensor("psv", [P, 2, 512], F32))
        ids_in, pos_in, row_in, lam_in, w_in, rest_in = (sem(x) for x in ("ids_in", "pos_in", "row_in", "lam_in", "w_in", "rest_in"))
        gathered = [sem(f"gathered{g}") for g in range(NG)]
        const_set, const_step = sem("const_set"), sem("const_step")
        emb_ready, var0_ready, std0_ready = (sem(x) for x in ("emb_ready", "var0_ready", "std0_ready"))
        var1_ready, stds_ready, normed_ready = (sem(x) for x in ("var1_ready", "stds_ready", "normed_ready"))
        wh_ready, hh_ready, hl_ready = (sem(x) for x in ("wh_readyA", "hh_ready", "hl_ready"))
        turned, hT_ready, qk_ready, v_ready, v_kept = (sem(x) for x in ("turned", "hT_ready", "qk_ready", "v_ready", "v_kept"))
        hi_ready, rest_ready, mid_ready, lo_ready = (sem(x) for x in ("hi_ready", "rest_ready", "mid_ready", "lo_ready"))
        dve_step = sem("dve_stepA")
        block = ctx.enter_context(nc.Block())

        @block.sync
        def _(sp):
            sp.dma_start(ids[:], io.ids).then_inc(ids_in, 16)
            sp.dma_start(pos[:], io.pos).then_inc(pos_in, 16)
            for dst, src in ((gamma, io.gamma), (beta, io.beta)):
                sp.dma_start(dst[:], src.partition_broadcast(P)).then_inc(row_in, 16)
            sp.dma_start(ln1[:], io.ln1).then_inc(w_in, 16)
            load_split(sp, wqk, lambda row, n: io.wqk[row:row + n, :], w_in)
            load_split(sp, wv, lambda row, n: io.wv[row:row + n, :], w_in)

            def weights(dst, src):
                return lambda: sp.dma_start(dst[:], src.rearrange("(k p) n -> p k n", p=dst.shape[0])).then_inc(rest_in, 16)

            def rows_and_columns():
                for k, row in enumerate((io.lam1, io.lam2)):
                    sp.dma_start(lam[:, k, :], row.partition_broadcast(P)).then_inc(lam_in, 16)
                for dst, src in ((m.projb, io.projb), (m.fc2b, io.fc2b)):
                    sp.dma_start(dst[:], src.partition_broadcast(P)).then_inc(rest_in, 16)
                for dst, src in ((m.rmsw, io.rmsw), (m.ln2, io.ln2), (m.fc1b, io.fc1b)):
                    sp.dma_start(dst[:], src).then_inc(rest_in, 16)

            def stack(pair, half):
                return lambda: load_pair(sp, scratch, qs, ks, stacked, pair, pair, half)

            def fc1():
                load_split(sp, early.wfc1, lambda row, n: io.fc1[row:row + n, :], rest_in)

            between = {1: rows_and_columns, 2: weights(m.wproj, io.proj), 3: weights(m.wg, io.wg),
                       4: fc1, 6: weights(m.wfc2, io.fc2)}
            for i in range(4):
                between[STACK + 2 * i] = stack(i // 2, i % 2)

            for n in range(NG * QT):
                g, j = n // QT, n % QT
                sp.wait_ge(lo_ready, n + 1)
                rows = scratch.qk[j // (QT // 2)].rearrange("c r h t -> (r h) c t")
                dst = rows[(j % (QT // 2)) * P:(j % (QT // 2) + 1) * P, :, g * GT:(g + 1) * GT]
                sp.dma_start(dst, parts[:, n % NB]).then_inc(parts_out[n % NB], 16)
                if n == STACK:
                    for i in range(NB):
                        sp.wait_ge(parts_out[i], 16 * len(range(i, n + 1, NB)))
                if n in between:
                    between[n]()
            sp.wait_ge(rest_in, 16 * 11)

        @block.gpsimd
        def _(pool):
            steps = Steps(pool, const_step)
            pool.wait_ge(ids_in, 16)
            for b in range(B):
                pool.indirect_dma_start(
                    out=emb[:, b, :], out_offset=None, in_=io.table,
                    in_offset=bass.IndirectOffsetOnAxis(ap=ids[:, b:b + 1], axis=0),
                ).then_inc(gathered[b // G], 16)
                if b == G - 1:
                    pool.memset(m.eps[:, 0:1], LN_EPS)
                    pool.memset(m.eps[:, 1:2], RMS_EPS)
                    pool.memset(m.eps[:, 2:3], LN_EPS ** 2)
                    pool.memset(m.ident[:], 0.0)
                    steps.mark(pool.memset(m.ones[:], 1.0))
                    steps.settle()
                    steps.mark(pool.affine_select(out=m.ident[:], in_=m.ident[:], compare_op=ALU.not_equal, fill=1.0,
                                                  base=0, pattern=[[-1, P]], channel_multiplier=1))
                    pool.affine_select(out=m.before[:], in_=m.ones[:], compare_op=ALU.is_gt, fill=0.0,
                                       base=0, pattern=[[1, P]], channel_multiplier=-1)
                    steps.settle()
                    pool.tensor_copy(m.identb[:], m.ident[:]).then_inc(const_set, 1)
            pool.wait_ge(pos_in, 16)

            def add_pos(g):
                e = emb[:, g * G:(g + 1) * G, :]
                pool.wait_ge(gathered[g], 16 * G)
                pool.tensor_tensor(e, e, over_tiles(pos[:], G), ALU.add).then_inc(emb_ready, 1)

            def low_part(n):
                pool.wait_ge(mid_ready, n + 1)
                pool.tensor_tensor(parts[:, n % NB, 2, :], rest[:, n % NB, :], parts[:, n % NB, 1, :],
                                   ALU.subtract).then_inc(lo_ready, 1)

            add_pos(1)
            add_pos(2)
            for n in range(NG * QT):
                low_part(n)
                if n == 3:
                    add_pos(3)

        @block.scalar
        def _(act):
            act.wait_ge(const_set, 1)

            def root0(g):
                T = slice(g * G, (g + 1) * G)
                act.wait_ge(var0_ready, g + 1)
                nc.scalar.activation(std0[:, T], var0[:, T], ACT.Sqrt, bias=m.eps[:, 0:1]).then_inc(std0_ready, 1)

            def root1(g):
                T = slice(g * G, (g + 1) * G)
                act.wait_ge(var1_ready, g + 1)
                nc.scalar.activation(stds[:, 0, T], var1[:, T], ACT.Sqrt, bias=m.eps[:, 0:1])
                nc.scalar.activation(stds[:, 1, T], var1[:, T], ACT.Sqrt, bias=m.eps[:, 2:3],
                                     scale=1.0 + LN_EPS).then_inc(stds_ready, 1)

            def high(n):
                act.wait_ge(qk_ready, n + 1)
                if n >= NB:
                    act.wait_ge(parts_out[n % NB], 16 * (n // NB))
                nc.scalar.activation(parts[:, n % NB, 0, :], psq[:, n % NQ, :], ACT.Copy).then_inc(hi_ready, 1)

            def middle(n):
                act.wait_ge(rest_ready, n + 1)
                nc.scalar.activation(parts[:, n % NB, 1, :], rest[:, n % NB, :], ACT.Copy).then_inc(mid_ready, 1)

            def features(g):
                act.wait_ge(turned, g + 1)
                if g >= 2:
                    act.wait_ge(v_ready, 2 * (g - 1))
                for k in range(2):
                    last = nc.scalar.activation(hT[:, g % 2, k, :], psT[:, k, :], ACT.Identity,
                                                bias=ln1[:, 1, k:k + 1], scale=ln1[:, 0, k:k + 1])
                last.then_inc(hT_ready, 1)
                act.wait_ge(hT_ready, g + 1)
                nc.scalar.activation(hh[:, g % 2], hT[:, g % 2], ACT.Copy).then_inc(hh_ready, 1)

            def keep_v(g, i):
                act.wait_ge(v_ready, 2 * g + i + 1)
                b = g * G + 2 * i
                nc.scalar.activation(m.v[:, b:b + 2, :], psv[:, i, 0:2 * D].rearrange("p (b d) -> p b d", b=2),
                                     ACT.Copy).then_inc(v_kept, 1)

            act.wait_ge(w_in, 16 * 7)
            nc.scalar.activation(wqkh[:], wqk[:], ACT.Copy).then_inc(wh_ready, 1)
            root0(0)
            root1(0)
            features(0)
            for n in range(NG * QT + 1):
                if n < NG * QT:
                    high(n)
                if n:
                    middle(n - 1)
                for g in NORM_AT:
                    if n == NORM_AT[g][1] + 1:
                        root0(g)
                    if n == NORM_AT[g][4] + 1:
                        root1(g)
                if n and n % QT == 0:
                    keep_v(n // QT - 1, 0)
                    keep_v(n // QT - 1, 1)
                if n % QT == QT - 1 and n // QT + 1 < NG:
                    features(n // QT + 1)

        @block.vector
        def _(dve):
            st = Steps(dve, dve_step)

            def stats0(g, T, tiles):
                if g:
                    dve.wait_ge(emb_ready, g)
                for b in tiles:
                    last = dve.bn_stats(stats[:, b, :], emb[:, b, :])
                st.mark(last)
                st.settle()

            def moments0(g, T, tiles):
                moments(dve, st, stats[:, T, :], mean0[:, T], var0[:, T], small).then_inc(var0_ready, 1)

            def scale0(g, T, tiles):
                dve.wait_ge(std0_ready, g + 1)
                st.mark(dve.reciprocal(r0[:, T], std0[:, T]))
                for b in tiles:
                    last = dve.scalar_tensor_tensor(out=m.h0[:, b, :], in0=emb[:, b, :], scalar=mean0[:, b:b + 1],
                                                    in1=gamma[:], op0=ALU.subtract, op1=ALU.mult)
                st.mark(last)
                st.settle()

            def shift0(g, T, tiles):
                for b in tiles:
                    last = dve.scalar_tensor_tensor(out=m.h0[:, b, :], in0=m.h0[:, b, :], scalar=r0[:, b:b + 1],
                                                    in1=beta[:], op0=ALU.mult, op1=ALU.add)
                st.mark(last)
                st.settle()

            def stats1(g, T, tiles):
                for b in tiles:
                    last = dve.bn_stats(stats[:, b, :], m.h0[:, b, :])
                st.mark(last)
                st.settle()
                moments(dve, st, stats[:, T, :], mean1[:, T], var1[:, T], small).then_inc(var1_ready, 1)

            def norm1(g, T, tiles):
                dve.wait_ge(stds_ready, g + 1)
                st.mark(dve.reciprocal(rs[:, :, T], stds[:, :, T]))
                st.settle()
                if g >= 2:
                    dve.wait_ge(turned, g - 1)
                for b in tiles:
                    for dst, src in ((slice(0, D), slice(0, D)), (slice(D, 2 * P), slice(P, D))):
                        last = dve.tensor_scalar(normed[:, g % 2, b % G, dst], m.h0[:, b, src], mean1[:, b:b + 1],
                                                 rs[:, 1, b:b + 1], ALU.subtract, ALU.mult)
                last.then_inc(normed_ready, 1)

            NORMS = (stats0, moments0, scale0, shift0, stats1, norm1)

            def norms(g, k):
                NORMS[k](g, slice(g * G, (g + 1) * G), range(g * G, (g + 1) * G))

            dve.wait_ge(const_set, 1)
            R = PARTS * HH
            st.mark(dve.tensor_tensor(chosen[:], m.ident[0:R, 0:HH], m.ident[0:R, HH:2 * HH], ALU.add))
            st.settle()
            st.mark(dve.tensor_tensor(chosen[:], chosen[:], m.ident[0:R, 2 * HH:R], ALU.add))
            st.settle()
            dve.tensor_copy(early.pick[:], chosen[:].unsqueeze(2).broadcast_to([R, HH, P]))
            dve.wait_ge(pos_in, 16)
            dve.wait_ge(gathered[0], 16 * G)
            st.mark(dve.tensor_tensor(emb[:, 0:G, :], emb[:, 0:G, :], over_tiles(pos[:], G), ALU.add))
            st.settle()
            dve.wait_ge(row_in, 16 * 2)
            for k in range(len(NORMS)):
                norms(0, k)
            dve.wait_ge(wh_ready, 1)
            st.mark(dve.tensor_tensor(wqkl[:], wqk[:], wqkh[:], ALU.subtract))

            def low_parts(g):
                dve.wait_ge(hh_ready, g + 1)
                dve.tensor_tensor(hl[:, g % 2, :], hT[:, g % 2, 0, :], hh[:, g % 2, 0, :], ALU.subtract)
                dve.tensor_tensor(hh[PAD:P, g % 2, 1, :], hT[PAD:P, g % 2, 1, :], hh[PAD:P, g % 2, 1, :],
                                  ALU.subtract).then_inc(hl_ready, 1)

            low_parts(0)
            for g in range(NG):
                for j in range(QT):
                    n = g * QT + j
                    dve.wait_ge(hi_ready, n + 1)
                    if n >= NB:
                        dve.wait_ge(lo_ready, n - NB + 1)
                    dve.tensor_tensor(rest[:, n % NB, :], psq[:, n % NQ, :], parts[:, n % NB, 0, :],
                                      ALU.subtract).then_inc(rest_ready, 1)
                    for later in NORM_AT:
                        for k in range(len(NORMS)):
                            if NORM_AT[later][k] == n:
                                norms(later, k)
                if g + 1 < NG:
                    low_parts(g + 1)
            dve.wait_ge(lam_in, 16 * 2)
            st.mark(dve.tensor_tensor(m.nlam[:], lam[:, 1, :], lam[:, 0, :], ALU.subtract))
            st.settle()
            dve.tensor_scalar(m.nlam[:], m.nlam[:], -LAMBDA_INIT, None, ALU.add)

        @block.tensor
        def _(pe):
            pe.wait_ge(const_set, 1)
            pe.wait_ge(w_in, 16 * 7)

            def turn(g):
                pe.wait_ge(normed_ready, g + 1)
                if g:
                    pe.wait_ge(hT_ready, g)
                for k in range(2):
                    for t in range(G):
                        last = pe.transpose(psT[:, k, t * P:(t + 1) * P], normed[:, g % 2, t, k * P:(k + 1) * P], m.ident[:])
                last.then_inc(turned, 1)

            turn(0)
            for g in range(NG):
                pe.wait_ge(hl_ready, g + 1)
                for j in range(QT):
                    n = g * QT + j
                    if n >= NQ:
                        pe.wait_ge(rest_ready, n - NQ + 1)
                    J = slice(j * P, (j + 1) * P)
                    split_product(pe, psq[:, n % NQ, :], wqkh[:, :, J], wqkl[:, :, J], hh[:, g % 2],
                                  hl[:, g % 2]).then_inc(qk_ready, 1)
                if g + 1 < NG:
                    turn(g + 1)
                for i in range(2):
                    if g:
                        pe.wait_ge(v_kept, 2 * (g - 1) + i + 1)
                    for t in range(2 * i, 2 * i + 2):
                        for k, K in enumerate((P, PAD)):
                            last = pe.matmul(psv[:, i, (t % 2) * D:(t % 2 + 1) * D], hT[0:K, g % 2, k, t * P:(t + 1) * P],
                                             wv[0:K, k, :], start=(k == 0), stop=(k == 1))
                    last.then_inc(v_ready, 1)


def runs(slots):
    cut = [j for j in range(len(slots)) if j == 0 or slots[j] != slots[j - 1] + 1] + [len(slots)]
    return [(a, slots[a], b - a) for a, b in zip(cut[:-1], cut[1:])]


NB = 4
PAIR_LOADS = len(runs(Q_SLOTS)) + len(runs(K_SLOTS))


def load_pair(engine, scratch, qs, ks, stacked, pair, par, half):
    H = slice(half * NHS // 2, (half + 1) * NHS // 2)
    for side, (dst, slots) in enumerate(((qs, Q_SLOTS), (ks, K_SLOTS))):
        for slot, part, n in runs(slots):
            src = scratch.qk[side, part:part + n].rearrange("c r h t -> (c r) h t")
            engine.dma_start(dst[slot * HD:(slot + n) * HD, par, H, :],
                             src[:, H, ds(pair * 2 * P, 2 * P)]).then_inc(stacked[par][half], 16)


def attention_phase(nc, m, early, scratch, parts_out, qs, ks, stacked):
    R = NH // 2
    with ExitStack() as ctx:
        sb = lambda n, s, d=F32: ctx.enter_context(nc.sbuf_tensor(n, s, d))
        ps = lambda n, s, d=F32: ctx.enter_context(nc.psum_tensor(n, s, d))
        sem = lambda n: ctx.enter_context(nc.semaphore(n))
        ex = sb("ex", [P, 6, 512])
        vcur = sb("vcur", [P, 2, NH, 32])
        nmax = sb("nmax", [P, 2, HH])
        nrest = sb("nrest", [P, 2, HH])
        mparts = sb("mparts", [P, 2, 2 * PARTS, HH], BF16)
        mT = sb("mT", [PARTS * HH, 2, P], BF16)
        oT = sb("oTB", [P, 3, 2 * P])
        rs = sb("rs", [P, 6, 4])
        o1 = sb("o1", [P, 3, 4, HD])
        o2 = sb("o2", [P, 3, 4, HD])
        psS = ps("psS", [P, 2, 4, P])
        psE = ps("psE", [P, 2, 4, P])
        psO = ps("psO", [P, 4, 256])
        psR = ps("psR", [P, 8, P])
        psM = [psO[0:2 * PARTS * HH, 3, i * P // 2:(i + 1) * P // 2].bitcast(BF16) for i in range(2)]
        sums_set, zeros_set, v_cur, high_set = sem("sums_set"), sem("zeros_setB"), sem("v_cur"), sem("high_set")
        s_ready, s_max, m_split, m_turned, mT_ready = (sem(x) for x in ("s_ready", "s_max", "m_split", "m_turned", "mT_ready"))
        st_ready, exp_ready, pv_ready, oT_ready, o_turned, o_normed = (
            sem(x) for x in ("st_ready", "exp_ready", "pv_ready", "oT_ready", "o_turned", "o_normed"))
        dve_step = sem("dve_stepB")
        block = ctx.enter_context(nc.Block())
        DM, DN = 2 * 3, 3
        TURNS = B // 4

        def rows(engine, step):
            for c in range(4):
                step(c, 0, c)
            with engine.Fori(1, TURNS - 1) as i:
                for c in range(4):
                    step(4 * i + c, i, c)
            for c in range(4):
                step(B - 4 + c, TURNS - 1, c)

        def exists(b):
            return not isinstance(b, int) or 0 <= b < B

        def passed(engine, signal, value):
            if not isinstance(value, int) or value > 0:
                engine.wait_ge(signal, value)

        @block.sync
        def _(sp):
            for i in range(NB):
                sp.wait_ge(parts_out[i], 16 * len(range(i, NG * QT, NB)))

            def step(b, i, c):
                for half in range(2):
                    if c % 2 == 1 and (not isinstance(i, int) or i < TURNS - 1):
                        sp.wait_ge(st_ready, R * b + (half + 1) * R // 2)
                        load_pair(sp, scratch, qs, ks, stacked, 2 * i + c // 2 + 2, c // 2, half)

            rows(sp, step)

        @block.gpsimd
        def _(pool):
            pool.memset(vcur[:], 1.0).then_inc(sums_set, 1)
            pool.wait_ge(sums_set, 1)
            pool.memset(mparts[:, :, PARTS:, :], 0.0).then_inc(zeros_set, 1)
            pool.wait_ge(zeros_set, 1)

            def copy(b, c):
                pool.tensor_copy(vcur[:, c % 2, :, 0:HD],
                                 m.v[:, ds(b, 1), :].rearrange("p o (h d) -> p (o h) d", h=NH)).then_inc(v_cur, 1)

            copy(0, 0)

            def step(b, i, c):
                if exists(b + 1):
                    passed(pool, pv_ready, 2 * b)
                    copy(b + 1, c + 1)
                if isinstance(b, int):
                    n = b if b < 4 else b - (B - 8)
                    for t in (2 * n, 2 * n + 1):
                        pool.tensor_scalar(m.x1[:, t, :], m.h0[:, t, :], early.mean1[:, t:t + 1], early.rs[:, 0, t:t + 1],
                                           ALU.subtract, ALU.mult)
                if isinstance(b, int) and b < 2:
                    pool.tensor_copy(early.wfc1h[:, b, :], early.wfc1[:, b, :]).then_inc(high_set, 1)
                    pool.wait_ge(high_set, b + 1)
                    pool.tensor_tensor(early.wfc1l[:, b, :], early.wfc1[:, b, :], early.wfc1h[:, b, :], ALU.subtract)

            rows(pool, step)

        @block.tensor
        def _(pe):
            def scores(b, c, r):
                par, T = c // 2, slice((c % 2) * P, (c % 2 + 1) * P)
                passed(pe, s_max, b * R + r - 1)
                for x in range(4):
                    h = 4 * r + x
                    last = pe.matmul(psS[:, r % 2, x, :], qs[:, par, h, T], ks[:, par, h, T],
                                     start=True, stop=True)
                last.then_inc(s_ready, 1)

            def turn_maxima(b, half):
                pe.wait_ge(m_split, 2 * b + half + 1)
                passed(pe, mT_ready, 2 * b + half)
                if half == 0:
                    passed(pe, oT_ready, 2 * (b - 1))
                pe.transpose(psM[half], mparts[:, half, :, :].rearrange("p a h -> p (a h)"), m.identb[:]).then_inc(m_turned, 1)

            def values(b, c, r):
                pe.wait_ge(exp_ready, R * b + r + 2)
                if r == 0:
                    pe.wait_ge(v_cur, b + 1)
                    passed(pe, oT_ready, 2 * b - 1)
                if r == 4:
                    passed(pe, oT_ready, 2 * b)
                    if exists(b + 1):
                        pe.wait_ge(mT_ready, 2 * b + 4)
                for x in range(4):
                    h = 2 * r + x
                    last = pe.matmul(psO[32 * x:32 * x + 32, h // 4, :], vcur[:, c % 2, h, :],
                                     ex[:, r + x // 2, (x % 2) * 256:(x % 2 + 1) * 256], start=True, stop=True)
                if r >= 2:
                    last.then_inc(pv_ready, 1)

            def turn_back(b):
                pe.wait_ge(oT_ready, 2 * b + 2)
                passed(pe, o_normed, b)
                for x in range(6):
                    last = pe.transpose(psR[:, x, :], oT[:, x // 2, (x % 2) * P:(x % 2 + 1) * P], m.ident[:])
                last.then_inc(o_turned, 1)

            def step(b, i, c):
                par, T = c // 2, slice((c % 2) * P, (c % 2 + 1) * P)
                for r in range(R):
                    half = r // (R // 2)
                    passed(pe, exp_ready, R * b + r - 1)
                    for x in range(4):
                        h = 4 * r + x
                        pe.matmul(psE[:, r % 2, x, :], ks[:, par, h, T], qs[:, par, h, T], start=True, stop=False)
                        if x == 0 and r % (R // 2) == 0:
                            pe.wait_ge(mT_ready, 2 * b + half + 1)
                        last = pe.matmul(psE[:, r % 2, x, :], early.pick[:, h % HH, :], mT[:, half, :], start=False, stop=True)
                    last.then_inc(st_ready, 1)
                    if r == 1 and c % 2 == 1 and exists(b + 1):
                        pe.wait_ge(stacked[1 - par][1], 16 * PAIR_LOADS * (i + 1 + par))
                    if r < R - 2 and exists(b + 1):
                        scores(b + 1, (c + 1) % 4, r + 2)
                    if r >= R - 2 and exists(b + 2):
                        if r == R - 2 and c % 2 == 0:
                            pe.wait_ge(stacked[1 - par][0], 16 * PAIR_LOADS * (i + 1 + par))
                        scores(b + 2, (c + 2) % 4, r - (R - 2))
                    if r == 2 and exists(b + 1):
                        turn_maxima(b + 1, 0)
                    if r == 5 and exists(b + 1):
                        turn_maxima(b + 1, 1)
                    if r == 3 and exists(b - 1):
                        turn_back(b - 1)
                    if r in (3, 5):
                        values(b, c, r - 3)
                    elif r == 1 and exists(b - 1):
                        values(b - 1, c - 1, 4)

            for half in range(2):
                pe.wait_ge(stacked[0][half], 16 * PAIR_LOADS)
            pe.wait_ge(zeros_set, 1)
            for r in range(R):
                scores(0, 0, r)
            turn_maxima(0, 0)
            turn_maxima(0, 1)
            for r in range(2):
                scores(1, 1, r)
            rows(pe, step)
            values(B - 1, 3, 4)
            turn_back(B - 1)

        @block.scalar
        def _(act):
            def turn_maxima(b, i, c, half):
                act.wait_ge(m_turned, 2 * b + 2 + half + 1)
                nc.scalar.activation(mT[:, half, :], psM[half][0:PARTS * HH, :], ACT.Copy).then_inc(mT_ready, 1)

            def keep(b, bank):
                act.wait_ge(pv_ready, 2 * b + 1 + bank)
                H = slice(0, 2) if bank == 0 else slice(2, 3)
                if bank == 0:
                    passed(act, o_turned, b)
                nc.scalar.activation(oT[:, H, :], psO[:, H, :], ACT.Copy).then_inc(oT_ready, 1)

            def step(b, i, c):
                for r in range(R):
                    act.wait_ge(st_ready, R * b + r + 1)
                    if r % 4 == 0:
                        passed(act, pv_ready, 2 * b - 1 + r // 4)
                    nc.scalar.activation(ex[:, r, :].rearrange("p (x q) -> p x q", x=4), psE[:, r % 2], ACT.Exp,
                                         scale=HD ** -0.5).then_inc(exp_ready, 1)
                    if r == 1 and exists(b - 1):
                        keep(b - 1, 1)
                    if r in (2, 5) and exists(b + 1):
                        turn_maxima(b, i, c, r // 3)
                keep(b, 0)

            for half in range(2):
                act.wait_ge(m_turned, half + 1)
                nc.scalar.activation(mT[:, half, :], psM[half][0:PARTS * HH, :], ACT.Copy).then_inc(mT_ready, 1)
            rows(act, step)
            keep(B - 1, 1)

        @block.vector
        def _(dve):
            def maximum(b, r, st):
                half, k = divmod(r, R // 2)
                dve.wait_ge(s_ready, R * b + r + 1)
                if k == 0:
                    passed(dve, m_split, 2 * b - 1 + half)
                dve.tensor_reduce(nmax[:, half, 4 * k:4 * k + 4], psS[:, r % 2], AX.X, ALU.max,
                                  negate=True).then_inc(s_max, 1)
                if k < R // 2 - 1:
                    return
                n, w = nmax[:, half, :], nrest[:, half, :]
                dve.wait_ge(s_max, R * b + r + 1)
                passed(dve, m_turned, 2 * b - 1 + half)
                st.mark(dve.tensor_copy(mparts[:, half, 0, :], n))
                st.settle()
                st.mark(dve.tensor_tensor(w, n, mparts[:, half, 0, :], ALU.subtract))
                st.settle()
                st.mark(dve.tensor_copy(mparts[:, half, 1, :], w))
                st.settle()
                dve.tensor_tensor(mparts[:, half, 2, :], w, mparts[:, half, 1, :], ALU.subtract).then_inc(m_split, 1)

            def norm(b, st):
                dve.wait_ge(o_turned, b + 1)
                o = psR[:, 0:6, :].rearrange("p (g s) (h w) -> p g s h w", s=2, h=4)
                r4 = rs[:].rearrange("p (g s) h -> p g s h", s=2)
                st.mark(dve.reciprocal(rs[:], psR[:, 0:6, :].rearrange("p x (h w) -> p x h w", h=4)[:, :, :, HD]))
                st.settle()
                st.mark(dve.tensor_tensor(r4[:, :, 1, :], r4[:, :, 1, :], m.nlam[:].rearrange("p (g h) -> p g h", g=3), ALU.mult))
                st.settle()
                wide = lambda s: r4[:, :, s, :].unsqueeze(3).broadcast_to([P, 3, 4, HD])
                dve.tensor_tensor(o1[:], o[:, :, 0, :, 0:HD], wide(0), ALU.mult)
                st.mark(dve.tensor_tensor(o2[:], o[:, :, 1, :, 0:HD], wide(1), ALU.mult))
                st.settle()
                dve.tensor_tensor(m.o[:, ds(b, 1), :].rearrange("p o d -> p (o d)"),
                                  o1[:].rearrange("p g h d -> p (g h d)"),
                                  o2[:].rearrange("p g h d -> p (g h d)"), ALU.add).then_inc(o_normed, 1)

            def step(b, i, c):
                st = Steps(dve, dve_step, DM if isinstance(b, int) and b == 0 else (DM + DN) * b + DM - DN)
                if exists(b + 1):
                    for r in range(2, R):
                        maximum(b + 1, r, st)
                if exists(b - 1):
                    norm(b - 1, st)
                if exists(b + 2):
                    for r in range(2):
                        maximum(b + 2, r, st)

            st = Steps(dve, dve_step)
            for r in range(R):
                maximum(0, r, st)
            for r in range(2):
                maximum(1, r, st)
            rows(dve, step)
            norm(B - 1, Steps(dve, dve_step, DM * B + DN * (B - 1)))


def mlp_phase(nc, m, early, scratch):
    with ExitStack() as ctx:
        sb = lambda n, s, d=F32: ctx.enter_context(nc.sbuf_tensor(n, s, d))
        ps = lambda n, s, d=F32: ctx.enter_context(nc.psum_tensor(n, s, d))
        sem = lambda n: ctx.enter_context(nc.semaphore(n))
        zeros = sb("zeros", [P, D * 8])
        zeros_set, zeros_out, x_out = sem("zeros_set"), sem("zeros_out"), sem("x_out")
        staged = sb("staged", [P, 2, G, D + PAD])
        fT = sb("fT", [P, 2, 2, GT])
        fh = sb("fh", [P, 2, GT], F32R)
        fl = sb("fl", [P, GT], F32R)
        gT = sb("gT", [P, 2, MT, GT])
        stats = sb("statsC", [P, B, 6])
        small = sb("smallC", [P, 3, B])
        mv = sb("mvC", [P, 3, 4, B])
        psT = ps("psTC", [P, 2, 512])
        psG = ps("psG", [P, 3, 512])
        psY = ps("psY", [P, 2, 512])
        psL = ps("psL", [P, 512])
        var_ready, std_ready, staged_ready, turned, fT_ready, y_ready, y_kept = (
            sem(x) for x in ("var_ready", "std_ready", "staged_ready", "turnedC", "fT_ready", "y_ready", "y_kept"))
        g_ready, gelu_ready, dve_step, l_ready = (sem(x) for x in ("g_ready", "gelu_ready", "dve_stepC", "l_ready"))
        biased, bias2_ready, summed, fh_ready, fl_ready, square_ready, square_root = (
            sem(x) for x in ("biased", "bias2_ready", "summed", "fh_ready", "fl_ready", "square_ready", "square_root"))
        block = ctx.enter_context(nc.Block())
        ITEMS = [(0, 0), (0, 1), (0, 2), (0, 3), (1, 0), (1, 1), (2, 0), (1, 2), (2, 1), (1, 3), (2, 2), (2, 3)]
        WITH_Y = [x for x in ITEMS if x[0] < 2]

        def y_count(s, g):
            return 2 * (WITH_Y.index((s, g)) + 1)

        def tiles(g):
            return slice(g * G, (g + 1) * G)

        def norms_to(k):
            return len([x for x in ITEMS[:k + 1] if x[0]])

        def staged_in(k):
            s, g = ITEMS[k]
            return k - 2 if s == 0 or ITEMS.index((s - 1, g)) < k - 2 else k - 1

        def nested(k):
            return ITEMS[k][0] == 2 and ITEMS[k - 1][0] == 1

        def rooted_in(k):
            n = staged_in(k)
            return n + 1 if n >= 0 and nested(n) and ITEMS[n + 1][0] == 1 else n

        @block.sync
        def _(sp):
            sp.wait_ge(zeros_set, 1)
            sp.dma_start(scratch.x[N:N + P, :], zeros[:, 0:D + PAD]).then_inc(zeros_out, 16)
            flat = scratch.y[0:TOPK * N, :].rearrange("(c p r) d -> c p (r d)", p=P, r=8)
            for c in range(TOPK * N // (8 * P)):
                sp.dma_start(flat[c], zeros[:]).then_inc(zeros_out, 16)
            for g in range(NG):
                sp.wait_ge(staged_ready, norms_to(ITEMS.index((2, g))))
                for dst, src in ((slice(0, D), slice(0, D)), (slice(D, D + PAD), slice(D - PAD, D))):
                    sp.dma_start(scratch.x[g * GT:(g + 1) * GT, dst].rearrange("(b p) d -> p b d", p=P),
                                 m.xg[:, tiles(g), src]).then_inc(x_out, 16)
            sp.wait_ge(zeros_out, 16 * (TOPK * N // (8 * P) + 1))
            sp.wait_ge(x_out, 2 * 16 * NG)

        @block.vector
        def _(dve):
            st = Steps(dve, dve_step)

            def statistics(s, T):
                src = (m.o, m.x1, m.h0)[s]
                for b in range(T.start, T.stop):
                    last = dve.bn_stats(stats[:, b, :], src[:, b, :])
                st.mark(last)
                st.settle()
                return moments(dve, st, stats[:, T], mv[:, s, 0, T], mv[:, s, 1, T], small)

            def mean_squares():
                st.mark(statistics(0, slice(0, B)))
                mean, var, std, rr = (mv[:, 0, i, :] for i in range(4))
                st.mark(dve.tensor_tensor(std, mean, mean, ALU.mult))
                st.settle()
                dve.tensor_tensor(var, var, std, ALU.add).then_inc(square_ready, 1)
                dve.wait_ge(square_root, 1)
                st.mark(dve.reciprocal(rr, std))
                st.settle()

            def stage(k):
                s, g = ITEMS[k]
                if s == 0:
                    return
                T = tiles(g)
                src = (m.o, m.x1, m.h0)[s]
                dve.wait_ge(y_kept, y_count(s - 1, g))
                statistics(s, T).then_inc(var_ready, 1)
                dve.wait_ge(std_ready, norms_to(k))
                st.mark(dve.reciprocal(mv[:, s, 3, T], mv[:, s, 2, T]))
                st.settle()
                dve.wait_ge(turned, k - 1)
                for t in range(G):
                    b = g * G + t
                    mb, rb = mv[:, s, 0, b:b + 1], mv[:, s, 3, b:b + 1]
                    dst = staged[:, k % 2, t, 0:D] if s == 1 else m.xg[:, b, :]
                    last = dve.tensor_scalar(dst, src[:, b, :], mb, rb, ALU.subtract, ALU.mult)
                    if s == 1:
                        last = dve.tensor_scalar(staged[:, k % 2, t, D:], src[:, b, P:], mb, rb, ALU.subtract, ALU.mult)
                last.then_inc(staged_ready, 1)

            def low_parts(k):
                s, g = ITEMS[k]
                dve.wait_ge(fh_ready, g + 1)
                if g:
                    dve.wait_ge(g_ready, MT * g)
                dve.tensor_tensor(fl[:], fT[:, k % 2, 0, :], fh[:, 0, :], ALU.subtract)
                dve.tensor_tensor(fh[PAD:P, 1, :], fT[PAD:P, k % 2, 1, :], fh[PAD:P, 1, :], ALU.subtract).then_inc(fl_ready, 1)

            def keep(s, g):
                dst = m.h0 if s else m.x1
                if s:
                    dve.wait_ge(summed, g + 1)
                else:
                    dve.wait_ge(biased, g + 1)
                for i in range(2):
                    dve.wait_ge(y_ready, y_count(s, g) - 1 + i)
                    b = g * G + 2 * i
                    if s == 0:
                        for t in range(2):
                            last = dve.scalar_tensor_tensor(out=dst[:, b + t, :], in0=psY[:, i, t * D:(t + 1) * D],
                                                            scalar=mv[:, 0, 3, b + t:b + t + 1], in1=dst[:, b + t, :],
                                                            op0=ALU.mult, op1=ALU.add)
                    else:
                        x = dst[:, b:b + 2, :]
                        last = dve.tensor_tensor(x, psY[:, i, 0:2 * D].rearrange("p (b d) -> p b d", b=2), x, ALU.add)
                    last.then_inc(y_kept, 1)
                    if i == 0 and s == 1:
                        n = ITEMS.index((s, g)) + 1
                        following(n + 1 if nested(n) else n)

            def following(k):
                if ITEMS[k][0] == 1:
                    low_parts(k)

            mean_squares()
            for k, (s, g) in enumerate(ITEMS):
                for ahead in (1, 2):
                    if k + ahead < len(ITEMS) and staged_in(k + ahead) == k:
                        stage(k + ahead)
                if s < 2:
                    keep(s, g)
                if s == 0:
                    following(k + 1)
            dve.wait_ge(l_ready, NG)
            dve.tensor_copy(m.logits[:], psL[:, 0:B * E].rearrange("p (b e) -> p b e", e=E))

        @block.gpsimd
        def _(pool):
            for g in range(NG):
                x = m.x1[:, tiles(g), :]
                pool.tensor_tensor(x, x, over_tiles(m.projb[:], G), ALU.add).then_inc(biased, 1)
            pool.memset(zeros[:], 0.0).then_inc(zeros_set, 1)
            for g in range(NG):
                h = m.h0[:, tiles(g), :]
                pool.tensor_tensor(h, h, over_tiles(m.fc2b[:], G), ALU.add).then_inc(bias2_ready, 1)
            for g in range(NG):
                h = m.h0[:, tiles(g), :]
                pool.wait_ge(bias2_ready, g + 1)
                pool.wait_ge(y_kept, y_count(0, g))
                pool.tensor_tensor(h, h, m.x1[:, tiles(g), :], ALU.add).then_inc(summed, 1)

        @block.scalar
        def _(act):
            def root(k):
                s, g = ITEMS[k]
                if s:
                    act.wait_ge(var_ready, norms_to(k))
                    nc.scalar.activation(mv[:, s, 2, tiles(g)], mv[:, s, 1, tiles(g)], ACT.Sqrt,
                                         bias=m.eps[:, 0:1]).then_inc(std_ready, 1)

            def features(k):
                s, g = ITEMS[k]
                act.wait_ge(turned, k + 1)
                if k >= 2:
                    s2, g2 = ITEMS[k - 2]
                    if s2 == 0:
                        act.wait_ge(y_ready, y_count(s2, g2))
                    elif s2 == 1:
                        act.wait_ge(fl_ready, g2 + 1)
                    else:
                        act.wait_ge(l_ready, g2 + 1)
                R = slice(0, P if s == 1 else KH)
                for h in range(2):
                    src, dst = psT[R, h, :], fT[R, k % 2, h, :]
                    if s == 0:
                        last = nc.scalar.activation(dst, src, ACT.Identity, scale=m.rmsw[:, h:h + 1])
                    elif s == 1:
                        last = nc.scalar.activation(dst, src, ACT.Identity, bias=m.ln2[:, 1, h:h + 1], scale=m.ln2[:, 0, h:h + 1])
                    else:
                        last = nc.scalar.activation(dst, src, ACT.Identity)
                last.then_inc(fT_ready, 1)
                if s == 1:
                    act.wait_ge(fT_ready, k + 1)
                    if g:
                        act.wait_ge(g_ready, MT * g)
                    nc.scalar.activation(fh[:], fT[:, k % 2], ACT.Copy).then_inc(fh_ready, 1)

            for k, (s, g) in enumerate(ITEMS):
                features(k)
                if k == 0:
                    act.wait_ge(square_ready, 1)
                    nc.scalar.activation(mv[:, 0, 2, :], mv[:, 0, 1, :], ACT.Sqrt, bias=m.eps[:, 1:2]).then_inc(square_root, 1)
                if s == 1:
                    for j in range(MT):
                        n = g * MT + j
                        act.wait_ge(g_ready, n + 1)
                        if j == 0 and g >= 2:
                            act.wait_ge(y_ready, y_count(1, g - 2))
                        nc.scalar.activation(gT[:, g % 2, j, :], psG[:, n % 3, :], ACT.Gelu,
                                             bias=m.fc1b[:, j:j + 1]).then_inc(gelu_ready, 1)
                for n in range(k + 1, len(ITEMS)):
                    if rooted_in(n) == k:
                        root(n)

        @block.tensor
        def _(pe):
            def turn(k):
                s, g = ITEMS[k]
                if s:
                    pe.wait_ge(staged_ready, norms_to(k))
                if k:
                    pe.wait_ge(fT_ready, k)
                for t in range(G):
                    src = (m.o[:, g * G + t, :], staged[:, k % 2, t, :], m.xg[:, g * G + t, :])[s]
                    W = P if s == 1 else KH
                    for h in range(2):
                        last = pe.transpose(psT[0:W, h, t * P:(t + 1) * P], src[:, h * W:(h + 1) * W], m.ident[:])
                last.then_inc(turned, 1)

            def products(k, tiles):
                s, g = ITEMS[k]
                for t in tiles:
                    i = t // 2
                    if t % 2 == 0 and WITH_Y.index((s, g)):
                        pe.wait_ge(y_kept, y_count(s, g) - 3 + i)
                    out = psY[:, i, (t % 2) * D:(t % 2 + 1) * D]
                    T = slice(t * P, (t + 1) * P)
                    if s == 0:
                        for h in range(2):
                            last = pe.matmul(out, fT[0:KH, k % 2, h, T], m.wproj[:, h, :], start=(h == 0), stop=(h == 1))
                    else:
                        for j in range(MT):
                            last = pe.matmul(out, gT[:, g % 2, j, T], m.wfc2[:, j, :], start=(j == 0), stop=(j == MT - 1))
                    if t % 2:
                        last.then_inc(y_ready, 1)

            def gate(k):
                g = ITEMS[k][1]
                pe.wait_ge(fT_ready, k + 1)
                for t in range(G):
                    b = g * G + t
                    for h in range(2):
                        last = pe.matmul(psL[:, b * E:(b + 1) * E], fT[0:KH, k % 2, h, t * P:(t + 1) * P], m.wg[:, h, :],
                                         start=(h == 0), stop=(h == 1))
                last.then_inc(l_ready, 1)

            turn(0)
            for k, (s, g) in enumerate(ITEMS):
                if s == 0:
                    pe.wait_ge(fT_ready, k + 1)
                    before = ITEMS[k + 1][0] == 0
                    if before:
                        turn(k + 1)
                    products(k, range(G))
                    if not before:
                        turn(k + 1)
                elif s == 1:
                    pe.wait_ge(fl_ready, g + 1)
                    for j in range(MT):
                        q = g * MT + j
                        if q >= 3:
                            pe.wait_ge(gelu_ready, q - 2)
                        J = slice(j * P, (j + 1) * P)
                        split_product(pe, psG[:, q % 3, :], early.wfc1h[:, :, J], early.wfc1l[:, :, J],
                                      fh[:], fl[:]).then_inc(g_ready, 1)
                    pe.wait_ge(gelu_ready, MT * (g + 1))
                    products(k, (0, 1))
                    turn(k + 1)
                    products(k, (2,))
                    if nested(k + 1):
                        gate(k + 1)
                        if staged_in(k + 2) <= k:
                            turn(k + 2)
                    products(k, (3,))
                elif not nested(k):
                    gate(k)
                elif staged_in(k + 1) == k:
                    turn(k + 1)


def route_phase(nc, m):
    with ExitStack() as ctx:
        sb = lambda n, s, d=F32: ctx.enter_context(nc.sbuf_tensor(n, s, d))
        sem = lambda n: ctx.enter_context(nc.semaphore(n))
        best = sb("best", [P, B, 8])
        besti = sb("besti", [P, B, 8], U32)
        chosen = sb("chosen", [P, TOPK, B])
        hot = sb("hot", [P, TOPK, B, E])
        hotb = sb("hotb", [P, TOPK, B, E], BF16)
        lane = sb("lane", [P, TOPK, B, E])
        picked = sb("picked", [P, TOPK, B, E])
        place = sb("place", [P, TOPK, B])
        keep = sb("keep", [P, TOPK, B])
        local = sb("local", [P, TOPK, B])
        bound = sb("bound", [P, TOPK * B, ST + 1])
        over = sb("over", [P, TOPK * B, ST + 1])
        inner = sb("inner", [P, TOPK * B, ST])
        within = sb("within", [P, TOPK * B])
        slot = sb("slot", [P, TOPK * B, P], BF16)
        point = sb("point", [P, P])
        token = sb("token", [P, 1])
        row = sb("row", [P, TOPK * B])
        marked = sb("marked", [P, 2, TOPK * B, ST])
        values = sb("values", [P, TOPK * B, 2, E, ST], BF16)
        second = sb("second", [P, SLOTS])
        spare = sb("spare", [P, SLOTS])
        full = sb("full", [P, SLOTS])
        target = sb("target", [P, SLOTS])
        source = sb("source", [P, SLOTS])
        e1 = sb("e1", [P, B])
        den = sb("den", [P, B])
        psC = ctx.enter_context(nc.psum_tensor("psC", [P, TOPK, B, E], F32))
        psI = ctx.enter_context(nc.psum_tensor("psI", [P, 2, SLOTS], F32))
        const_set, hot_ready, counted, gap_ready, exp_ready, marked_ready, slot_ready, values_ready, values2_ready, found = (
            sem(x) for x in ("const_setD", "hot_ready", "counted", "gap_ready", "exp_readyD", "marked_ready", "slot_ready",
                             "values_ready", "values2_ready", "found"))
        dve_step = sem("dve_stepD")
        block = ctx.enter_context(nc.Block())
        CONSTS = 7

        @block.gpsimd
        def _(pool):
            def iota(out, pattern, base=0, down=0):
                pool.iota(out, pattern=pattern, base=base, channel_multiplier=down,
                          allow_small_or_imprecise_dtypes=True).then_inc(const_set, 1)

            iota(lane[:], [[0, TOPK * B], [1, E]])
            iota(bound[:], [[0, TOPK * B], [P, ST + 1]])
            iota(row[:], [[1, TOPK * B]])
            iota(token[:], [[0, 1]], base=1, down=1)
            iota(point[:], [[1, P]])
            iota(second[:], [[0, E], [P, ST]], down=1)
            iota(spare[:], [[P, SLOTS]], base=TOPK * N, down=1)
            T = slice(B, TOPK * B)
            pool.wait_ge(marked_ready, 1)
            for x in range(2):
                pool.tensor_tensor(values[:, T, x], hot[:, 1].unsqueeze(3).broadcast_to([P, B, E, ST]),
                                   marked[:, x, T].unsqueeze(2).broadcast_to([P, B, E, ST]), ALU.mult).then_inc(values2_ready, 1)

        @block.scalar
        def _(act):
            act.wait_ge(gap_ready, 1)
            nc.scalar.activation(e1[:], den[:], ACT.Exp).then_inc(exp_ready, 1)

        @block.tensor
        def _(pe):
            pe.wait_ge(hot_ready, 1)
            pe.matmul(psC[:], m.before[:], hotb[:], start=True, stop=False, skip_group_check=True)
            for d in range(1, B):
                last = pe.matmul(psC[:, :, d:B, :], m.ones[:], hotb[:, :, 0:B - d, :], start=False,
                                 stop=(d == B - 1), skip_group_check=True)
            last.then_inc(counted, 1)
            for k in range(TOPK):
                pe.wait_ge(values2_ready if k else values_ready, 2)
                pe.wait_ge(slot_ready, k + 1)
                for n in range(k * B, (k + 1) * B):
                    last = pe.matmul(psI[:], slot[:, n, :], values[:, n], start=(n == 0), stop=(n == TOPK * B - 1))
            last.then_inc(found, 1)

        @block.vector
        def _(dve):
            st = Steps(dve, dve_step)
            for b in range(B):
                last = dve.max(best[:, b, :], m.logits[:, b, :])
            st.mark(last)
            st.settle()
            for b in range(B):
                last = dve.max_index(besti[:, b, :], best[:, b, :], m.logits[:, b, :])
            st.mark(last)
            st.settle()
            for k in range(TOPK):
                last = dve.tensor_copy(chosen[:, k, :], besti[:, :, k])
            st.mark(last)
            dve.tensor_tensor(den[:], best[:, :, 1], best[:, :, 0], ALU.subtract).then_inc(gap_ready, 1)
            st.settle()
            dve.wait_ge(const_set, CONSTS)
            for k in range(TOPK):
                last = dve.tensor_tensor(hot[:, k], lane[:, k], chosen[:, k, :].unsqueeze(2).broadcast_to([P, B, E]),
                                         ALU.is_equal)
            st.mark(last)
            st.settle()
            dve.tensor_copy(hotb[:], hot[:]).then_inc(hot_ready, 1)
            dve.wait_ge(exp_ready, 1)
            st.mark(dve.tensor_scalar(den[:], e1[:], 1.0, None, ALU.add))
            st.mark(dve.tensor_scalar(second[:], second[:], float(CAP), float(N), ALU.is_ge, ALU.mult))
            st.settle()
            st.mark(dve.reciprocal(m.gate[:, 0, :], den[:]))
            st.settle()
            st.mark(dve.tensor_tensor(m.gate[:, 1, :], m.gate[:, 0, :], e1[:], ALU.mult))
            dve.wait_ge(counted, 1)
            st.mark(dve.tensor_tensor(picked[:], hot[:], psC[:], ALU.mult))
            st.settle()
            st.mark(dve.tensor_reduce(place[:], picked[:], AX.X, ALU.add))
            st.settle()
            dve.tensor_scalar(keep[:], place[:], float(CAP), None, ALU.is_lt)
            dve.tensor_copy(local[:, 0, :], place[:, 0, :])
            st.mark(dve.tensor_scalar(local[:, 1, :], place[:, 1, :], float(CAP), None, ALU.add))
            st.settle()
            flat = local[:].rearrange("p k b -> p (k b)")
            kept = keep[:].rearrange("p k b -> p (k b)")
            wide = lambda x: x.unsqueeze(2).broadcast_to([P, TOPK * B, ST])
            dve.tensor_tensor(m.gate[:], m.gate[:], keep[:], ALU.mult)
            st.mark(dve.tensor_tensor(over[:], flat.unsqueeze(2).broadcast_to([P, TOPK * B, ST + 1]), bound[:], ALU.is_ge))
            st.settle()
            dve.tensor_tensor(inner[:], over[:, :, 0:ST], over[:, :, 1:ST + 1], ALU.subtract)
            st.mark(dve.tensor_reduce(within[:], over[:, :, 1:ST + 1], AX.X, ALU.add))
            st.settle()
            st.mark(dve.scalar_tensor_tensor(out=within[:], in0=within[:], scalar=-float(P), in1=flat,
                                             op0=ALU.mult, op1=ALU.add))
            st.mark(dve.tensor_tensor(inner[:], inner[:], wide(kept), ALU.mult))
            st.settle()
            dve.tensor_scalar(marked[:, 0], inner[:], token[:], None, ALU.mult)
            st.mark(dve.tensor_tensor(marked[:, 1], inner[:], wide(row[:]), ALU.mult))
            st.settle()
            dve.nop().then_inc(marked_ready, 1)
            for x in range(2):
                dve.tensor_tensor(values[:, 0:B, x], hot[:, 0].unsqueeze(3).broadcast_to([P, B, E, ST]),
                                  marked[:, x, 0:B].unsqueeze(2).broadcast_to([P, B, E, ST]), ALU.mult).then_inc(values_ready, 1)
            for k in range(TOPK):
                T = slice(k * B, (k + 1) * B)
                dve.tensor_tensor(slot[:, T, :], within[:, T].unsqueeze(2).broadcast_to([P, B, P]),
                                  point[:].unsqueeze(1).broadcast_to([P, B, P]), ALU.is_equal).then_inc(slot_ready, 1)
            dve.wait_ge(found, 1)
            dve.tensor_scalar(full[:], psI[:, 0, :], 0.5, None, ALU.is_ge)
            st.mark(dve.tensor_scalar(target[:], psI[:, 0, :], -1.0, None, ALU.add))
            st.settle()
            st.mark(dve.scalar_tensor_tensor(out=target[:], in0=psI[:, 1, :], scalar=float(P), in1=target[:],
                                             op0=ALU.mult, op1=ALU.add))
            st.settle()
            st.mark(dve.tensor_tensor(source[:], target[:], second[:], ALU.subtract))
            st.mark(dve.tensor_tensor(target[:], target[:], spare[:], ALU.subtract))
            st.settle()
            st.mark(dve.scalar_tensor_tensor(out=source[:], in0=source[:], scalar=-float(N), in1=full[:],
                                             op0=ALU.add, op1=ALU.mult))
            st.mark(dve.tensor_tensor(target[:], target[:], full[:], ALU.mult))
            st.settle()
            dve.tensor_scalar(m.fetch[:], source[:], float(N), None, ALU.add)
            dve.tensor_tensor(m.send[:], target[:], spare[:], ALU.add)


def expert_phase(nc, io, m, scratch):
    with ExitStack() as ctx:
        sb = lambda n, s, d=F32: ctx.enter_context(nc.sbuf_tensor(n, s, d))
        ps = lambda n, s, d=F32: ctx.enter_context(nc.psum_tensor(n, s, d))
        sem = lambda n: ctx.enter_context(nc.semaphore(n))
        w1 = sb("w1", [P, 2, 2 * HF])
        w1h = sb("w1h", [P, 2, 2, 2 * HF], F32R)
        w1l = sb("w1l", [P, 2, 2, 2 * HF], F32R)
        w2 = sb("w2", [P, 2, HF // P, D])
        rows = sb("rows", [P, 2, ST, D + PAD])
        xh = sb("xh", [P, 2, 2, EROWS], F32R)
        xl = sb("xl", [P, 2, EROWS], F32R)
        silu = sb("silu", [P, 2, SPAN])
        act_ = sb("act_", [P, 2, HF // P, EROWS])
        y = sb("y", [P, 2, ST, D])
        psT = ps("psTE", [P, 2, 512])
        psU = ps("psU", [P, 4, 512])
        psY = ps("psYE", [P, 2, 512])
        w1_in = sem("w1_in")
        w2_in = [sem(f"w2_in{i}") for i in range(2)]
        first_in = [sem(f"first_in{t}") for t in range(ST)]
        rows_in = [sem(f"rows_in{i}") for i in range(2)]
        y_out = [sem(f"y_out{i}") for i in range(2)]
        turned, xh_ready, xl_ready, wh_ready, wl_ready, up_ready, silu_ready, act_ready, down_ready, y_kept = (
            sem(x) for x in ("turnedE", "xh_ready", "xl_ready", "wh_ready", "wl_ready", "up_ready", "silu_ready", "act_ready",
                             "down_ready", "y_keptE"))
        act_zeroed, y_free = sem("act_zeroed"), sem("y_free")
        block = ctx.enter_context(nc.Block())
        HT = HF // P
        UPS = HT * 2

        def loop(engine, step):
            with engine.Fori(0, E // 2 - 1) as i:
                for c in range(2):
                    step(2 * i + c, c, i, True)
            for c in range(2):
                step(E - 2 + c, c, E // 2 - 1, c == 0)

        @block.sync
        def _(sp):
            def load_w1(e):
                load_split(sp, w1, lambda row, n: io.w1[ds(e * D + row, n), :], w1_in)

            def load_w2(e, c):
                sp.dma_start(w2[:, c], io.w2[ds(e * HF, HF), :].rearrange("(k p) n -> p k n", k=HT)).then_inc(w2_in[c], 16)

            credit(sp, y_free, y_free)
            load_w1(0)
            load_w2(0, 0)
            sp.wait_ge(wl_ready, 1)
            load_w1(1)
            load_w2(1, 1)

            def step(e, c, i, more):
                two_more = not isinstance(e, int)
                if two_more:
                    sp.wait_ge(wl_ready, e + 2)
                    load_w1(e + 2)
                sp.wait_ge(y_kept, ST * (e + 1) + 1)
                if two_more:
                    load_w2(e + 2, c)
                sp.wait_ge(y_out[c], 16 * ST * (i + 1))
                sp.nop().then_inc(y_free, 1)

            loop(sp, step)

        @block.tensor
        def _(pe):
            def turn(e, c, t):
                pe.wait_ge(xl_ready, ST * e + max(t, 1))
                for h in range(2):
                    last = pe.transpose(psT[:, t % 2, h * P:(h + 1) * P], rows[:, c, t, h * P:(h + 1) * P], m.ident[:])
                last.then_inc(turned, 1)

            def step(e, c, i, more):
                pe.wait_ge(wl_ready, e + 1)
                pe.wait_ge(xl_ready, ST * (e + 1) + 1)
                for u in range(UPS):
                    k, j = divmod(u, HT)
                    T = slice(k * SPAN, (k + 1) * SPAN)
                    pe.wait_ge(act_ready, UPS * e + max(u, 1))
                    for half in range(2):
                        C = slice(half * HF + j * P, half * HF + (j + 1) * P)
                        last = split_product(pe, psU[:, 2 * (u % 2) + half, 0:SPAN], w1h[:, c, :, C], w1l[:, c, :, C],
                                             xh[:, c, :, T], xl[:, c, T])
                    last.then_inc(up_ready, 1)
                pe.wait_ge(w2_in[c], 16 * (i + 1))
                if more:
                    pe.wait_ge(rows_in[1 - c], 16 * ST * (i + 1))
                for t in range(ST):
                    if more:
                        turn(e + 1, 1 - c, t)
                    pe.wait_ge(act_ready, UPS * e + (HT if (t + 1) * P <= SPAN else UPS) + 1)
                    pe.wait_ge(y_kept, ST * e + max(t, 1))
                    for j in range(HT):
                        last = pe.matmul(psY[:, t % 2, 0:D], act_[:, c, j, t * P:(t + 1) * P], w2[:, c, j, :],
                                         start=(j == 0), stop=(j == HT - 1))
                    last.then_inc(down_ready, 1)

            pe.wait_ge(act_zeroed, 1)
            for t in range(ST):
                pe.wait_ge(first_in[t], 16)
                turn(0, 0, t)
            loop(pe, step)

        @block.scalar
        def _(act):
            def rows_high(e, c, t):
                act.wait_ge(turned, ST * e + t + 1)
                nc.scalar.activation(xh[:, c, :, t * P:(t + 1) * P], psT[:, t % 2, 0:2 * P].rearrange("p (h q) -> p h q", h=2),
                                     ACT.Copy).then_inc(xh_ready, 1)

            def weights_high(e, c, half):
                if half == 0:
                    act.wait_ge(w1_in, 16 * 3 * (e + 1))
                nc.scalar.activation(w1h[:, c, half, :], w1[:, half, :], ACT.Copy).then_inc(wh_ready, 1)

            def step(e, c, i, more):
                for u in range(UPS):
                    act.wait_ge(up_ready, UPS * e + u + 1)
                    act.wait_ge(act_ready, UPS * e + max(u, 1))
                    nc.scalar.activation(silu[:, u % 2, :], psU[:, 2 * (u % 2) + 1, 0:SPAN], ACT.Silu).then_inc(silu_ready, 1)
                    if more and u in (2, 4):
                        weights_high(e + 1, 1 - c, u // 2 - 1)
                act.wait_ge(y_free, e + 1)
                for t in range(ST):
                    if more:
                        rows_high(e + 1, 1 - c, t)
                    act.wait_ge(down_ready, ST * e + t + 1)
                    nc.scalar.activation(y[:, c, t, :], psY[:, t % 2, 0:D], ACT.Copy).then_inc(y_kept, 1)

            credit(act, y_kept)
            for t in range(ST):
                if t in (0, 2):
                    weights_high(0, 0, t // 2)
                rows_high(0, 0, t)
            loop(act, step)

        @block.gpsimd
        def _(pool):
            def gather(e):
                for t in range(ST):
                    pool.indirect_dma_start(
                        out=rows[:, e % 2, t, :], out_offset=None, in_=scratch.x,
                        in_offset=bass.IndirectOffsetOnAxis(ap=m.fetch[:, e * ST + t:e * ST + t + 1], axis=0),
                    ).then_inc(rows_in[e % 2] if e else first_in[t], 16)

            def scatter(e):
                for t in range(ST):
                    pool.wait_ge(y_kept, ST * e + t + 2)
                    pool.indirect_dma_start(
                        out=scratch.y, out_offset=bass.IndirectOffsetOnAxis(ap=m.send[:, e * ST + t:e * ST + t + 1], axis=0),
                        in_=y[:, e % 2, t, :], in_offset=None).then_inc(y_out[e % 2], 16)

            pool.memset(act_[:, :, :, 2 * SPAN:EROWS], 0.0).then_inc(act_zeroed, 1)
            gather(0)
            gather(1)
            for e in range(E):
                if e + 2 < E:
                    pool.wait_ge(turned, ST * (e + 1))
                    gather(e + 2)
                scatter(e)
            for c in range(2):
                pool.wait_ge(y_out[c], 16 * ST * E // 2)

        @block.vector
        def _(dve):
            def rows_low(e, c, t):
                T = slice(t * P, (t + 1) * P)
                dve.wait_ge(xh_ready, ST * e + t + 1)
                dve.tensor_tensor(xl[:, c, T], psT[:, t % 2, 0:P], xh[:, c, 0, T], ALU.subtract)
                dve.tensor_tensor(xh[PAD:P, c, 1, T], psT[PAD:P, t % 2, P:2 * P], xh[PAD:P, c, 1, T],
                                  ALU.subtract).then_inc(xl_ready, 1)

            def weights_low(e, c, half):
                dve.wait_ge(wh_ready, 2 * e + half + 1)
                last = dve.tensor_tensor(w1l[:, c, half, :], w1[:, half, :], w1h[:, c, half, :], ALU.subtract)
                if half:
                    last.then_inc(wl_ready, 1)

            def step(e, c, i, more):
                for u in range(UPS):
                    k, j = divmod(u, HT)
                    dve.wait_ge(silu_ready, UPS * e + u + 1)
                    dve.tensor_tensor(act_[:, c, j, k * SPAN:(k + 1) * SPAN], psU[:, 2 * (u % 2), 0:SPAN], silu[:, u % 2, :],
                                      ALU.mult).then_inc(act_ready, 1)
                    if more and u in (3, 5):
                        weights_low(e + 1, 1 - c, (u - 3) // 2)
                if more:
                    for t in range(ST):
                        rows_low(e + 1, 1 - c, t)

            credit(dve, xl_ready, act_ready)
            for t in range(ST):
                if t in (2, 4):
                    weights_low(0, 0, t // 2 - 1)
                rows_low(0, 0, t)
            loop(dve, step)


def combine_phase(nc, m, scratch, out):
    with ExitStack() as ctx:
        sem = lambda n: ctx.enter_context(nc.semaphore(n))
        back = ctx.enter_context(nc.sbuf_tensor("back", [P, TOPK, B, D], F32))
        fetched = [sem(f"fetched{g}") for g in range(NG)]
        first, done, stored = sem("first"), sem("done"), sem("stored")
        block = ctx.enter_context(nc.Block())

        @block.sync
        def _(sp):
            for g in range(NG):
                for k in range(TOPK):
                    src = scratch.y[k * N + g * GT:k * N + (g + 1) * GT, :]
                    sp.dma_start(back[:, k, g * G:(g + 1) * G, :],
                                 src.rearrange("(b p) d -> p b d", p=P)).then_inc(fetched[g], 16)
            for b in range(0, B, 2):
                sp.wait_ge(done, b + 2)
                T = slice(b, b + 2)
                sp.dma_start(out[T].rearrange("b p d -> p b d"), m.h0[:, T, :]).then_inc(stored, 16)
            sp.wait_ge(stored, 16 * B // 2)

        @block.vector
        def _(dve):
            for g in range(NG):
                dve.wait_ge(fetched[g], 16 * TOPK)
                for k in range(TOPK):
                    if k:
                        dve.wait_ge(first, G * (g + 1))
                    for b in range(g * G, (g + 1) * G):
                        h = m.h0[:, b, :]
                        dve.scalar_tensor_tensor(out=h, in0=back[:, k, b, :], scalar=m.gate[:, k, b:b + 1], in1=h,
                                                 op0=ALU.mult, op1=ALU.add).then_inc(done if k else first, 1)


def build(nc, io, out):
    scratch = Scratch(nc)
    with ExitStack() as ctx:
        def sb(n, s, d=F32):
            return ctx.enter_context(nc.sbuf_tensor(n, s, d))

        m = Resident(sb)
        with ExitStack() as until_experts:
            early = Early(lambda n, s, d=F32: until_experts.enter_context(nc.sbuf_tensor(n, s, d)))
            qs = until_experts.enter_context(nc.sbuf_tensor("qs", [KS, 2, NHS, 2 * P], BF16))
            ks = until_experts.enter_context(nc.sbuf_tensor("ks", [KS, 2, NHS, 2 * P], BF16))
            stacked = [[ctx.enter_context(nc.semaphore(f"stacked{i}_{j}")) for j in range(2)] for i in range(2)]
            with nc.sbuf_tensor("parts", [P, NB, PARTS, GT], BF16) as parts:
                parts_out = [ctx.enter_context(nc.semaphore(f"parts_out{i}")) for i in range(NB)]
                project_phase(nc, io, m, early, scratch, parts, parts_out, qs, ks, stacked)
                attention_phase(nc, m, early, scratch, parts_out, qs, ks, stacked)
            mlp_phase(nc, m, early, scratch)
        route_phase(nc, m)
        expert_phase(nc, io, m, scratch)
        combine_phase(nc, m, scratch, out)


def kernel(**inputs):
    import concourse.bacc as _bacc
    from concourse.bass_utils import run_bass_kernel_spmd as _run

    a = {k: np.asarray(v) for k, v in inputs.items()}
    columns = lambda w: w.reshape(2, KH).T
    split_columns = lambda w: np.stack([w[:P], np.concatenate([w[P:], w[P:]])], 1)
    qkv1, qkv2 = (a[f"L0_attn_qkv{i}_w"].T.reshape(D, 3, NH, HD) for i in (1, 2))
    laid = {
        "ids": a["x"].T, "table": a["L0_tok_word_table"], "pos": a["L0_tok_pos_table"],
        "gamma": a["L0_tok_gamma"], "beta": a["L0_tok_beta"],
        "ln1": np.stack([split_columns(a["L0_attn_ln1_w"]), split_columns(a["L0_attn_ln1_b"])], 1),
        "ln2": np.stack([split_columns(a["L0_attn_ln2_w"]), split_columns(a["L0_attn_ln2_b"])], 1),
        "wqk": np.stack([qkv1[:, 0:2], qkv2[:, 0:2]], 3).transpose(0, 1, 4, 2, 3).reshape(D, FQK), "wv": qkv1[:, 2].reshape(D, D), "proj": a["L0_attn_proj_w"].T,
        "projb": a["L0_attn_proj_b"], "rmsw": columns(a["L0_attn_rms_w"]),
        "lam1": a["L0_attn_lam1"].reshape(NH), "lam2": a["L0_attn_lam2"].reshape(NH),
        "fc1": a["L0_attn_fc1_w"].T, "fc1b": a["L0_attn_fc1_b"].reshape(MT, P).T,
        "fc2": a["L0_attn_fc2_w"].T, "fc2b": a["L0_attn_fc2_b"],
        "wg": a["L0_ffn_Wg"], "w1": a["L0_ffn_W1"].reshape(E * D, 2 * HF), "w2": a["L0_ffn_W2"].reshape(E * HF, D),
    }
    nc = _bacc.Bacc("TRN2", target_bir_lowering=False, num_devices=1)
    arrays, io = {}, {}
    for name, x in laid.items():
        x = np.ascontiguousarray(x)
        arrays[f"in_{name}"] = x
        io[name] = nc.dram_tensor(f"in_{name}", x.shape, mybir.dt.from_np(x.dtype), kind="ExternalInput").ap()
    out = nc.dram_tensor("out", (B, S, D), F32, kind="ExternalOutput").ap()
    build(nc, Inputs(io), out)
    r = _run(nc, [arrays], core_ids=[0])
    return r.results[0]["out"]
```
